# Optimizing a Trainium2 kernel written in Bass

```python
import numpy as np
import jax
import jax.numpy as jnp

def _softmax(x, axis=-1):
    return jax.nn.softmax(x, axis=axis)

def _gelu(x):
    return jax.nn.gelu(x, approximate=True)

def _silu(x):
    return jax.nn.silu(x)

def _sigmoid(x):
    return jax.nn.sigmoid(x)

def _layernorm(x, axis=-1, eps=1e-05):
    m = jnp.mean(x, axis=axis, keepdims=True)
    v = jnp.var(x, axis=axis, keepdims=True)
    return (x - m) / jnp.sqrt(v + eps)

def _scatter_add(tgt, idx, src, axis=0):
    return tgt.at[idx].add(src)

def _segment_sum(src, seg, n):
    return jax.ops.segment_sum(src, seg, n)
kernel_name = 'mk_xattn_seq_d2_seqx_r8_09662a'

def setup_inputs(seed: int=0):
    np.random.seed(seed)
    _w = jnp.asarray

    def _rec_inputs():
        import jax
        import jax.numpy as jnp
        _rk = jax.random.key(seed)
        x = -0.0002928 + 1 * jax.random.normal(jax.random.fold_in(_rk, 1), (8, 256, 128), jnp.float32)
        _lenS = 256 - jax.random.randint(jax.random.fold_in(_rk, 7), (8,), 0, max(1, 256 // 4) + 1, jnp.int32)
        _lenS2 = 1601 - jax.random.randint(jax.random.fold_in(_rk, 8), (8,), 0, max(1, 1601 // 4) + 1, jnp.int32)
        _ctx_1024P = jax.random.normal(jax.random.fold_in(_rk, 11), (8, 16, 128), jnp.float32)
        _ctx_1024c = jax.random.dirichlet(jax.random.fold_in(_rk, 511), 0.3 * jnp.ones((16,), jnp.float32), (8, 1601))
        _ctx_1024t = jnp.einsum('bsk,bkd->bsd', _ctx_1024c, _ctx_1024P)
        _ctx_1024t = _ctx_1024t * jax.lax.rsqrt(jnp.mean(jnp.square(_ctx_1024t)) + 1e-12) * 0.953939
        ctx_1024 = -1.39393e-06 + 0.999914 * (_ctx_1024t + 0.3 * jax.random.normal(jax.random.fold_in(_rk, 611), (8, 1601, 128), jnp.float32))
        return (x, ctx_1024)
    x, ctx_1024 = _rec_inputs()

    def _L0_xattn_setup():
        import jax, jax.numpy as jnp
        import numpy as np
        B, Q, KV = (2, 256, 256)
        D_MODEL = 128
        N_HEADS = 16
        D_KV = 64
        EPS = 1e-06
        key = jax.random.key(seed)
        ks = jax.random.split(key, 7)
        s = 0.02
        return {'hidden_states': jax.random.normal(ks[0], (B, Q, D_MODEL), jnp.float32), 'key_value_states': jax.random.normal(ks[1], (B, KV, D_MODEL), jnp.float32), 'wq': jax.random.normal(ks[2], (D_MODEL, N_HEADS * D_KV), jnp.float32) * s, 'wk': jax.random.normal(ks[3], (D_MODEL, N_HEADS * D_KV), jnp.float32) * s, 'wv': jax.random.normal(ks[4], (D_MODEL, N_HEADS * D_KV), jnp.float32) * s, 'wo': jax.random.normal(ks[5], (N_HEADS * D_KV, D_MODEL), jnp.float32) * s, 'norm_w': jnp.ones((D_MODEL,), jnp.float32)}
    _L0_xattn_all = _L0_xattn_setup()
    _L0_xattn_in = {k: v for k, v in _L0_xattn_all.items() if k in ('wq', 'wk', 'wv', 'wo', 'norm_w')}
    del _L0_xattn_all

    def _L1_xattn_setup():
        import jax, jax.numpy as jnp
        import numpy as np
        B, LX, LY = (2, 256, 256)
        E, H = (128, 16)
        HD = E // H
        FF = 512
        EPS = 1e-05

        def _rope_tables(L, d):
            inv = 1.0 / 10000.0 ** (jnp.arange(0, d, 2, dtype=jnp.float32) / d)
            t = jnp.arange(L, dtype=jnp.float32)
            f = jnp.outer(t, inv)
            return (jnp.cos(f), jnp.sin(f))

        def _apply_rope(x, cos, sin):
            d2 = x.shape[-1] // 2
            x1, x2 = (x[..., :d2], x[..., d2:])
            c = cos[None, :, None, :]
            s = sin[None, :, None, :]
            return jnp.concatenate([x1 * c - x2 * s, x2 * c + x1 * s], axis=-1)

        def _ln(x, g, b):
            m = jnp.mean(x, axis=-1, keepdims=True)
            v = jnp.var(x, axis=-1, keepdims=True)
            return (x - m) / jnp.sqrt(v + EPS) * g + b

        def _attn(q, k, v, causal):
            s = jnp.einsum('blhd,bmhd->bhlm', q, k)
            if causal:
                Lq, Lk = (s.shape[2], s.shape[3])
                mask = jnp.tril(jnp.ones((Lq, Lk), dtype=bool))
                s = jnp.where(mask, s, -jnp.inf)
            p = jax.nn.softmax(s, axis=-1)
            return jnp.einsum('bhlm,bmhd->blhd', p, v)

        def _forward(x, y, ln1_g, ln1_b, sa_wq, sa_bq, sa_wk, sa_bk, sa_wv, sa_bv, sa_wo, sa_bo, ln2_g, ln2_b, ca_wq, ca_bq, ca_wk, ca_bk, ca_wv, ca_bv, ca_wo, ca_bo, ln3_g, ln3_b, fc1_w, fc1_b, fc2_w, fc2_b):
            Bx, Lx, _ = x.shape
            Ly = y.shape[1]
            cos, sin = _rope_tables(max(Lx, Ly), HD)
            scale = HD ** (-0.5)
            h = _ln(x, ln1_g, ln1_b)
            q = (h @ sa_wq + sa_bq).reshape(Bx, Lx, H, HD) * scale
            k = (h @ sa_wk + sa_bk).reshape(Bx, Lx, H, HD)
            v = (h @ sa_wv + sa_bv).reshape(Bx, Lx, H, HD)
            q = _apply_rope(q, cos[:Lx], sin[:Lx])
            k = _apply_rope(k, cos[:Lx], sin[:Lx])
            a = _attn(q, k, v, causal=True).reshape(Bx, Lx, E)
            x = x + (a @ sa_wo + sa_bo)
            h = _ln(x, ln2_g, ln2_b)
            q = (h @ ca_wq + ca_bq).reshape(Bx, Lx, H, HD) * scale
            k = (y @ ca_wk + ca_bk).reshape(Bx, Ly, H, HD)
            v = (y @ ca_wv + ca_bv).reshape(Bx, Ly, H, HD)
            q = _apply_rope(q, cos[:Lx], sin[:Lx])
            k = _apply_rope(k, cos[:Ly], sin[:Ly])
            a = _attn(q, k, v, causal=False).reshape(Bx, Lx, E)
            x = x + (a @ ca_wo + ca_bo)
            h = _ln(x, ln3_g, ln3_b)
            return x + (jax.nn.gelu(h @ fc1_w + fc1_b) @ fc2_w + fc2_b)
        key = jax.random.key(seed)
        ks = jax.random.split(key, 16)

        def w(k, *s):
            return jax.random.normal(k, s, jnp.float32) * 0.02
        z = lambda *s: jnp.zeros(s, jnp.float32)
        o = lambda *s: jnp.ones(s, jnp.float32)
        return {'x': jax.random.normal(ks[0], (B, LX, E), jnp.float32), 'y': jax.random.normal(ks[1], (B, LY, E), jnp.float32), 'ln1_g': o(E), 'ln1_b': z(E), 'sa_wq': w(ks[2], E, E), 'sa_bq': z(E), 'sa_wk': w(ks[3], E, E), 'sa_bk': z(E), 'sa_wv': w(ks[4], E, E), 'sa_bv': z(E), 'sa_wo': w(ks[5], E, E), 'sa_bo': z(E), 'ln2_g': o(E), 'ln2_b': z(E), 'ca_wq': w(ks[6], E, E), 'ca_bq': z(E), 'ca_wk': w(ks[7], E, E), 'ca_bk': z(E), 'ca_wv': w(ks[8], E, E), 'ca_bv': z(E), 'ca_wo': w(ks[9], E, E), 'ca_bo': z(E), 'ln3_g': o(E), 'ln3_b': z(E), 'fc1_w': w(ks[10], E, FF), 'fc1_b': z(FF), 'fc2_w': w(ks[11], FF, E), 'fc2_b': z(E)}
    _L1_xattn_all = _L1_xattn_setup()
    _L1_xattn_in = {k: v for k, v in _L1_xattn_all.items() if k in ('ln1_g', 'ln1_b', 'sa_wq', 'sa_bq', 'sa_wk', 'sa_bk', 'sa_wv', 'sa_bv', 'sa_wo', 'sa_bo', 'ln2_g', 'ln2_b', 'ca_wq', 'ca_bq', 'ca_wk', 'ca_bk', 'ca_wv', 'ca_bv', 'ca_wo', 'ca_bo', 'ln3_g', 'ln3_b', 'fc1_w', 'fc1_b', 'fc2_w', 'fc2_b')}
    del _L1_xattn_all
    return {'x': x, 'ctx_1024': ctx_1024, 'L0_xattn_wq': _L0_xattn_in['wq'], 'L0_xattn_wk': _L0_xattn_in['wk'], 'L0_xattn_wv': _L0_xattn_in['wv'], 'L0_xattn_wo': _L0_xattn_in['wo'], 'L0_xattn_norm_w': _L0_xattn_in['norm_w'], 'L1_xattn_ln1_g': _L1_xattn_in['ln1_g'], 'L1_xattn_ln1_b': _L1_xattn_in['ln1_b'], 'L1_xattn_sa_wq': _L1_xattn_in['sa_wq'], 'L1_xattn_sa_bq': _L1_xattn_in['sa_bq'], 'L1_xattn_sa_wk': _L1_xattn_in['sa_wk'], 'L1_xattn_sa_bk': _L1_xattn_in['sa_bk'], 'L1_xattn_sa_wv': _L1_xattn_in['sa_wv'], 'L1_xattn_sa_bv': _L1_xattn_in['sa_bv'], 'L1_xattn_sa_wo': _L1_xattn_in['sa_wo'], 'L1_xattn_sa_bo': _L1_xattn_in['sa_bo'], 'L1_xattn_ln2_g': _L1_xattn_in['ln2_g'], 'L1_xattn_ln2_b': _L1_xattn_in['ln2_b'], 'L1_xattn_ca_wq': _L1_xattn_in['ca_wq'], 'L1_xattn_ca_bq': _L1_xattn_in['ca_bq'], 'L1_xattn_ca_wk': _L1_xattn_in['ca_wk'], 'L1_xattn_ca_bk': _L1_xattn_in['ca_bk'], 'L1_xattn_ca_wv': _L1_xattn_in['ca_wv'], 'L1_xattn_ca_bv': _L1_xattn_in['ca_bv'], 'L1_xattn_ca_wo': _L1_xattn_in['ca_wo'], 'L1_xattn_ca_bo': _L1_xattn_in['ca_bo'], 'L1_xattn_ln3_g': _L1_xattn_in['ln3_g'], 'L1_xattn_ln3_b': _L1_xattn_in['ln3_b'], 'L1_xattn_fc1_w': _L1_xattn_in['fc1_w'], 'L1_xattn_fc1_b': _L1_xattn_in['fc1_b'], 'L1_xattn_fc2_w': _L1_xattn_in['fc2_w'], 'L1_xattn_fc2_b': _L1_xattn_in['fc2_b']}

def reference(x, ctx_1024, L0_xattn_wq, L0_xattn_wk, L0_xattn_wv, L0_xattn_wo, L0_xattn_norm_w, L1_xattn_ln1_g, L1_xattn_ln1_b, L1_xattn_sa_wq, L1_xattn_sa_bq, L1_xattn_sa_wk, L1_xattn_sa_bk, L1_xattn_sa_wv, L1_xattn_sa_bv, L1_xattn_sa_wo, L1_xattn_sa_bo, L1_xattn_ln2_g, L1_xattn_ln2_b, L1_xattn_ca_wq, L1_xattn_ca_bq, L1_xattn_ca_wk, L1_xattn_ca_bk, L1_xattn_ca_wv, L1_xattn_ca_bv, L1_xattn_ca_wo, L1_xattn_ca_bo, L1_xattn_ln3_g, L1_xattn_ln3_b, L1_xattn_fc1_w, L1_xattn_fc1_b, L1_xattn_fc2_w, L1_xattn_fc2_b):
    import jax
    import jax.numpy as jnp

    def _L0_xattn_ref(hidden_states, key_value_states, wq, wk, wv, wo, norm_w):
        import jax, jax.numpy as jnp
        import numpy as np
        B, Q, KV = (2, 256, 256)
        D_MODEL = 128
        N_HEADS = 16
        D_KV = 64
        EPS = 1e-06
        var = jnp.mean(jnp.square(hidden_states), axis=-1, keepdims=True)
        normed = hidden_states * jax.lax.rsqrt(var + EPS) * norm_w
        b, q_len, _ = hidden_states.shape
        kv_len = key_value_states.shape[1]

        def split_heads(x):
            return x.reshape(b, -1, N_HEADS, D_KV).transpose(0, 2, 1, 3)
        q = split_heads(normed @ wq)
        k = split_heads(key_value_states @ wk)
        v = split_heads(key_value_states @ wv)
        scores = jnp.einsum('bhqd,bhkd->bhqk', q, k)
        attn = jax.nn.softmax(scores.astype(jnp.float32), axis=-1).astype(scores.dtype)
        ctx = jnp.einsum('bhqk,bhkd->bhqd', attn, v)
        ctx = ctx.transpose(0, 2, 1, 3).reshape(b, q_len, N_HEADS * D_KV)
        attn_out = ctx @ wo
        return hidden_states + attn_out

    def _L1_xattn_ref(x, y, ln1_g, ln1_b, sa_wq, sa_bq, sa_wk, sa_bk, sa_wv, sa_bv, sa_wo, sa_bo, ln2_g, ln2_b, ca_wq, ca_bq, ca_wk, ca_bk, ca_wv, ca_bv, ca_wo, ca_bo, ln3_g, ln3_b, fc1_w, fc1_b, fc2_w, fc2_b):
        import jax, jax.numpy as jnp
        import numpy as np
        B, LX, LY = (2, 256, 256)
        E, H = (128, 16)
        HD = E // H
        FF = 512
        EPS = 1e-05

        def _rope_tables(L, d):
            inv = 1.0 / 10000.0 ** (jnp.arange(0, d, 2, dtype=jnp.float32) / d)
            t = jnp.arange(L, dtype=jnp.float32)
            f = jnp.outer(t, inv)
            return (jnp.cos(f), jnp.sin(f))

        def _apply_rope(x, cos, sin):
            d2 = x.shape[-1] // 2
            x1, x2 = (x[..., :d2], x[..., d2:])
            c = cos[None, :, None, :]
            s = sin[None, :, None, :]
            return jnp.concatenate([x1 * c - x2 * s, x2 * c + x1 * s], axis=-1)

        def _ln(x, g, b):
            m = jnp.mean(x, axis=-1, keepdims=True)
            v = jnp.var(x, axis=-1, keepdims=True)
            return (x - m) / jnp.sqrt(v + EPS) * g + b

        def _attn(q, k, v, causal):
            s = jnp.einsum('blhd,bmhd->bhlm', q, k)
            if causal:
                Lq, Lk = (s.shape[2], s.shape[3])
                mask = jnp.tril(jnp.ones((Lq, Lk), dtype=bool))
                s = jnp.where(mask, s, -jnp.inf)
            p = jax.nn.softmax(s, axis=-1)
            return jnp.einsum('bhlm,bmhd->blhd', p, v)

        def _forward(x, y, ln1_g, ln1_b, sa_wq, sa_bq, sa_wk, sa_bk, sa_wv, sa_bv, sa_wo, sa_bo, ln2_g, ln2_b, ca_wq, ca_bq, ca_wk, ca_bk, ca_wv, ca_bv, ca_wo, ca_bo, ln3_g, ln3_b, fc1_w, fc1_b, fc2_w, fc2_b):
            Bx, Lx, _ = x.shape
            Ly = y.shape[1]
            cos, sin = _rope_tables(max(Lx, Ly), HD)
            scale = HD ** (-0.5)
            h = _ln(x, ln1_g, ln1_b)
            q = (h @ sa_wq + sa_bq).reshape(Bx, Lx, H, HD) * scale
            k = (h @ sa_wk + sa_bk).reshape(Bx, Lx, H, HD)
            v = (h @ sa_wv + sa_bv).reshape(Bx, Lx, H, HD)
            q = _apply_rope(q, cos[:Lx], sin[:Lx])
            k = _apply_rope(k, cos[:Lx], sin[:Lx])
            a = _attn(q, k, v, causal=True).reshape(Bx, Lx, E)
            x = x + (a @ sa_wo + sa_bo)
            h = _ln(x, ln2_g, ln2_b)
            q = (h @ ca_wq + ca_bq).reshape(Bx, Lx, H, HD) * scale
            k = (y @ ca_wk + ca_bk).reshape(Bx, Ly, H, HD)
            v = (y @ ca_wv + ca_bv).reshape(Bx, Ly, H, HD)
            q = _apply_rope(q, cos[:Lx], sin[:Lx])
            k = _apply_rope(k, cos[:Ly], sin[:Ly])
            a = _attn(q, k, v, causal=False).reshape(Bx, Lx, E)
            x = x + (a @ ca_wo + ca_bo)
            h = _ln(x, ln3_g, ln3_b)
            return x + (jax.nn.gelu(h @ fc1_w + fc1_b) @ fc2_w + fc2_b)
        return _forward(x, y, ln1_g, ln1_b, sa_wq, sa_bq, sa_wk, sa_bk, sa_wv, sa_bv, sa_wo, sa_bo, ln2_g, ln2_b, ca_wq, ca_bq, ca_wk, ca_bk, ca_wv, ca_bv, ca_wo, ca_bo, ln3_g, ln3_b, fc1_w, fc1_b, fc2_w, fc2_b)
    x = _L0_xattn_ref(x, ctx_1024, L0_xattn_wq, L0_xattn_wk, L0_xattn_wv, L0_xattn_wo, L0_xattn_norm_w)
    x = _L1_xattn_ref(x, ctx_1024, L1_xattn_ln1_g, L1_xattn_ln1_b, L1_xattn_sa_wq, L1_xattn_sa_bq, L1_xattn_sa_wk, L1_xattn_sa_bk, L1_xattn_sa_wv, L1_xattn_sa_bv, L1_xattn_sa_wo, L1_xattn_sa_bo, L1_xattn_ln2_g, L1_xattn_ln2_b, L1_xattn_ca_wq, L1_xattn_ca_bq, L1_xattn_ca_wk, L1_xattn_ca_bk, L1_xattn_ca_wv, L1_xattn_ca_bv, L1_xattn_ca_wo, L1_xattn_ca_bo, L1_xattn_ln3_g, L1_xattn_ln3_b, L1_xattn_fc1_w, L1_xattn_fc1_b, L1_xattn_fc2_w, L1_xattn_fc2_b)
    return x

_drawn_inputs = setup_inputs


def setup_inputs(seed=0):
    import zlib

    import numpy as np

    out = dict(_drawn_inputs(seed))
    spreads = {'L0_xattn_norm_w': (1.0, 0.6),
     'L1_xattn_ln1_g': (1.0, 0.6),
     'L1_xattn_ln1_b': (0.0, 0.8),
     'L1_xattn_sa_bq': (0.0, 0.8),
     'L1_xattn_sa_bk': (0.0, 0.8),
     'L1_xattn_sa_bv': (0.0, 0.391),
     'L1_xattn_sa_bo': (0.0, 0.1),
     'L1_xattn_ln2_g': (1.0, 0.6),
     'L1_xattn_ln2_b': (0.0, 2.0),
     'L1_xattn_ca_bq': (0.0, 2.0),
     'L1_xattn_ca_bk': (0.0, 2.0),
     'L1_xattn_ca_bv': (0.0, 0.332),
     'L1_xattn_ca_bo': (0.0, 0.1),
     'L1_xattn_ln3_g': (1.0, 0.6),
     'L1_xattn_ln3_b': (0.0, 0.8),
     'L1_xattn_fc1_b': (0.0, 0.346),
     'L1_xattn_fc2_b': (0.0, 0.1)}
    factors = {'L0_xattn_wq': 4.947,
     'L0_xattn_wk': 4.935,
     'L1_xattn_sa_wq': 8.0,
     'L1_xattn_sa_wk': 8.0,
     'L1_xattn_sa_wv': 5.369,
     'L1_xattn_ca_wq': 8.0,
     'L1_xattn_ca_wk': 8.0}
    for name, (base, spread) in spreads.items():
        noise = np.random.default_rng([zlib.crc32(name.encode()), seed]).standard_normal(out[name].shape)
        drawn = base * np.exp(spread * noise) if base else spread * noise
        out[name] = jnp.asarray(drawn.astype(out[name].dtype))
    for name, factor in factors.items():
        out[name] = (out[name] * factor).astype(out[name].dtype)
    return out
```

```python
from contextlib import ExitStack

import numpy as np

import concourse.bass as bass
from concourse import mybir

F32 = mybir.dt.float32
F32R = mybir.dt.float32r
BF16 = mybir.dt.bfloat16
ALU = mybir.AluOpType
ACT = mybir.ActivationFunctionType
AX = mybir.AxisListType
ds = bass.ds

P = 128
B, LQ, D = 8, 256, 128
LK = 1601
QT = LQ // P
KT = (LK + P - 1) // P
LAST = LK - (KT - 1) * P
NCH = 4
CH = (LK + NCH - 1) // NCH
CH += CH % 2
CSTART = [min(c * CH, LK - CH) for c in range(NCH)]
CSKIP = [c * CH - CSTART[c] for c in range(NCH)]
H0, HD0 = 16, 64
NP0 = H0 // 2
TG = 4
GROUPS = [list(range(g, min(g + TG, KT))) for g in range(0, KT, TG)]
NG = len(GROUPS)
UNITS = 2 * QT
H1, HD1 = 16, 8
KVG = [list(range(t, min(t + 2, KT))) for t in range(0, KT, 2)]
HG = 4
G1 = H1 // HG
R = HG * HD1
NEG = -1e30


def width(kt):
    return LAST if kt == KT - 1 else P


def row_everywhere(row):
    return row.rearrange("(o n) -> o n", o=1).broadcast_to([P, row.shape[0]])


def layer0_setup(nc, x, norm_w, wq, wk, ident, xs, xnT, M, identf, epsc):
    NT = B * QT
    with ExitStack() as ctx:
        def sb(name, shape, dt=F32):
            return ctx.enter_context(nc.sbuf_tensor(name, shape, dt))

        def sem(name):
            return ctx.enter_context(nc.semaphore(name))

        wq_sb = sb("wq_sb", [P, H0 * HD0])
        wk_sb = sb("wk_sb", [P, H0 * HD0])
        wqT = sb("wqT", [P, NP0, D])
        wkT = sb("wkT", [P, NP0, D])
        sq = sb("sq", [P, NT * D])
        ms = sb("ms", [P, 4, NT])
        nw = sb("nw", [P, 1])
        banks = [ctx.enter_context(nc.psum_tensor(f"a_bank{i}", [P, 512], F32)) for i in range(8)]

        x_in, w_in, c_in = sem("x_in"), sem("w_in"), sem("c_in")
        squared, meansq, rms, inv, normed = sem("squared"), sem("meansq"), sem("rms"), sem("inv"), sem("normed")
        wT_mm, wT_act, wT_dve = sem("wT_mm"), sem("wT_act"), sem("wT_dve")
        m_mm, m_ev = sem("m_mm"), sem("m_ev")
        xt_mm, xt_ev = sem("xt_mm"), sem("xt_ev")
        block = ctx.enter_context(nc.Block())

        @block.sync
        def _(sp):
            sp.dma_start(identf[:], ident).then_inc(c_in, 16)
            sp.dma_start(wq_sb[:], wq).then_inc(w_in, 16)
            sp.dma_start(wk_sb[:], wk).then_inc(w_in, 16)
            sp.dma_start(xs[:].rearrange("p (t d) -> p t d", d=D),
                         x.rearrange("b (t p) d -> p (b t) d", p=P)).then_inc(x_in, 16)
            sp.dma_start(nw[:], norm_w.rearrange("(p o) -> p o", o=1)).then_inc(c_in, 16)

        @block.vector
        def _(dve):
            dve.wait_ge(wT_mm, 2)
            nc.vector.tensor_copy(wqT[:, 4:8, :], banks[1][:].rearrange("p (n d) -> p n d", d=D)).then_inc(wT_dve, 1)
            dve.wait_ge(wT_mm, 4)
            nc.vector.tensor_copy(wkT[:, 4:8, :], banks[3][:].rearrange("p (n d) -> p n d", d=D)).then_inc(wT_dve, 1)
            dve.wait_ge(x_in, 16)
            nc.vector.memset(epsc[:], 1e-6)
            nc.vector.tensor_tensor(sq[:], xs[:], xs[:], ALU.mult).then_inc(squared, 1)
            dve.wait_ge(squared, 1)
            nc.vector.tensor_reduce(ms[:, 0, :], sq[:].rearrange("p (t d) -> p t d", d=D), AX.X, ALU.add).then_inc(meansq, 1)
            dve.wait_ge(rms, 1)
            nc.vector.reciprocal(ms[:, 2, :], ms[:, 1, :]).then_inc(inv, 1)
            dve.wait_ge(inv, 1)
            nc.vector.tensor_tensor(sq[:].rearrange("p (t d) -> p t d", d=D), xs[:].rearrange("p (t d) -> p t d", d=D),
                                    ms[:, 2, :].unsqueeze(2).broadcast_to([P, NT, D]), ALU.mult).then_inc(normed, 1)
            for g in range(4):
                dve.wait_ge(m_mm, g + 1)
                nc.vector.tensor_copy(M[:].rearrange("p (n r d) -> p n r d", r=2, d=D)[:, 4 * (g // 2):4 * (g // 2) + 4, g % 2, :],
                                      banks[4 + g % 2][:].rearrange("p (n d) -> p n d", d=D)).then_inc(m_ev, 1)

        @block.scalar
        def _(act):
            act.wait_ge(wT_mm, 1)
            nc.scalar.copy(wqT[:, 0:4, :], banks[0][:].rearrange("p (n d) -> p n d", d=D)).then_inc(wT_act, 1)
            act.wait_ge(wT_mm, 3)
            nc.scalar.copy(wkT[:, 0:4, :], banks[2][:].rearrange("p (n d) -> p n d", d=D)).then_inc(wT_act, 1)
            act.wait_ge(meansq, 1)
            nc.scalar.activation(ms[:, 1, :], ms[:, 0, :], ACT.Sqrt, bias=epsc[:], scale=1.0 / D).then_inc(rms, 1)
            act.wait_ge(c_in, 32)
            for g in range(4):
                act.wait_ge(xt_mm, g + 1)
                nc.scalar.activation(xnT[:, g * 512:(g + 1) * 512], banks[6 + g % 2][:], ACT.Copy,
                                     scale=nw[:]).then_inc(xt_ev, 1)

        @block.tensor
        def _(pe):
            pe.wait_ge(c_in, 32)
            pe.wait_ge(w_in, 32)
            for w, src in enumerate((wq_sb, wk_sb)):
                for n in range(NP0):
                    last = nc.tensor.transpose(banks[2 * w + n // 4][:, (n % 4) * D:(n % 4 + 1) * D],
                                               src[:, n * P:(n + 1) * P], identf[:])
                    if n % 4 == 3:
                        last.then_inc(wT_mm, 1)
            pe.wait_ge(wT_act, 2)
            pe.wait_ge(wT_dve, 2)
            for g in range(4):
                if g >= 2:
                    pe.wait_ge(m_ev, g - 1)
                rows = slice((g % 2) * HD0, (g % 2 + 1) * HD0)
                for i in range(4):
                    n = 4 * (g // 2) + i
                    last = nc.tensor.matmul(banks[4 + g % 2][:, i * D:(i + 1) * D], wqT[rows, n, :],
                                            wkT[rows, n, :], start=True, stop=True)
                last.then_inc(m_mm, 1)
            pe.wait_ge(normed, 1)
            for g in range(4):
                if g >= 2:
                    pe.wait_ge(xt_ev, g - 1)
                for i in range(4):
                    t = 4 * g + i
                    last = nc.tensor.transpose(banks[6 + g % 2][:, i * D:(i + 1) * D], sq[:, t * D:(t + 1) * D], identf[:])
                last.then_inc(xt_mm, 1)


def layer0_attention(nc, ctx_in, wv, wo, cross_wk, cross_wv, cross_bk, cross_bv, cos_k, sin_k, kv_dram, xs, xnT, M, identf):
    with ExitStack() as ctx:
        def sb(name, shape, dt=F32):
            return ctx.enter_context(nc.sbuf_tensor(name, shape, dt))

        def sem(name):
            return ctx.enter_context(nc.semaphore(name))

        tok = sb("ctx_tok", [P, KT, D])
        cT = sb("cT", [P, LK + 1])
        cTh = sb("cTh", [P, LK + 1], F32R)
        cTl = sb("cTl", [P, LK + 1], F32R)
        wv_sb = sb("wv_sb", [P, H0 * HD0])
        wo_sb = sb("wo_sb", [P, NP0, D])
        Mr = sb("Mr", [P, 2, 2 * D])
        qh = sb("qh", [P, 2, 2, LQ], F32R)
        ql = sb("ql", [P, 2, 2, LQ], F32R)
        prob = sb("prob", [P, 2, KT * P])
        pT = [[sb(f"pT{s}{h}", [P, KT, LQ]) for h in range(2)] for s in range(2)]
        V = sb("V0", [P, 2, KT, P])
        OA = sb("OA", [P, 2, LQ])
        wkv = sb("wkv", [P, 2 * D])
        bkv = sb("bkv", [P, 2 * D])
        cosk = sb("cosk", [P, KT, HD1])
        sink = sb("sink", [P, KT, HD1])
        kv = sb("kv", [P, KT, 2 * D])
        rot = sb("rot", [P, KT, D])
        mx4 = sb("mx4", [P, 2, NCH])
        negm = sb("negm", [P, 2])
        dens = sb("dens", [P, 2, UNITS, NCH])
        den = sb("den", [P, 2, UNITS])
        rden = sb("rden", [P, 2, UNITS])
        S = ctx.enter_context(nc.psum_tensor("S0", [P, NCH, 512], F32))
        tb = [ctx.enter_context(nc.psum_tensor(f"tb{i}", [P, 512], F32)) for i in range(2)]
        pO = ctx.enter_context(nc.psum_tensor("pO", [P, 512], F32))
        pX = ctx.enter_context(nc.psum_tensor("pX", [P, 512], F32))

        w_in, tok_in = sem("w_in0"), sem("tok_in")
        m_in = [sem(f"m_in{i}") for i in range(2)]
        zeroed = sem("zeroed")
        ct_mm, ct_ev, ct_hi, ct_lo = sem("ct_mm"), sem("ct_ev"), sem("ct_hi"), sem("ct_lo")
        q_mm, q_hi, q_lo = sem("q_mm"), sem("q_hi"), sem("q_lo")
        s_mm = sem("s_mm")
        mx_c, mx = sem("mx_c"), sem("mx")
        ex = sem("ex")
        t_mm = sem("t_mm")
        t_act, t_dve = sem("t_act"), sem("t_dve")
        v_mm, v_act, v_dve = sem("v_mm"), sem("v_act"), sem("v_dve")
        o_mm, o_ev = sem("o_mm"), sem("o_ev")
        y_mm, y_add = sem("y_mm"), sem("y_add")
        kv_mm, kv_ev, kv_bias, kv_rot, kv_cos, kv_done, kv_out = (
            sem("kv_mm"), sem("kv_ev"), sem("kv_bias"), sem("kv_rot"), sem("kv_cos"), sem("kv_done"), sem("kv_out"))
        padded = sem("padded")
        den_s, den_r, added = sem("den_s"), sem("den_r"), sem("added")
        kv_banks = [tb[0], tb[1], pO]
        block = ctx.enter_context(nc.Block())

        NU = NP0 * UNITS

        def walk(eng, pair, first=None, last=None):
            pair(0, 0, False, True)
            with eng.Fori(0, (NP0 - 2) // 2) as j:
                pair(2 * j + 1, 1, True, True)
                pair(2 * j + 2, 0, True, True)
            pair(NP0 - 1, 1, True, False)

        @block.sync
        def _(sp):
            sp.sem_inc(kv_out, 1)
            sp.dma_start(wv_sb[:], wv).then_inc(w_in, 16)
            sp.dma_start(wo_sb[:], wo.rearrange("(n p) d -> p n d", p=P)).then_inc(w_in, 16)
            for i, (w, bias) in enumerate(((cross_wk, cross_bk), (cross_wv, cross_bv))):
                sp.dma_start(wkv[:, i * D:(i + 1) * D], w).then_inc(w_in, 16)
                sp.dma_start(bkv[:, i * D:(i + 1) * D], row_everywhere(bias)).then_inc(w_in, 16)
            sp.dma_start(cosk[:], cos_k).then_inc(w_in, 16)
            sp.dma_start(sink[:], sin_k).then_inc(w_in, 16)
            with sp.Fori(0, B) as b:
                sp.wait_ge(ct_mm, 1 + b * NG)
                sp.dma_start(tok[:, 0:KT - 1, :],
                             ctx_in[ds(b, 1), 0:(KT - 1) * P, :].rearrange("b (t p) d -> p (b t) d", p=P)).then_inc(tok_in, 16)
                sp.dma_start(tok[0:LAST, KT - 1, :],
                             ctx_in[ds(b, 1), (KT - 1) * P:LK, :].rearrange("b p d -> p (b d)")).then_inc(tok_in, 16)
                for p in range(2):
                    sp.wait_ge(q_mm, 1 + b * NP0)
                    sp.dma_start(Mr[:, p, :], M[:, p * 2 * D:(p + 1) * 2 * D]).then_inc(m_in[p], 16)

                def refill(p, slot, has_prev, has_next):
                    sp.wait_ge(q_mm, 1 + b * NP0 + p + 1)
                    sp.dma_start(Mr[:, slot, :], M[:, ds((p + 2) * 2 * D, 2 * D)]).then_inc(m_in[slot], 16)
                sp.wait_ge(kv_done, b + 1)
                sp.dma_start(kv_dram[ds(b, 1)].rearrange("b p n -> p (b n)"),
                             kv[:].rearrange("p t n -> p (t n)")).then_inc(kv_out, 16)
                with sp.Fori(0, (NP0 - 2) // 2) as j:
                    refill(2 * j, 0, True, True)
                    refill(2 * j + 1, 1, True, True)
            sp.wait_ge(kv_out, 1 + 16 * B)

        @block.gpsimd
        def _(pool):
            nc.gpsimd.memset(kv[LAST // 32 * 32:, KT - 1, :], 0.0).then_inc(padded, 1)
            pool.wait_ge(w_in, 8 * 16)
            heads = kv[:, :, 0:D].rearrange("p t (h e) -> p t h e", e=HD1)
            rheads = rot[:].rearrange("p t (h e) -> p t h e", e=HD1)
            half = HD1 // 2
            with pool.Fori(0, B) as b:
                pool.wait_ge(kv_ev, (b + 1) * len(KVG))
                nc.gpsimd.tensor_tensor(kv[:], kv[:], bkv[:].unsqueeze(1).broadcast_to([P, KT, 2 * D]),
                                        ALU.add).then_inc(kv_bias, 1)
                pool.wait_ge(kv_bias, b + 1)
                for lo, hi in ((0, half), (half, 0)):
                    last = nc.gpsimd.tensor_tensor(rheads[:, :, :, lo:lo + half], heads[:, :, :, hi:hi + half],
                                                   sink[:, :, lo:lo + half].unsqueeze(2).broadcast_to([P, KT, H1, half]), ALU.mult)
                last.then_inc(kv_rot, 1)
                pool.wait_ge(kv_rot, b + 1)
                nc.gpsimd.tensor_tensor(heads, heads, cosk[:].unsqueeze(2).broadcast_to([P, KT, H1, HD1]), ALU.mult).then_inc(kv_cos, 1)
                pool.wait_ge(kv_cos, b + 1)
                nc.gpsimd.tensor_tensor(kv[:, :, 0:D], kv[:, :, 0:D], rot[:], ALU.add).then_inc(kv_done, 1)

        @block.tensor
        def _(pe):
            pe.sem_inc(ct_mm, 1)
            pe.sem_inc(q_mm, 1)
            pe.sem_inc(y_mm, 1)
            pe.wait_ge(w_in, 8 * 16)

            def make_q(b, p, slot, nbefore):
                pe.wait_ge(m_in[slot], 8 * (b * NP0 + p - slot) + 16)
                pe.wait_ge(y_add, 1 + nbefore)
                for h in range(2):
                    last = nc.tensor.matmul(pX[:, h * LQ:(h + 1) * LQ], Mr[:, slot, h * D:(h + 1) * D],
                                            xnT[:, ds(b * LQ, LQ)], start=True, stop=True)
                last.then_inc(q_mm, 1)

            def scores(c, slot, u):
                h, qt = u // QT, u % QT
                k = slice(CSTART[c], CSTART[c] + CH)
                q = slice(qt * P, (qt + 1) * P)
                nc.tensor.matmul(S[:, c, 0:CH], qh[:, slot, h, q], cTh[:, k], start=True, stop=False)
                nc.tensor.matmul(S[:, c, 0:CH], ql[:, slot, h, q], cTh[:, k], start=False, stop=False)
                nc.tensor.matmul(S[:, c, 0:CH], qh[:, slot, h, q], cTl[:, k], start=False, stop=True).then_inc(s_mm, 1)

            def make_v(b, p, g, slot, has_next=True):
                if g == 0 and has_next:
                    pe.wait_ge(q_lo, b * NP0 + p + 2)
                elif g == 0:
                    pe.wait_ge(y_add, 1 + b * NP0 + p - 1)
                elif g % 2:
                    pe.wait_ge(v_act, (b * NP0 + p) * 2 + g // 2 + 1)
                else:
                    pe.wait_ge(v_dve, (b * NP0 + p) * 2 + g // 2)
                for i, kt in enumerate(GROUPS[g]):
                    w = width(kt)
                    last = nc.tensor.matmul(pX[0:w, i * P:(i + 1) * P], cT[:, kt * P:kt * P + w],
                                            wv_sb[:, ds(p * P, P)], start=True, stop=True)
                last.then_inc(v_mm, 1)

            def values(prev, kts):
                for kt in kts:
                    w = width(kt)
                    for h in range(2):
                        last = nc.tensor.matmul(pO[h * HD0:(h + 1) * HD0, 0:LQ], V[0:w, prev, kt, h * HD0:(h + 1) * HD0],
                                                pT[prev][h][0:w, kt, :], start=kt == 0, stop=kt == KT - 1)
                if kts[-1] == KT - 1:
                    last.then_inc(o_mm, 1)

            def project(b, pp):
                pe.wait_ge(o_ev, 1 + 2 * (b * NP0 + pp + 1))
                for h in range(2):
                    for qt in range(QT):
                        i = h * QT + qt
                        last = nc.tensor.matmul(pX[:, i * D:(i + 1) * D], OA[:, h, qt * P:(qt + 1) * P],
                                                wo_sb[:, ds(pp, 1), :].rearrange("p a d -> p (a d)"), start=True, stop=True)
                last.then_inc(y_mm, 1)

            with pe.Fori(0, B) as b:
                pe.wait_ge(tok_in, 32 * (b + 1))
                pe.wait_ge(y_add, 1 + b * NP0)
                for g, kts in enumerate(GROUPS):
                    for i, kt in enumerate(kts):
                        w = width(kt)
                        last = nc.tensor.transpose(S[:, g, i * P:i * P + w], tok[0:w, kt, :], identf[0:w, 0:w])
                    last.then_inc(ct_mm, 1)
                make_q(b, 0, 0, b * NP0)
                pe.wait_ge(ct_ev, (b + 1) * NG)
                for i, kts in enumerate(KVG):
                    if i >= len(kv_banks):
                        pe.wait_ge(kv_ev, b * len(KVG) + i - len(kv_banks) + 1)
                    for n, kt in enumerate(kts):
                        w = width(kt)
                        last = nc.tensor.matmul(kv_banks[i % 3][0:w, n * 2 * D:(n + 1) * 2 * D], cT[:, kt * P:kt * P + w],
                                                wkv[:], start=True, stop=True)
                    last.then_inc(kv_mm, 1)
                pe.wait_ge(kv_ev, (b + 1) * len(KVG))
                pe.wait_ge(ct_lo, b + 1)
                pe.wait_ge(q_lo, b * NP0 + 1)
                for c in range(NCH):
                    scores(c, 0, 0)

                def pair(p, slot, has_prev, has_next):
                    prev = 1 - slot
                    for k in range(UNITS):
                        u = (b * NP0 + p) * UNITS + k
                        more = has_next or k < UNITS - 1
                        nslot, nu = (slot, k + 1) if k < UNITS - 1 else (prev, 0)

                        def next_scores(c):
                            if more:
                                pe.wait_ge(ex, u * NCH + c + 1)
                                scores(c, nslot, nu)

                        def turn(g):
                            pe.wait_ge(ex, u * NCH + min(NCH, (GROUPS[g][-1] * P + P - 1) // CH + 1))
                            if g >= 2:
                                pe.wait_ge((t_dve, t_act)[g % 2], 1 + u * 2 + 1)
                            else:
                                pe.wait_ge((t_dve, t_act)[g % 2], 1 + u * 2)
                            for i, kt in enumerate(GROUPS[g]):
                                w = width(kt)
                                last = nc.tensor.transpose(tb[g % 2][0:w, i * P:(i + 1) * P],
                                                           prob[:, k % 2, kt * P:kt * P + w], identf[:])
                            last.then_inc(t_mm, 1)

                        if k == UNITS - 1 and more:
                            pe.wait_ge(q_lo, b * NP0 + p + 2)
                        next_scores(0)
                        next_scores(1)
                        turn(0)
                        if k == 0 and has_next:
                            make_q(b, p + 1, prev, b * NP0 + p - 1 if has_prev else b * NP0)
                        if k == 1:
                            make_v(b, p, 1, slot)
                        if k == 2:
                            make_v(b, p, 3, slot)
                        next_scores(2)
                        turn(1)
                        next_scores(3)
                        turn(2)
                        turn(3)
                        if has_prev and k < 3:
                            if k == 0:
                                pe.wait_ge(t_act, 1 + u * 2)
                                pe.wait_ge(t_dve, 1 + u * 2)
                                pe.wait_ge(v_act, (b * NP0 + p) * 2)
                                pe.wait_ge(v_dve, (b * NP0 + p) * 2)
                                pe.wait_ge(o_ev, 1 + 2 * (b * NP0 + p - 1))
                            values(prev, ([0, 1, 2, 3, 4], [5, 6, 7, 8], [9, 10, 11, 12])[k])
                        if k == 0:
                            make_v(b, p, 0, slot, has_next)
                        if k == 1:
                            make_v(b, p, 2, slot)
                        if k == 3 and has_prev:
                            pe.wait_ge(v_dve, (b * NP0 + p) * 2 + 2)
                            project(b, p - 1)

                walk(pe, pair)
                end = (b + 1) * NP0
                pe.wait_ge(t_act, 1 + end * UNITS * 2)
                pe.wait_ge(t_dve, 1 + end * UNITS * 2)
                pe.wait_ge(o_ev, 1 + 2 * (end - 1))
                values(1, list(range(KT)))
                pe.wait_ge(y_add, 1 + end - 1)
                project(b, NP0 - 1)

        @block.scalar
        def _(act):
            act.sem_inc(t_act, 1)
            act.sem_inc(o_ev, 1)
            act.preload_act_table(ACT.Exp)

            def q_high(n, slot):
                act.wait_ge(q_mm, 1 + n + 1)
                nc.scalar.copy(qh[:, slot, :, :], pX[:].rearrange("p (h q) -> p h q", h=2)).then_inc(q_hi, 1)

            def exps(u, k, slot, chunks):
                for c in chunks:
                    if c == 0:
                        act.wait_ge(mx, u + 1)
                    lo = CSKIP[c]
                    nc.scalar.activation(prob[:, k % 2, c * CH:c * CH + CH - lo], S[:, c, lo:CH], ACT.Exp,
                                         bias=negm[:, k % 2:k % 2 + 1],
                                         accum_out=dens[:, slot, k, c:c + 1]).then_inc(ex, 1)

            def t_copy(g, u, k, slot):
                act.wait_ge(t_mm, u * NG + g + 1)
                h, qt = k // QT, k % QT
                n, w = len(GROUPS[g]), width(GROUPS[g][-1])
                nc.scalar.copy(pT[slot][h][0:w, GROUPS[g][0]:GROUPS[g][-1] + 1, qt * P:(qt + 1) * P],
                               tb[g % 2][0:w, 0:n * P].rearrange("p (n q) -> p n q", n=n)).then_inc(t_act, 1)

            def v_copy(n, g, slot):
                act.wait_ge(v_mm, n * NG + g + 1)
                nc.scalar.copy(V[:, slot, GROUPS[g][0]:GROUPS[g][-1] + 1, :],
                               pX[:].rearrange("p (n e) -> p n e", n=TG)).then_inc(v_act, 1)

            def o_copy(n):
                act.wait_ge(o_mm, n + 1)
                act.wait_ge(y_mm, 1 + n)
                act.wait_ge(zeroed, 1)
                for h in range(2):
                    r = slice(h * HD0, (h + 1) * HD0)
                    nc.scalar.copy(OA[r, h, :], pO[r, 0:LQ]).then_inc(o_ev, 1)

            with act.Fori(0, B) as b:
                for g, kts in enumerate(GROUPS):
                    act.wait_ge(ct_mm, 1 + b * NG + g + 1)
                    n = (len(kts) - 1) * P + width(kts[-1])
                    nc.scalar.copy(cT[:, kts[0] * P:kts[0] * P + n], S[:, g, 0:n]).then_inc(ct_ev, 1)
                q_high(b * NP0, 0)
                act.wait_ge(padded, 1)
                act.wait_ge(kv_out, 1 + 16 * b)
                for i, kts in enumerate(KVG):
                    act.wait_ge(kv_mm, b * len(KVG) + i + 1)
                    w, n = width(kts[-1]), len(kts)
                    nc.scalar.copy(kv[0:w, kts[0]:kts[0] + n, :],
                                   kv_banks[i % 3][0:w, 0:n * 2 * D].rearrange("p (n d) -> p n d", n=n)).then_inc(kv_ev, 1)
                exps(b * NU, 0, 0, range(NCH))

                def pair(p, slot, has_prev, has_next):
                    prev = 1 - slot
                    n = b * NP0 + p
                    for k in range(UNITS):
                        u = n * UNITS + k
                        more = has_next or k < UNITS - 1
                        nk, nslot = (k + 1, slot) if k < UNITS - 1 else (0, prev)
                        if k == 0 and has_next:
                            q_high(n + 1, prev)
                        t_copy(1, u, k, slot)
                        if more:
                            exps(u + 1, nk, nslot, [0])
                        t_copy(3, u, k, slot)
                        if more:
                            exps(u + 1, nk, nslot, [1, 2])
                        if k == 0:
                            v_copy(n, 0, slot)
                        if k == 1:
                            v_copy(n, 2, slot)
                        if k == 2 and has_prev:
                            o_copy(n - 1)
                        if more:
                            exps(u + 1, nk, nslot, [3])

                walk(act, pair)
                o_copy((b + 1) * NP0 - 1)

        @block.vector
        def _(dve):
            dve.sem_inc(t_dve, 1)
            dve.sem_inc(y_add, 1)
            nc.vector.memset(OA[:], 0.0).then_inc(zeroed, 1)

            def q_low(n, slot):
                dve.wait_ge(q_hi, n + 1)
                nc.vector.tensor_tensor(ql[:, slot, :, :], pX[:].rearrange("p (h q) -> p h q", h=2),
                                        qh[:, slot, :, :].bitcast(F32), ALU.subtract).then_inc(q_lo, 1)

            def maxima(u, k, chunks):
                for c in chunks:
                    dve.wait_ge(s_mm, u * NCH + c + 1)
                    nc.vector.reduce_max(mx4[:, k % 2, c:c + 1], S[:, c, 0:CH], AX.X).then_inc(mx_c, 1)
                if chunks[-1] == NCH - 1:
                    dve.wait_ge(mx_c, (u + 1) * NCH)
                    nc.vector.tensor_reduce(negm[:, k % 2:k % 2 + 1], mx4[:, k % 2, :], AX.X, ALU.max,
                                            negate=True).then_inc(mx, 1)

            def t_copy(g, u, k, slot):
                dve.wait_ge(t_mm, u * NG + g + 1)
                h, qt = k // QT, k % QT
                nc.vector.tensor_copy(pT[slot][h][:, GROUPS[g][0]:GROUPS[g][-1] + 1, qt * P:(qt + 1) * P],
                                      tb[g % 2][:].rearrange("p (n q) -> p n q", n=TG)).then_inc(t_dve, 1)

            def v_copy(n, g, slot):
                dve.wait_ge(v_mm, n * NG + g + 1)
                w, m = width(GROUPS[g][-1]), len(GROUPS[g])
                nc.vector.tensor_copy(V[0:w, slot, GROUPS[g][0]:GROUPS[g][-1] + 1, :],
                                      pX[0:w, 0:m * P].rearrange("p (n e) -> p n e", n=m)).then_inc(v_dve, 1)

            def sums(n, slot):
                nc.vector.tensor_reduce(den[:, slot, :], dens[:, slot, :, :], AX.X, ALU.add).then_inc(den_s, 1)
                dve.wait_ge(den_s, n + 1)
                nc.vector.reciprocal(rden[:, slot, :], den[:, slot, :]).then_inc(den_r, 1)

            def add(b, n, slot):
                dve.wait_ge(y_mm, 1 + n + 1)
                dve.wait_ge(den_r, n + 1)
                for h in range(2):
                    if h:
                        dve.wait_ge(added, n + 1)
                    for qt in range(QT):
                        i = h * QT + qt
                        xt = xs[:, ds((b * QT + qt) * D, D)]
                        last = nc.vector.scalar_tensor_tensor(xt, pX[:, i * D:(i + 1) * D], rden[:, slot, i:i + 1], xt,
                                                              ALU.mult, ALU.add)
                    if h == 0:
                        last.then_inc(added, 1)
                last.then_inc(y_add, 1)

            with dve.Fori(0, B) as b:
                dve.wait_ge(ct_ev, (b + 1) * NG)
                nc.vector.tensor_copy(cTh[:, 0:LK], cT[:, 0:LK]).then_inc(ct_hi, 1)
                dve.wait_ge(ct_hi, b + 1)
                nc.vector.tensor_tensor(cTl[:, 0:LK], cT[:, 0:LK], cTh[:, 0:LK].bitcast(F32), ALU.subtract).then_inc(ct_lo, 1)
                q_low(b * NP0, 0)
                maxima(b * NU, 0, range(NCH))

                def pair(p, slot, has_prev, has_next):
                    prev = 1 - slot
                    n = b * NP0 + p
                    for k in range(UNITS):
                        u = n * UNITS + k
                        more = has_next or k < UNITS - 1
                        if more:
                            maxima(u + 1, k + 1, [0, 1])
                        t_copy(0, u, k, slot)
                        if k == 0 and has_next:
                            q_low(n + 1, prev)
                        if k == 1:
                            v_copy(n, 1, slot)
                        if k == 2:
                            v_copy(n, 3, slot)
                        if more:
                            maxima(u + 1, k + 1, [2, 3])
                        t_copy(2, u, k, slot)
                        if k == 0 and has_prev:
                            dve.wait_ge(ex, n * UNITS * NCH)
                            sums(n - 1, prev)
                        if k == 3 and has_prev:
                            add(b, n - 1, prev)

                walk(dve, pair)
                last = (b + 1) * NP0
                dve.wait_ge(ex, last * UNITS * NCH)
                sums(last - 1, 1)
                add(b, last - 1, 1)



def normed_projection(nc, name, xs, g, beta, w, b, rope, identf, q_hi, q_lo, kv_all, eps=1e-5):
    NT = B * QT
    n = len(w)
    with ExitStack() as ctx:
        def sb(nm, shape, dt=F32):
            return ctx.enter_context(nc.sbuf_tensor(f"{name}_{nm}", shape, dt))

        def sem(nm):
            return ctx.enter_context(nc.semaphore(f"{name}_{nm}"))

        wsb = sb("w", [P, n * D])
        bsb = sb("b", [P, n * D])
        gcol, bcol, eps_c = sb("g", [P, 1]), sb("beta", [P, 1]), sb("eps", [P, 1])
        tabs = sb("tabs", [P, 4, QT * D])
        stats, mv = sb("stats", [P, NT, 6]), sb("mv", [P, NT, 2])
        std, rstd = sb("std", [P, NT]), sb("rstd", [P, NT])
        xh = sb("xh", [P, NT * D])
        hT = sb("hT", [P, NT * D])
        qs = sb("qs", [P, NT * D])
        rot = sb("rot", [P, NT * D])
        rotk = sb("rotk", [P, NT * D])
        banks = [ctx.enter_context(nc.psum_tensor(f"{name}_bank{i}", [P, 512], F32)) for i in range(8)]
        c_in, st, ag, sd, rs, xn = sem("c_in"), sem("st"), sem("ag"), sem("sd"), sem("rs"), sem("xn")
        t_mm, t_ev, p_mm, p_ev = sem("t_mm"), sem("t_ev"), sem("p_mm"), sem("p_ev")
        r1, r2, r3, r4, k1, k2 = sem("r1"), sem("r2"), sem("r3"), sem("r4"), sem("k1"), sem("k2")
        block = ctx.enter_context(nc.Block())
        loads = 2 * n + 2 + 1

        @block.sync
        def _(sp):
            for i in range(n):
                sp.dma_start(wsb[:, i * D:(i + 1) * D], w[i]).then_inc(c_in, 16)
                sp.dma_start(bsb[:, i * D:(i + 1) * D], row_everywhere(b[i])).then_inc(c_in, 16)
            sp.dma_start(gcol[:], g.rearrange("(p o) -> p o", o=1)).then_inc(c_in, 16)
            sp.dma_start(bcol[:], beta.rearrange("(p o) -> p o", o=1)).then_inc(c_in, 16)
            sp.dma_start(tabs[:], rope).then_inc(c_in, 16)

        @block.vector
        def _(dve):
            nc.vector.memset(eps_c[:], eps)
            for t in range(NT):
                last = nc.vector.bn_stats(stats[:, t, :], xs[:, t * D:(t + 1) * D])
            last.then_inc(st, 1)
            dve.wait_ge(st, 1)
            for t in range(NT):
                last = nc.vector.bn_aggr(mv[:, t, :], stats[:, t, :])
            last.then_inc(ag, 1)
            dve.wait_ge(sd, 1)
            nc.vector.reciprocal(rstd[:], std[:]).then_inc(rs, 1)
            dve.wait_ge(rs, 1)
            for t in range(NT):
                nc.vector.tensor_scalar(xh[:, t * D:(t + 1) * D], xs[:, t * D:(t + 1) * D], mv[:, t, 0:1],
                                        rstd[:, t:t + 1], ALU.subtract, ALU.mult).then_inc(xn, 1)
            dve.wait_ge(c_in, 16 * loads)
            for t in range(NT):
                dve.wait_ge(p_mm, t + 1)
                bank = banks[4 + t % 4]
                last = nc.vector.tensor_tensor(qs[:, t * D:(t + 1) * D], bank[:, 0:D], bsb[:, 0:D], ALU.add)
                if n > 1:
                    last = nc.vector.tensor_tensor(kv_all[:, t, :], bank[:, D:3 * D], bsb[:, D:3 * D], ALU.add)
                last.then_inc(p_ev, 1)
            dve.wait_ge(p_ev, NT)
            half = HD1 // 2
            src = qs[:].rearrange("p (b m e) -> p b m e", b=B, e=HD1)
            dst = rot[:].rearrange("p (b m e) -> p b m e", b=B, e=HD1)
            tab = tabs[:, 1, :].rearrange("p (m e) -> p m e", e=HD1).unsqueeze(1).broadcast_to([P, B, QT * H1, HD1])
            for lo, hi in ((0, half), (half, 0)):
                last = nc.vector.tensor_tensor(dst[:, :, :, lo:lo + half], src[:, :, :, hi:hi + half],
                                               tab[:, :, :, lo:lo + half], ALU.mult)
            last.then_inc(r1, 1)
            dve.wait_ge(r1, 1)
            qb = qs[:].rearrange("p (b m) -> p b m", b=B)
            nc.vector.tensor_tensor(qb, qb, tabs[:, 0, :].unsqueeze(1).broadcast_to([P, B, QT * D]), ALU.mult).then_inc(r2, 1)
            dve.wait_ge(r2, 1)
            nc.vector.tensor_tensor(qs[:], qs[:], rot[:], ALU.add).then_inc(r3, 1)
            dve.wait_ge(r3, 1)
            nc.vector.tensor_copy(q_hi[:], qs[:]).then_inc(r4, 1)
            dve.wait_ge(r4, 1)
            nc.vector.tensor_tensor(q_lo[:], qs[:], q_hi[:].bitcast(F32), ALU.subtract)

        @block.gpsimd
        def _(pool):
            if n == 1:
                return
            pool.wait_ge(p_ev, NT)
            half = HD1 // 2
            keys = kv_all[:, :, 0:D].rearrange("p (b t) (h e) -> p b t h e", b=B, e=HD1)
            dst = rotk[:].rearrange("p (b t h e) -> p b t h e", b=B, t=QT, e=HD1)
            for t in range(QT):
                for lo, hi in ((0, half), (half, 0)):
                    tab = tabs[:, 3, t * D:(t + 1) * D].rearrange("p (h e) -> p h e", e=HD1)
                    last = nc.gpsimd.tensor_tensor(dst[:, :, t, :, lo:lo + half], keys[:, :, t, :, hi:hi + half],
                                                   tab[:, :, lo:lo + half].unsqueeze(1).broadcast_to([P, B, H1, half]), ALU.mult)
            last.then_inc(k1, 1)
            pool.wait_ge(k1, 1)
            for t in range(QT):
                kk = kv_all[:, :, 0:D].rearrange("p (b t) d -> p b t d", b=B)[:, :, t, :]
                last = nc.gpsimd.tensor_tensor(kk, kk, tabs[:, 2, t * D:(t + 1) * D].unsqueeze(1).broadcast_to([P, B, D]), ALU.mult)
            last.then_inc(k2, 1)
            pool.wait_ge(k2, 1)
            nc.gpsimd.tensor_tensor(kv_all[:, :, 0:D], kv_all[:, :, 0:D], rotk[:].rearrange("p (t d) -> p t d", d=D), ALU.add)

        @block.scalar
        def _(act):
            act.wait_ge(ag, 1)
            nc.scalar.activation(std[:], mv[:, :, 1], ACT.Sqrt, bias=eps_c[:]).then_inc(sd, 1)
            act.wait_ge(c_in, 16 * loads)
            for q in range(NT // 4):
                act.wait_ge(t_mm, q + 1)
                nc.scalar.activation(hT[:, q * 512:(q + 1) * 512], banks[q][:], ACT.Identity, bias=bcol[:],
                                     scale=gcol[:]).then_inc(t_ev, 1)

        @block.tensor
        def _(pe):
            pe.wait_ge(c_in, 16 * loads)
            for t in range(NT):
                pe.wait_ge(xn, t + 1)
                last = nc.tensor.transpose(banks[t // 4][:, (t % 4) * D:(t % 4 + 1) * D], xh[:, t * D:(t + 1) * D], identf[:])
                if t % 4 == 3:
                    last.then_inc(t_mm, 1)
            for t in range(NT):
                pe.wait_ge(t_ev, t // 4 + 1)
                if t >= 4:
                    pe.wait_ge(p_ev, t - 3)
                nc.tensor.matmul(banks[4 + t % 4][:, 0:n * D], hT[:, t * D:(t + 1) * D], wsb[:], start=True, stop=True).then_inc(p_mm, 1)


def layer1_attention(nc, name, xs, q_hi, q_lo, kv_all, kv_dram, wo, bo, nkt, last_w, causal, consts, identf, identb, maskq, maskk):
    NK = nkt
    LKC = (NK - 1) * P + last_w
    S1 = B * G1
    chunks = 1 if causal else NCH
    RING = 2

    def kw(kt):
        return last_w if kt == NK - 1 else P

    with ExitStack() as ctx:
        def sb(nm, shape, dt=F32):
            return ctx.enter_context(nc.sbuf_tensor(f"{name}_{nm}", shape, dt))

        def sem(nm):
            return ctx.enter_context(nc.semaphore(f"{name}_{nm}"))

        wo_sb, bo_sb = sb("wo", [P, D]), sb("bo", [P, D])
        hmask = sb("hmask", [P, HG])
        kvb = None if causal else sb("kvb", [P, NK, 2 * D])
        ksrc = sb("ksrc", [P, NK, 4, R])
        qsrc = sb("qsrc", [P, QT, 4, R])
        kraw = sb("kraw", [P, NK, R]) if causal else None
        KX = sb("KX", [P, G1, NK * P], F32R)
        QX = sb("QX", [P, H1, LQ], F32R)
        V = sb("V", [P, G1, NK, HG, 32])
        pT = sb("pT", [P, RING, HG * LQ])
        mxc = sb("mxc", [P, QT, HG, NCH])
        negm = sb("negm", [P, QT, HG])
        OT = sb("OT", [P, LQ])
        rden = sb("rden", [P, QT, HG])
        A = sb("A", [P, QT, D])
        AT = sb("AT", [P, LQ])
        st = [ctx.enter_context(nc.psum_tensor(f"{name}_st{i}", [P, 1024], F32)) for i in range(2)]
        mb = [ctx.enter_context(nc.psum_tensor(f"{name}_mb{i}", [P, 512], F32)) for i in range(2)]
        pO = ctx.enter_context(nc.psum_tensor(f"{name}_pO", [P, 512], F32))
        pX = ctx.enter_context(nc.psum_tensor(f"{name}_pX", [P, 512], F32))

        c_in, kv_in, fixed = sem("c_in"), sem("kv_in"), sem("fixed")
        khi_done, src_done = sem("khi_done"), sem("src_done")
        v_done = sem("v_done")
        x_mm, x_ev = sem("x_mm"), sem("x_ev")
        c_mm, c_red = sem("c_mm"), sem("c_red")
        m_done, mt_mm, mt_ev = sem("m_done"), sem("mt_mm"), sem("mt_ev")
        s_mm, ex, pv = sem("s_mm"), sem("ex"), sem("pv")
        o_ev, rd, biased = sem("o_ev"), sem("rd"), sem("biased")
        block = ctx.enter_context(nc.Block())

        groups = [list(range(t, min(t + TG, NK))) for t in range(0, NK, TG)]
        NXG = len(groups)
        PREP = NXG + 1
        NC = HG * QT * chunks if not causal else HG

        def task(b, g, kind, i=0, prep=True):
            start = 3 * PREP + b * (G1 * (PREP + 1) + 2)
            if prep == "last":
                start += g * 1 + (PREP if g else 0)
                own = PREP if g == 0 else 0
            else:
                start += g * (PREP + 1)
                own = PREP
            return start + {"k": i + 1, "q": NXG + 1, "o": own + 1, "a": own + 2, "y": own + 3}[kind]

        per = -(-NC // max(1, NK - 1))
        after = {kt: list(range(kt * per, min(NC, (kt + 1) * per))) for kt in range(NK)}
        if NK == 2:
            ktask = {0: ["k0"], 1: ["q"]}
        else:
            ktask = {1: ["k0"], 3: ["k1"], 5: ["k2"], 7: ["k3"], 9: ["q"]}
        kcopy = {0: ["k0"]} if NK == 2 else {2: ["k0"], 4: ["k1"], 6: ["k2"], 8: ["k3"]}

        def steps(eng, step):
            with eng.Fori(0, B - 1) as b:
                for g in range(G1):
                    step(b, g, True, True, True)
            for g in range(G1):
                step(B - 1, g, g < G1 - 1, g < 1, "last")

        @block.sync
        def _(sp):
            sp.dma_start(wo_sb[:], wo).then_inc(c_in, 16)
            sp.dma_start(bo_sb[:], row_everywhere(bo)).then_inc(c_in, 16)
            sp.dma_start(hmask[:], consts["hmask"]).then_inc(c_in, 16)
            if not causal:
                with sp.Fori(0, B) as b:
                    sp.wait_ge(v_done, 1 + b * G1)
                    sp.wait_ge(src_done, 1 + b * G1)
                    sp.dma_start(kvb[:].rearrange("p t n -> p (t n)"),
                                 kv_dram[ds(b, 1)].rearrange("b p n -> p (b n)")).then_inc(kv_in, 16)

        @block.gpsimd
        def _(pool):
            pool.sem_inc(v_done, 1)
            pool.sem_inc(src_done, 1)
            for g in range(G1):
                nc.gpsimd.memset(V[:, g, :, :, HD1:32], 0.0)
            nc.gpsimd.memset(qsrc[:, :, 3, :], 0.0)
            nc.gpsimd.memset(ksrc[:, :, 3, :], 1.0).then_inc(fixed, 1)
            pool.wait_ge(fixed, 1)
            for g in range(G1):
                last = nc.gpsimd.memset(V[:, g, :, :, HD1:HD1 + 1], 1.0)
            last.then_inc(fixed, 1)

            def prepare(b, g, before):
                t = b * G1 + g
                cols = slice(g * R, (g + 1) * R)
                vcols = slice(D + g * R, D + (g + 1) * R)
                if causal:
                    k, v = kv_all[:, ds(b * QT, NK), cols], kv_all[:, ds(b * QT, NK), vcols]
                else:
                    pool.wait_ge(kv_in, 16 * (b + 1))
                    k, v = kvb[:, :, cols], kvb[:, :, vcols]
                pool.wait_ge(fixed, 2)
                pool.wait_ge(x_mm, before)
                if not (isinstance(t, int) and t < G1):
                    pool.wait_ge(pv, 1 + (t - G1 + 1) * NK)
                hi = ksrc[:].bitcast(F32R)

                def query(blk, part):
                    nc.gpsimd.tensor_copy(qsrc[:, :, blk, :], part[:, ds(b * QT * D, QT * D)].bitcast(F32)
                                          .rearrange("p (t d) -> p t d", d=D)[:, :, cols])

                query(0, q_hi)
                nc.gpsimd.tensor_copy(V[:, g, :, :, 0:HD1], v.rearrange("p t (j e) -> p t j e", e=HD1)).then_inc(v_done, 1)
                if causal:
                    nc.gpsimd.tensor_copy(kraw[:], k)
                nc.gpsimd.tensor_copy(hi[:, :, 0:2, :], k.unsqueeze(2).broadcast_to([P, NK, 2, R])).then_inc(khi_done, 1)
                query(2, q_hi)
                query(1, q_lo)
                pool.wait_ge(khi_done, t + 1)
                nc.gpsimd.tensor_tensor(ksrc[:, :, 2, :], kraw[:] if causal else k, ksrc[:, :, 0, :], ALU.subtract).then_inc(src_done, 1)

            for g in range(3):
                prepare(0, g, g * PREP)

            def step(b, g, has_max, has_prep, kind):
                if has_prep and g == 0:
                    prepare(b, G1 - 1, task(b, 0, "k", 0, kind) - 1)
                elif has_prep:
                    prepare(b + 1, g - 1, task(b, g - 1, "q", 0, kind))
            steps(pool, step)

        @block.tensor
        def _(pe):
            pe.sem_inc(pv, 1)
            pe.wait_ge(c_in, 48)

            def key_turn(kts, before):
                if not (isinstance(before, int) and before == 0):
                    pe.wait_ge(x_ev, before)
                for i, kt in enumerate(kts):
                    w = kw(kt)
                    last = nc.tensor.transpose(pX[:, i * P:i * P + w], ksrc[0:w, kt, :, :].rearrange("p a r -> p (a r)"),
                                               identf[0:w, 0:w])
                last.then_inc(x_mm, 1)

            def query_turn(before):
                pe.wait_ge(x_ev, before)
                for qt in range(QT):
                    last = nc.tensor.transpose(pX[:, qt * P:(qt + 1) * P], qsrc[:, qt, :, :].rearrange("p a r -> p (a r)"), identf[:])
                last.then_inc(x_mm, 1)

            def row_scores(t, g, n):
                before = t * NC + n - 1
                if n >= 2 or not (isinstance(t, int) and t == 0):
                    pe.wait_ge(c_red, before)
                bank = mb[n % 2]
                if causal:
                    for qt in range(QT):
                        nc.tensor.matmul(bank[:, qt * LQ:(qt + 1) * LQ], QX[:, HG * g + n, qt * P:(qt + 1) * P], KX[:, g, 0:LQ],
                                         start=True, stop=False)
                        last = nc.tensor.matmul(bank[:, qt * LQ:(qt + 1) * LQ], identb[:], maskq[:, qt * LQ:(qt + 1) * LQ],
                                                start=False, stop=True)
                else:
                    j, qt, c = n // (QT * NCH), n // NCH % QT, n % NCH
                    last = nc.tensor.matmul(bank[:, 0:CH], QX[:, HG * g + j, qt * P:(qt + 1) * P],
                                            KX[:, g, CSTART[c]:CSTART[c] + CH], start=True, stop=True)
                last.then_inc(c_mm, 1)

            def turn_maxima(t, g, kt0):
                if causal:
                    pe.wait_ge(c_red, (t + 1) * NC)
                else:
                    pe.wait_ge(m_done, t + 1)
                for qt in range(QT):
                    last = nc.tensor.transpose(st[kt0 % 2][0:HG, qt * P:(qt + 1) * P], negm[:, qt, :], identf[:])
                last.then_inc(mt_mm, 1)

            def key_scores(s, g, kt):
                i = g * NK + kt
                w = kw(kt)
                k = KX[:, g, kt * P:kt * P + w]
                out = st[i % 2]
                if causal and kt == 1:
                    nc.tensor.matmul(out[0:w, 0:HG * P].rearrange("p (j q) -> p j q", j=HG), k,
                                     QX[:, HG * g:HG * (g + 1), P:LQ], start=True, stop=False)
                    for j in range(HG):
                        last = nc.tensor.matmul(out[:, j * P:(j + 1) * P], identb[:], maskk[:], start=False, stop=j == HG - 1)
                else:
                    for h2 in range(2):
                        last = nc.tensor.matmul(out[0:w, h2 * 512:(h2 + 1) * 512], k,
                                                QX[:, HG * g + 2 * h2:HG * g + 2 * h2 + 2, :].rearrange("p h q -> p (h q)"),
                                                start=True, stop=not causal)
                        if causal:
                            for j in range(2):
                                at = h2 * 512 + j * LQ
                                last = nc.tensor.matmul(out[:, at:at + P], identb[:], maskk[:], start=False, stop=j == 1)
                last.then_inc(s_mm, 1)

            def values(s, g, kt):
                i = g * NK + kt
                w = kw(kt)
                lo, n = (P, P) if causal and kt == 1 else (0, LQ)
                for j in range(HG):
                    last = nc.tensor.matmul(pO[32 * j:32 * j + 32, lo:LQ], V[0:w, g, kt, j, :],
                                            pT[0:w, i % RING, j * n:(j + 1) * n], start=kt == 0, stop=kt == NK - 1)
                last.then_inc(pv, 1)

            pe.wait_ge(fixed, 2)
            for t in range(3):
                pe.wait_ge(src_done, 1 + t + 1)
                for i, kts in enumerate(groups):
                    key_turn(kts, t * PREP + i)
                query_turn(t * PREP + NXG)
            pe.wait_ge(x_ev, PREP)
            for n in range(NC):
                row_scores(0, 0, n)
            turn_maxima(0, 0, 0)

            def step(b, g, has_max, has_prep, kind):
                s = b * G1 + g
                ng = (g + 1) % G1
                pe.wait_ge(mt_ev, s + 1)
                pe.wait_ge(v_done, 1 + s + 1)
                key_scores(s, g, 0)
                key_scores(s, g, 1)
                for kt in range(NK):
                    pe.wait_ge(ex, s * NK + kt + 1)
                    if kt == 0:
                        pe.wait_ge(o_ev, 1 + s)
                    values(s, g, kt)
                    if kt + 2 < NK:
                        key_scores(s, g, kt + 2)
                    if has_max:
                        for n in after[kt]:
                            row_scores(s + 1, ng, n)
                    if has_prep:
                        for what in ktask.get(kt, ()):
                            if what == "q":
                                query_turn(task(b, g, "q", 0, kind) - 1)
                            else:
                                if what == "k0":
                                    pe.wait_ge(src_done, 1 + s + 4)
                                i = int(what[1:])
                                key_turn(groups[i], task(b, g, "k", i, kind) - 1)
                if has_max:
                    turn_maxima(s + 1, ng, (g + 1) * NK)
                at = task(b, g, "o", 0, kind)
                pe.wait_ge(x_ev, at - 1)
                pe.wait_ge(o_ev, 1 + s + 1)
                for qt in range(QT):
                    last = nc.tensor.transpose(pX[:, qt * P:(qt + 1) * P], OT[:, qt * P:(qt + 1) * P], identf[:])
                last.then_inc(x_mm, 1)
                if g == G1 - 1:
                    pe.wait_ge(x_ev, at)
                    for qt in range(QT):
                        last = nc.tensor.transpose(pX[:, qt * P:(qt + 1) * P], A[:, qt, :], identf[:])
                    last.then_inc(x_mm, 1)
                    pe.wait_ge(x_ev, at + 1)
                    for qt in range(QT):
                        last = nc.tensor.matmul(pX[:, qt * D:(qt + 1) * D], AT[:, qt * P:(qt + 1) * P], wo_sb[:], start=True, stop=True)
                    last.then_inc(x_mm, 1)

            steps(pe, step)

        @block.scalar
        def _(act):
            act.sem_inc(o_ev, 1)
            act.preload_act_table(ACT.Exp)

            def key_copy(n, g, i):
                act.wait_ge(x_mm, n)
                kts = groups[i]
                m = (len(kts) - 1) * P + kw(kts[-1])
                nc.scalar.copy(KX[:, g, kts[0] * P:kts[0] * P + m], pX[:, 0:m]).then_inc(x_ev, 1)

            for t in range(3):
                for i in range(NXG):
                    key_copy(t * PREP + i + 1, t, i)

            def step(b, g, has_max, has_prep, kind):
                s = b * G1 + g
                for kt in range(NK):
                    i = g * NK + kt
                    w = kw(kt)
                    act.wait_ge(s_mm, s * NK + kt + 1)
                    n = HG * P if causal and kt == 1 else HG * LQ
                    nc.scalar.activation(pT[0:w, i % RING, 0:n], st[i % 2][0:w, 0:n], ACT.Exp).then_inc(ex, 1)
                    if has_prep:
                        for what in kcopy.get(kt, ()):
                            j = int(what[1:])
                            key_copy(task(b, g, "k", j, kind), (g + 3) % G1, j)
                act.wait_ge(pv, 1 + (s + 1) * NK)
                nc.scalar.copy(OT[:], pO[:, 0:LQ]).then_inc(o_ev, 1)
                if g == G1 - 1:
                    at = task(b, g, "a", 0, kind)
                    act.wait_ge(x_mm, at)
                    nc.scalar.copy(AT[:], pX[:, 0:LQ]).then_inc(x_ev, 1)
            steps(act, step)

        @block.vector
        def _(dve):
            dve.wait_ge(c_in, 48)
            xt = xs[:].rearrange("p (t d) -> p t d", d=D)
            nc.vector.tensor_tensor(xt, xt, bo_sb[:].unsqueeze(1).broadcast_to([P, B * QT, D]), ALU.add).then_inc(biased, 1)

            def query_copy(n, g):
                dve.wait_ge(x_mm, n)
                nc.vector.tensor_tensor(QX[:, HG * g:HG * (g + 1), :], pX[:, 0:LQ].unsqueeze(1).broadcast_to([P, HG, LQ]),
                                        hmask[:].unsqueeze(2).broadcast_to([P, HG, LQ]), ALU.mult).then_inc(x_ev, 1)

            def chunk_max(t, n):
                dve.wait_ge(c_mm, t * NC + n + 1)
                if causal:
                    nc.vector.tensor_reduce(negm[:, :, n], mb[n % 2][:].rearrange("p (a k) -> p a k", a=QT), AX.X, ALU.max,
                                            negate=True).then_inc(c_red, 1)
                else:
                    j, qt, c = n // (QT * NCH), n // NCH % QT, n % NCH
                    nc.vector.reduce_max(mxc[:, qt, j, c:c + 1], mb[n % 2][:, 0:CH], AX.X).then_inc(c_red, 1)

            def maxima(t):
                dve.wait_ge(c_red, (t + 1) * NC)
                if causal:
                    return
                if True:
                    nc.vector.tensor_reduce(negm[:], mxc[:], AX.X, ALU.max, negate=True).then_inc(m_done, 1)

            def maxima_rows(t, g, kt0):
                dve.wait_ge(mt_mm, t + 1)
                rows = slice(3 * R, 3 * R + HG)
                nc.vector.tensor_tensor(QX[rows, HG * g:HG * (g + 1), :],
                                        st[kt0 % 2][0:HG, 0:LQ].unsqueeze(1).broadcast_to([HG, HG, LQ]),
                                        identf[0:HG, 0:HG].unsqueeze(2).broadcast_to([HG, HG, LQ]), ALU.mult).then_inc(mt_ev, 1)

            for t in range(3):
                query_copy((t + 1) * PREP, t)
            for n in range(NC):
                chunk_max(0, n)
            maxima(0)
            maxima_rows(0, 0, 0)

            def step(b, g, has_max, has_prep, kind):
                s = b * G1 + g
                ng = (g + 1) % G1
                for kt in range(NK):
                    if has_max:
                        for n in after[kt]:
                            chunk_max(s + 1, n)
                    if has_prep and "q" in ktask.get(kt, ()):
                        query_copy(task(b, g, "q", 0, kind), (g + 3) % G1)
                if has_max:
                    maxima(s + 1)
                    maxima_rows(s + 1, ng, (g + 1) * NK)
                at = task(b, g, "o", 0, kind)
                dve.wait_ge(x_mm, at)
                o = pX[:, 0:LQ].rearrange("p (t j e) -> p t j e", t=QT, e=32)
                nc.vector.reciprocal(rden[:], o[:, :, :, HD1]).then_inc(rd, 1)
                dve.wait_ge(rd, s + 1)
                for qt in range(QT):
                    last = nc.vector.tensor_tensor(A[:, qt, g * R:(g + 1) * R].rearrange("p (j e) -> p j e", e=HD1),
                                                   o[:, qt, :, 0:HD1],
                                                   rden[:, qt, :].unsqueeze(2).broadcast_to([P, HG, HD1]), ALU.mult)
                last.then_inc(x_ev, 1)
                if g == G1 - 1:
                    dve.wait_ge(x_mm, at + 2)
                    dve.wait_ge(biased, 1)
                    xb = xs[:, ds(b * QT * D, QT * D)]
                    nc.vector.tensor_tensor(xb, xb, pX[:, 0:QT * D], ALU.add).then_inc(x_ev, 1)
            steps(dve, step)


def mlp(nc, xs, g, beta, w1, b1, w2, b2, identf, out, eps=1e-5):
    NT = B * QT
    FF = w1.shape[1]
    NF = FF // P
    NB = NT // 4
    C0, C1 = 0.7978845608028654, 0.044715
    with ExitStack() as ctx:
        def sb(nm, shape, dt=F32):
            return ctx.enter_context(nc.sbuf_tensor(f"mlp_{nm}", shape, dt))

        def sem(nm):
            return ctx.enter_context(nc.semaphore(f"mlp_{nm}"))

        w1s, w2s = sb("w1", [P, FF]), sb("w2", [P, NF, D])
        b1c, b2s = sb("b1", [P, NF]), sb("b2", [P, D])
        gcol, bcol, eps_c = sb("g", [P, 1]), sb("beta", [P, 1]), sb("eps", [P, 1])
        stats, mv = sb("stats", [P, NT, 6]), sb("mv", [P, NT, 2])
        std, rstd = sb("std", [P, NT]), sb("rstd", [P, NT])
        xh, hT = sb("xh", [P, NT * D]), sb("hT", [P, NT * D])
        act_out = sb("gelu", [P, 2, NF, 512])
        banks = [ctx.enter_context(nc.psum_tensor(f"mlp_bank{i}", [P, 512], F32)) for i in range(8)]
        c_in, st, ag, sd, rs, xn = sem("c_in"), sem("st"), sem("ag"), sem("sd"), sem("rs"), sem("xn")
        t_mm, t_ev, f_mm, gl, y_mm, y_ev, stored = (sem("t_mm"), sem("t_ev"), sem("f_mm"), sem("gl"), sem("y_mm"),
                                                    sem("y_ev"), sem("stored"))
        biased = sem("biased")
        block = ctx.enter_context(nc.Block())

        @block.sync
        def _(sp):
            sp.dma_start(w1s[:], w1).then_inc(c_in, 16)
            sp.dma_start(w2s[:], w2.rearrange("(n p) d -> p n d", p=P)).then_inc(c_in, 16)
            for f in range(NF):
                sp.dma_start(b1c[:, f:f + 1], b1[f * P:(f + 1) * P].rearrange("(p o) -> p o", o=1)).then_inc(c_in, 16)
            sp.dma_start(b2s[:], row_everywhere(b2)).then_inc(c_in, 16)
            sp.dma_start(gcol[:], g.rearrange("(p o) -> p o", o=1)).then_inc(c_in, 16)
            sp.dma_start(bcol[:], beta.rearrange("(p o) -> p o", o=1)).then_inc(c_in, 16)
            o = out.rearrange("b (t p) d -> p (b t) d", p=P)
            for k in range(NB):
                sp.wait_ge(y_ev, k + 1)
                sp.dma_start(o[:, 4 * k:4 * k + 4, :], xs[:, k * 512:(k + 1) * 512].rearrange("p (t d) -> p t d", d=D)).then_inc(stored, 16)
            sp.wait_ge(stored, 16 * NB)

        @block.vector
        def _(dve):
            nc.vector.memset(eps_c[:], eps)
            for t in range(NT):
                last = nc.vector.bn_stats(stats[:, t, :], xs[:, t * D:(t + 1) * D])
            last.then_inc(st, 1)
            dve.wait_ge(st, 1)
            for t in range(NT):
                last = nc.vector.bn_aggr(mv[:, t, :], stats[:, t, :])
            last.then_inc(ag, 1)
            dve.wait_ge(sd, 1)
            nc.vector.reciprocal(rstd[:], std[:]).then_inc(rs, 1)
            dve.wait_ge(rs, 1)
            for t in range(NT):
                nc.vector.tensor_scalar(xh[:, t * D:(t + 1) * D], xs[:, t * D:(t + 1) * D], mv[:, t, 0:1],
                                        rstd[:, t:t + 1], ALU.subtract, ALU.mult).then_inc(xn, 1)
            dve.wait_ge(c_in, 16 * (5 + NF))
            xt = xs[:].rearrange("p (t d) -> p t d", d=D)
            dve.wait_ge(xn, NT)
            nc.vector.tensor_tensor(xt, xt, b2s[:].unsqueeze(1).broadcast_to([P, NT, D]), ALU.add).then_inc(biased, 1)
            dve.wait_ge(biased, 1)
            for k in range(NB):
                dve.wait_ge(y_mm, k + 1)
                xb = xs[:, k * 512:(k + 1) * 512]
                nc.vector.tensor_tensor(xb, xb, banks[6 + k % 2][:], ALU.add).then_inc(y_ev, 1)

        @block.scalar
        def _(act):
            act.wait_ge(ag, 1)
            nc.scalar.activation(std[:], mv[:, :, 1], ACT.Sqrt, bias=eps_c[:]).then_inc(sd, 1)
            act.wait_ge(c_in, 16 * (5 + NF))
            for q in range(NB):
                act.wait_ge(t_mm, q + 1)
                nc.scalar.activation(hT[:, q * 512:(q + 1) * 512], banks[q][:], ACT.Identity, bias=bcol[:], scale=gcol[:]).then_inc(t_ev, 1)
            for k in range(NB):
                for f in range(NF):
                    act.wait_ge(f_mm, k * NF + f + 1)
                    if k >= 2:
                        act.wait_ge(y_mm, k - 1)
                    nc.scalar.activation(act_out[:, k % 2, f, :], banks[(k * NF + f) % 4][:], ACT.Gelu_apprx_tanh,
                                         bias=b1c[:, f:f + 1]).then_inc(gl, 1)

        @block.tensor
        def _(pe):
            pe.wait_ge(c_in, 16 * (5 + NF))
            for t in range(NT):
                pe.wait_ge(xn, t + 1)
                last = nc.tensor.transpose(banks[t // 4][:, (t % 4) * D:(t % 4 + 1) * D], xh[:, t * D:(t + 1) * D], identf[:])
                if t % 4 == 3:
                    last.then_inc(t_mm, 1)
            pe.wait_ge(t_ev, NB)

            def up(k):
                for f in range(NF):
                    if k:
                        pe.wait_ge(gl, (k - 1) * NF + f + 1)
                    nc.tensor.matmul(banks[f][:], w1s[:, f * P:(f + 1) * P], hT[:, k * 512:(k + 1) * 512], start=True, stop=True).then_inc(f_mm, 1)

            up(0)
            for k in range(NB):
                if k + 1 < NB:
                    up(k + 1)
                pe.wait_ge(gl, (k + 1) * NF)
                if k >= 2:
                    pe.wait_ge(y_ev, k - 1)
                for i in range(4):
                    for f in range(NF):
                        last = nc.tensor.matmul(banks[6 + k % 2][:, i * D:(i + 1) * D], act_out[:, k % 2, f, i * P:(i + 1) * P],
                                                w2s[:, f, :], start=f == 0, stop=f == NF - 1)
                last.then_inc(y_mm, 1)


def build(nc, x, ctx_in, w, consts, out):
    kv_dram = nc.dram_tensor("kv_scratch", (B, P, KT * 2 * D), F32).ap()

    def w1(name):
        return w["L1_xattn_" + name]

    with ExitStack() as ctx:
        def sb(name, shape, dt=F32):
            return ctx.enter_context(nc.sbuf_tensor(name, shape, dt))

        xs = sb("xs", [P, B * QT * D])
        identf = sb("identf", [P, P])
        with ExitStack() as layer0:
            xnT = layer0.enter_context(nc.sbuf_tensor("xnT", [P, B * LQ], F32))
            M = layer0.enter_context(nc.sbuf_tensor("M", [P, H0 * D], F32))
            epsc = layer0.enter_context(nc.sbuf_tensor("epsc", [P, 1], F32))
            layer0_setup(nc, x, w["L0_xattn_norm_w"], w["L0_xattn_wq"], w["L0_xattn_wk"], consts["ident"], xs, xnT, M,
                         identf, epsc)
            layer0_attention(nc, ctx_in, w["L0_xattn_wv"], w["L0_xattn_wo"], w1("ca_wk"), w1("ca_wv"), w1("ca_bk"),
                             w1("ca_bv"), consts["cos_k"], consts["sin_k"], kv_dram, xs, xnT, M, identf)
        identb, maskq, maskk = sb("identb", [P, P], BF16), sb("maskq", [P, QT * LQ], BF16), sb("maskk", [P, P], BF16)
        q_hi, q_lo = sb("q_hi", [P, B * QT * D], F32R), sb("q_lo", [P, B * QT * D], F32R)
        with ExitStack() as self_attention:
            kv_all = self_attention.enter_context(nc.sbuf_tensor("kv_all", [P, B * QT, 2 * D], F32))
            load_masks(nc, consts, identf, identb, maskq, maskk)
            normed_projection(nc, "self", xs, w1("ln1_g"), w1("ln1_b"), [w1("sa_wq"), w1("sa_wk"), w1("sa_wv")],
                              [w1("sa_bq"), w1("sa_bk"), w1("sa_bv")], consts["rope"], identf, q_hi, q_lo, kv_all)
            layer1_attention(nc, "sa", xs, q_hi, q_lo, kv_all, None, w1("sa_wo"), w1("sa_bo"), QT, P, True, consts,
                             identf, identb, maskq, maskk)
        normed_projection(nc, "cross", xs, w1("ln2_g"), w1("ln2_b"), [w1("ca_wq")], [w1("ca_bq")], consts["rope"], identf,
                          q_hi, q_lo, None)
        layer1_attention(nc, "ca", xs, q_hi, q_lo, None, kv_dram, w1("ca_wo"), w1("ca_bo"), KT, LAST, False, consts,
                         identf, identb, maskq, maskk)
        mlp(nc, xs, w1("ln3_g"), w1("ln3_b"), w1("fc1_w"), w1("fc1_b"), w1("fc2_w"), w1("fc2_b"), identf, out)


def load_masks(nc, consts, identf, identb, maskq, maskk):
    with ExitStack() as ctx:
        mq = ctx.enter_context(nc.sbuf_tensor("mq32", [P, QT * LQ], F32))
        mk = ctx.enter_context(nc.sbuf_tensor("mk32", [P, P], F32))
        m_in = ctx.enter_context(nc.semaphore("masks_in"))
        block = ctx.enter_context(nc.Block())

        @block.sync
        def _(sp):
            sp.dma_start(mq[:], consts["mask_q"]).then_inc(m_in, 16)
            sp.dma_start(mk[:], consts["mask_k"]).then_inc(m_in, 16)

        @block.vector
        def _(dve):
            nc.vector.tensor_copy(identb[:], identf[:])
            dve.wait_ge(m_in, 32)
            nc.vector.tensor_copy(maskq[:], mq[:])
            nc.vector.tensor_copy(maskk[:], mk[:])


def constants():
    f = np.float32
    inv = (f(1.0) / np.power(f(10000.0), np.arange(0, HD1, 2, dtype=f) / f(HD1))).astype(f)
    pos = np.arange(KT * P, dtype=f)
    ang = np.outer(pos, inv).astype(f)
    cos, sin = np.cos(ang).astype(f), np.sin(ang).astype(f)
    live = (pos < LK)[:, None]
    cos8 = np.where(live, np.concatenate([cos, cos], 1), f(0))
    sin8 = np.where(live, np.concatenate([-sin, sin], 1), f(0))
    tiles = lambda a: np.ascontiguousarray(a.reshape(-1, P, HD1).transpose(1, 0, 2)).astype(f)
    heads = lambda a: np.repeat(tiles(a[:LQ])[:, :, None, :], H1, 2).reshape(P, QT * D)
    scale = f(HD1 ** -0.5)
    rope = np.stack([heads(cos8) * scale, heads(sin8) * scale, heads(cos8), heads(sin8)], 1).astype(f)
    r = np.arange(P)[:, None]
    j = np.arange(HG)[None, :]
    hmask = np.where(r < 3 * R, (r % R) // HD1 == j, r - 3 * R == j).astype(f)
    q, k = np.arange(LQ)[:, None], np.arange(LQ)[None, :]
    mask = np.where(k <= q, f(0), f(NEG)).astype(f)
    return {"ident": np.eye(P, dtype=f), "cos_k": tiles(cos8), "sin_k": tiles(sin8), "rope": rope, "hmask": hmask,
            "mask_q": np.ascontiguousarray(mask.reshape(QT, P, LQ).transpose(1, 0, 2).reshape(P, QT * LQ)),
            "mask_k": np.ascontiguousarray(mask[:P, :P].T)}


def kernel(**inputs):
    import concourse.bacc as bacc
    from concourse.bass_utils import run_bass_kernel_spmd

    nc = bacc.Bacc("TRN2", target_bir_lowering=False, num_devices=1)
    arrays, aps = {}, {}
    for name, a in [*inputs.items(), *constants().items()]:
        a = np.ascontiguousarray(a)
        arrays[f"in_{name}"] = a
        aps[name] = nc.dram_tensor(f"in_{name}", a.shape, mybir.dt.from_np(a.dtype), kind="ExternalInput").ap()
    out = nc.dram_tensor("out", (B, LQ, D), F32, kind="ExternalOutput").ap()
    build(nc, aps["x"], aps["ctx_1024"], aps, aps, out)
    return run_bass_kernel_spmd(nc, [arrays], core_ids=[0]).results[0]["out"]
```

```python
from contextlib import ExitStack

import numpy as np

import concourse.bass as bass
from concourse import mybir

F32 = mybir.dt.float32
F32R = mybir.dt.float32r
BF16 = mybir.dt.bfloat16
ALU = mybir.AluOpType
ACT = mybir.ActivationFunctionType
AX = mybir.AxisListType
ds = bass.ds

P = 128
B, LQ, D = 8, 256, 128
LK = 1601
QT = LQ // P
KT = (LK + P - 1) // P
LAST = LK - (KT - 1) * P
NCH = 4
CH = (LK + NCH - 1) // NCH
CH += CH % 2
CSTART = [min(c * CH, LK - CH) for c in range(NCH)]
CSKIP = [c * CH - CSTART[c] for c in range(NCH)]
H0, HD0 = 16, 64
NP0 = H0 // 2
TG = 4
GROUPS = [list(range(g, min(g + TG, KT))) for g in range(0, KT, TG)]
NG = len(GROUPS)
UNITS = 2 * QT
H1, HD1 = 16, 8
KVG = [list(range(t, min(t + 2, KT))) for t in range(0, KT, 2)]
HG = 4
G1 = H1 // HG
R = HG * HD1
NEG = -1e30


def width(kt):
    return LAST if kt == KT - 1 else P


def row_everywhere(row):
    return row.rearrange("(o n) -> o n", o=1).broadcast_to([P, row.shape[0]])


def layer0_setup(nc, x, norm_w, wq, wk, ident, xs, xnT, M, identf, epsc):
    NT = B * QT
    with ExitStack() as ctx:
        def sb(name, shape, dt=F32):
            return ctx.enter_context(nc.sbuf_tensor(name, shape, dt))

        def sem(name):
            return ctx.enter_context(nc.semaphore(name))

        wq_sb = sb("wq_sb", [P, H0 * HD0])
        wk_sb = sb("wk_sb", [P, H0 * HD0])
        wqT = sb("wqT", [P, NP0, D])
        wkT = sb("wkT", [P, NP0, D])
        sq = sb("sq", [P, NT * D])
        ms = sb("ms", [P, 4, NT])
        nw = sb("nw", [P, 1])
        banks = [ctx.enter_context(nc.psum_tensor(f"a_bank{i}", [P, 512], F32)) for i in range(8)]

        x_in, w_in, c_in = sem("x_in"), sem("w_in"), sem("c_in")
        squared, meansq, rms, inv, normed = sem("squared"), sem("meansq"), sem("rms"), sem("inv"), sem("normed")
        wT_mm, wT_act, wT_dve = sem("wT_mm"), sem("wT_act"), sem("wT_dve")
        m_mm, m_ev = sem("m_mm"), sem("m_ev")
        xt_mm, xt_ev = sem("xt_mm"), sem("xt_ev")
        block = ctx.enter_context(nc.Block())

        @block.sync
        def _(sp):
            sp.dma_start(identf[:], ident).then_inc(c_in, 16)
            sp.dma_start(wq_sb[:], wq).then_inc(w_in, 16)
            sp.dma_start(wk_sb[:], wk).then_inc(w_in, 16)
            sp.dma_start(xs[:].rearrange("p (t d) -> p t d", d=D),
                         x.rearrange("b (t p) d -> p (b t) d", p=P)).then_inc(x_in, 16)
            sp.dma_start(nw[:], norm_w.rearrange("(p o) -> p o", o=1)).then_inc(c_in, 16)

        @block.vector
        def _(dve):
            dve.wait_ge(wT_mm, 2)
            nc.vector.tensor_copy(wqT[:, 4:8, :], banks[1][:].rearrange("p (n d) -> p n d", d=D)).then_inc(wT_dve, 1)
            dve.wait_ge(wT_mm, 4)
            nc.vector.tensor_copy(wkT[:, 4:8, :], banks[3][:].rearrange("p (n d) -> p n d", d=D)).then_inc(wT_dve, 1)
            dve.wait_ge(x_in, 16)
            nc.vector.memset(epsc[:], 1e-6)
            nc.vector.tensor_tensor(sq[:], xs[:], xs[:], ALU.mult).then_inc(squared, 1)
            dve.wait_ge(squared, 1)
            nc.vector.tensor_reduce(ms[:, 0, :], sq[:].rearrange("p (t d) -> p t d", d=D), AX.X, ALU.add).then_inc(meansq, 1)
            dve.wait_ge(rms, 1)
            nc.vector.reciprocal(ms[:, 2, :], ms[:, 1, :]).then_inc(inv, 1)
            dve.wait_ge(inv, 1)
            nc.vector.tensor_tensor(sq[:].rearrange("p (t d) -> p t d", d=D), xs[:].rearrange("p (t d) -> p t d", d=D),
                                    ms[:, 2, :].unsqueeze(2).broadcast_to([P, NT, D]), ALU.mult).then_inc(normed, 1)
            for g in range(4):
                dve.wait_ge(m_mm, g + 1)
                nc.vector.tensor_copy(M[:].rearrange("p (n r d) -> p n r d", r=2, d=D)[:, 4 * (g // 2):4 * (g // 2) + 4, g % 2, :],
                                      banks[4 + g % 2][:].rearrange("p (n d) -> p n d", d=D)).then_inc(m_ev, 1)

        @block.scalar
        def _(act):
            act.wait_ge(wT_mm, 1)
            nc.scalar.copy(wqT[:, 0:4, :], banks[0][:].rearrange("p (n d) -> p n d", d=D)).then_inc(wT_act, 1)
            act.wait_ge(wT_mm, 3)
            nc.scalar.copy(wkT[:, 0:4, :], banks[2][:].rearrange("p (n d) -> p n d", d=D)).then_inc(wT_act, 1)
            act.wait_ge(meansq, 1)
            nc.scalar.activation(ms[:, 1, :], ms[:, 0, :], ACT.Sqrt, bias=epsc[:], scale=1.0 / D).then_inc(rms, 1)
            act.wait_ge(c_in, 32)
            for g in range(4):
                act.wait_ge(xt_mm, g + 1)
                nc.scalar.activation(xnT[:, g * 512:(g + 1) * 512], banks[6 + g % 2][:], ACT.Copy,
                                     scale=nw[:]).then_inc(xt_ev, 1)

        @block.tensor
        def _(pe):
            pe.wait_ge(c_in, 32)
            pe.wait_ge(w_in, 32)
            for w, src in enumerate((wq_sb, wk_sb)):
                for n in range(NP0):
                    last = nc.tensor.transpose(banks[2 * w + n // 4][:, (n % 4) * D:(n % 4 + 1) * D],
                                               src[:, n * P:(n + 1) * P], identf[:])
                    if n % 4 == 3:
                        last.then_inc(wT_mm, 1)
            pe.wait_ge(wT_act, 2)
            pe.wait_ge(wT_dve, 2)
            for g in range(4):
                if g >= 2:
                    pe.wait_ge(m_ev, g - 1)
                rows = slice((g % 2) * HD0, (g % 2 + 1) * HD0)
                for i in range(4):
                    n = 4 * (g // 2) + i
                    last = nc.tensor.matmul(banks[4 + g % 2][:, i * D:(i + 1) * D], wqT[rows, n, :],
                                            wkT[rows, n, :], start=True, stop=True)
                last.then_inc(m_mm, 1)
            pe.wait_ge(normed, 1)
            for g in range(4):
                if g >= 2:
                    pe.wait_ge(xt_ev, g - 1)
                for i in range(4):
                    t = 4 * g + i
                    last = nc.tensor.transpose(banks[6 + g % 2][:, i * D:(i + 1) * D], sq[:, t * D:(t + 1) * D], identf[:])
                last.then_inc(xt_mm, 1)


def layer0_attention(nc, ctx_in, wv, wo, cross_wk, cross_wv, cross_bk, cross_bv, cos_k, sin_k, kv_dram, xs, xnT, M, identf):
    with ExitStack() as ctx:
        def sb(name, shape, dt=F32):
            return ctx.enter_context(nc.sbuf_tensor(name, shape, dt))

        def sem(name):
            return ctx.enter_context(nc.semaphore(name))

        tok = sb("ctx_tok", [P, KT, D])
        cT = sb("cT", [P, LK + 1])
        cTh = sb("cTh", [P, LK + 1], F32R)
        cTl = sb("cTl", [P, LK + 1], F32R)
        wv_sb = sb("wv_sb", [P, H0 * HD0])
        wo_sb = sb("wo_sb", [P, NP0, D])
        Mr = sb("Mr", [P, 2, 2 * D])
        qh = sb("qh", [P, 2, 2, LQ], F32R)
        ql = sb("ql", [P, 2, 2, LQ], F32R)
        prob = sb("prob", [P, 2, KT * P])
        pT = [[sb(f"pT{s}{h}", [P, KT, LQ]) for h in range(2)] for s in range(2)]
        V = sb("V0", [P, 2, KT, P])
        OA = sb("OA", [P, 2, LQ])
        wkv = sb("wkv", [P, 2 * D])
        bkv = sb("bkv", [P, 2 * D])
        cosk = sb("cosk", [P, KT, HD1])
        sink = sb("sink", [P, KT, HD1])
        kv = sb("kv", [P, KT, 2 * D])
        rot = sb("rot", [P, KT, D])
        mx4 = sb("mx4", [P, 2, NCH])
        negm = sb("negm", [P, 2])
        dens = sb("dens", [P, 2, UNITS, NCH])
        den = sb("den", [P, 2, UNITS])
        rden = sb("rden", [P, 2, UNITS])
        S = ctx.enter_context(nc.psum_tensor("S0", [P, NCH, 512], F32))
        tb = [ctx.enter_context(nc.psum_tensor(f"tb{i}", [P, 512], F32)) for i in range(2)]
        pO = ctx.enter_context(nc.psum_tensor("pO", [P, 512], F32))
        pX = ctx.enter_context(nc.psum_tensor("pX", [P, 512], F32))

        w_in, tok_in = sem("w_in0"), sem("tok_in")
        m_in = [sem(f"m_in{i}") for i in range(2)]
        zeroed = sem("zeroed")
        ct_mm, ct_ev, ct_hi, ct_lo = sem("ct_mm"), sem("ct_ev"), sem("ct_hi"), sem("ct_lo")
        q_mm, q_hi, q_lo = sem("q_mm"), sem("q_hi"), sem("q_lo")
        s_mm = sem("s_mm")
        mx_c, mx = sem("mx_c"), sem("mx")
        ex = sem("ex")
        t_mm = sem("t_mm")
        t_act, t_dve = sem("t_act"), sem("t_dve")
        v_mm, v_act, v_dve = sem("v_mm"), sem("v_act"), sem("v_dve")
        o_mm, o_ev = sem("o_mm"), sem("o_ev")
        y_mm, y_add = sem("y_mm"), sem("y_add")
        kv_mm, kv_ev, kv_bias, kv_rot, kv_cos, kv_done, kv_out = (
            sem("kv_mm"), sem("kv_ev"), sem("kv_bias"), sem("kv_rot"), sem("kv_cos"), sem("kv_done"), sem("kv_out"))
        padded = sem("padded")
        den_s, den_r, added = sem("den_s"), sem("den_r"), sem("added")
        kv_banks = [tb[0], tb[1], pO]
        block = ctx.enter_context(nc.Block())

        NU = NP0 * UNITS

        def walk(eng, pair, first=None, last=None):
            pair(0, 0, False, True)
            with eng.Fori(0, (NP0 - 2) // 2) as j:
                pair(2 * j + 1, 1, True, True)
                pair(2 * j + 2, 0, True, True)
            pair(NP0 - 1, 1, True, False)

        @block.sync
        def _(sp):
            sp.sem_inc(kv_out, 1)
            sp.dma_start(wv_sb[:], wv).then_inc(w_in, 16)
            sp.dma_start(wo_sb[:], wo.rearrange("(n p) d -> p n d", p=P)).then_inc(w_in, 16)
            for i, (w, bias) in enumerate(((cross_wk, cross_bk), (cross_wv, cross_bv))):
                sp.dma_start(wkv[:, i * D:(i + 1) * D], w).then_inc(w_in, 16)
                sp.dma_start(bkv[:, i * D:(i + 1) * D], row_everywhere(bias)).then_inc(w_in, 16)
            sp.dma_start(cosk[:], cos_k).then_inc(w_in, 16)
            sp.dma_start(sink[:], sin_k).then_inc(w_in, 16)
            with sp.Fori(0, B) as b:
                sp.wait_ge(ct_mm, 1 + b * NG)
                sp.dma_start(tok[:, 0:KT - 1, :],
                             ctx_in[ds(b, 1), 0:(KT - 1) * P, :].rearrange("b (t p) d -> p (b t) d", p=P)).then_inc(tok_in, 16)
                sp.dma_start(tok[0:LAST, KT - 1, :],
                             ctx_in[ds(b, 1), (KT - 1) * P:LK, :].rearrange("b p d -> p (b d)")).then_inc(tok_in, 16)
                for p in range(2):
                    sp.wait_ge(q_mm, 1 + b * NP0)
                    sp.dma_start(Mr[:, p, :], M[:, p * 2 * D:(p + 1) * 2 * D]).then_inc(m_in[p], 16)

                def refill(p, slot, has_prev, has_next):
                    sp.wait_ge(q_mm, 1 + b * NP0 + p + 1)
                    sp.dma_start(Mr[:, slot, :], M[:, ds((p + 2) * 2 * D, 2 * D)]).then_inc(m_in[slot], 16)
                sp.wait_ge(kv_done, b + 1)
                sp.dma_start(kv_dram[ds(b, 1)].rearrange("b p n -> p (b n)"),
                             kv[:].rearrange("p t n -> p (t n)")).then_inc(kv_out, 16)
                with sp.Fori(0, (NP0 - 2) // 2) as j:
                    refill(2 * j, 0, True, True)
                    refill(2 * j + 1, 1, True, True)
            sp.wait_ge(kv_out, 1 + 16 * B)

        @block.gpsimd
        def _(pool):
            nc.gpsimd.memset(kv[LAST // 32 * 32:, KT - 1, :], 0.0).then_inc(padded, 1)
            pool.wait_ge(w_in, 8 * 16)
            heads = kv[:, :, 0:D].rearrange("p t (h e) -> p t h e", e=HD1)
            rheads = rot[:].rearrange("p t (h e) -> p t h e", e=HD1)
            half = HD1 // 2
            with pool.Fori(0, B) as b:
                pool.wait_ge(kv_ev, (b + 1) * len(KVG))
                nc.gpsimd.tensor_tensor(kv[:], kv[:], bkv[:].unsqueeze(1).broadcast_to([P, KT, 2 * D]),
                                        ALU.add).then_inc(kv_bias, 1)
                pool.wait_ge(kv_bias, b + 1)
                for lo, hi in ((0, half), (half, 0)):
                    last = nc.gpsimd.tensor_tensor(rheads[:, :, :, lo:lo + half], heads[:, :, :, hi:hi + half],
                                                   sink[:, :, lo:lo + half].unsqueeze(2).broadcast_to([P, KT, H1, half]), ALU.mult)
                last.then_inc(kv_rot, 1)
                pool.wait_ge(kv_rot, b + 1)
                nc.gpsimd.tensor_tensor(heads, heads, cosk[:].unsqueeze(2).broadcast_to([P, KT, H1, HD1]), ALU.mult).then_inc(kv_cos, 1)
                pool.wait_ge(kv_cos, b + 1)
                nc.gpsimd.tensor_tensor(kv[:, :, 0:D], kv[:, :, 0:D], rot[:], ALU.add).then_inc(kv_done, 1)

        @block.tensor
        def _(pe):
            pe.sem_inc(ct_mm, 1)
            pe.sem_inc(q_mm, 1)
            pe.sem_inc(y_mm, 1)
            pe.wait_ge(w_in, 8 * 16)

            def make_q(b, p, slot, nbefore):
                pe.wait_ge(m_in[slot], 8 * (b * NP0 + p - slot) + 16)
                pe.wait_ge(y_add, 1 + nbefore)
                for h in range(2):
                    last = nc.tensor.matmul(pX[:, h * LQ:(h + 1) * LQ], Mr[:, slot, h * D:(h + 1) * D],
                                            xnT[:, ds(b * LQ, LQ)], start=True, stop=True)
                last.then_inc(q_mm, 1)

            def scores(c, slot, u):
                h, qt = u // QT, u % QT
                k = slice(CSTART[c], CSTART[c] + CH)
                q = slice(qt * P, (qt + 1) * P)
                nc.tensor.matmul(S[:, c, 0:CH], qh[:, slot, h, q], cTh[:, k], start=True, stop=False)
                nc.tensor.matmul(S[:, c, 0:CH], ql[:, slot, h, q], cTh[:, k], start=False, stop=False)
                nc.tensor.matmul(S[:, c, 0:CH], qh[:, slot, h, q], cTl[:, k], start=False, stop=True).then_inc(s_mm, 1)

            def make_v(b, p, g, slot, has_next=True):
                if g == 0 and has_next:
                    pe.wait_ge(q_lo, b * NP0 + p + 2)
                elif g == 0:
                    pe.wait_ge(y_add, 1 + b * NP0 + p - 1)
                elif g % 2:
                    pe.wait_ge(v_act, (b * NP0 + p) * 2 + g // 2 + 1)
                else:
                    pe.wait_ge(v_dve, (b * NP0 + p) * 2 + g // 2)
                for i, kt in enumerate(GROUPS[g]):
                    w = width(kt)
                    last = nc.tensor.matmul(pX[0:w, i * P:(i + 1) * P], cT[:, kt * P:kt * P + w],
                                            wv_sb[:, ds(p * P, P)], start=True, stop=True)
                last.then_inc(v_mm, 1)

            def values(prev, kts):
                for kt in kts:
                    w = width(kt)
                    for h in range(2):
                        last = nc.tensor.matmul(pO[h * HD0:(h + 1) * HD0, 0:LQ], V[0:w, prev, kt, h * HD0:(h + 1) * HD0],
                                                pT[prev][h][0:w, kt, :], start=kt == 0, stop=kt == KT - 1)
                if kts[-1] == KT - 1:
                    last.then_inc(o_mm, 1)

            def project(b, pp):
                pe.wait_ge(o_ev, 1 + 2 * (b * NP0 + pp + 1))
                for h in range(2):
                    for qt in range(QT):
                        i = h * QT + qt
                        last = nc.tensor.matmul(pX[:, i * D:(i + 1) * D], OA[:, h, qt * P:(qt + 1) * P],
                                                wo_sb[:, ds(pp, 1), :].rearrange("p a d -> p (a d)"), start=True, stop=True)
                last.then_inc(y_mm, 1)

            with pe.Fori(0, B) as b:
                pe.wait_ge(tok_in, 32 * (b + 1))
                pe.wait_ge(y_add, 1 + b * NP0)
                for g, kts in enumerate(GROUPS):
                    for i, kt in enumerate(kts):
                        w = width(kt)
                        last = nc.tensor.transpose(S[:, g, i * P:i * P + w], tok[0:w, kt, :], identf[0:w, 0:w])
                    last.then_inc(ct_mm, 1)
                make_q(b, 0, 0, b * NP0)
                pe.wait_ge(ct_ev, (b + 1) * NG)
                for i, kts in enumerate(KVG):
                    if i >= len(kv_banks):
                        pe.wait_ge(kv_ev, b * len(KVG) + i - len(kv_banks) + 1)
                    for n, kt in enumerate(kts):
                        w = width(kt)
                        last = nc.tensor.matmul(kv_banks[i % 3][0:w, n * 2 * D:(n + 1) * 2 * D], cT[:, kt * P:kt * P + w],
                                                wkv[:], start=True, stop=True)
                    last.then_inc(kv_mm, 1)
                pe.wait_ge(kv_ev, (b + 1) * len(KVG))
                pe.wait_ge(ct_lo, b + 1)
                pe.wait_ge(q_lo, b * NP0 + 1)
                for c in range(NCH):
                    scores(c, 0, 0)

                def pair(p, slot, has_prev, has_next):
                    prev = 1 - slot
                    for k in range(UNITS):
                        u = (b * NP0 + p) * UNITS + k
                        more = has_next or k < UNITS - 1
                        nslot, nu = (slot, k + 1) if k < UNITS - 1 else (prev, 0)

                        def next_scores(c):
                            if more:
                                pe.wait_ge(ex, u * NCH + c + 1)
                                scores(c, nslot, nu)

                        def turn(g):
                            pe.wait_ge(ex, u * NCH + min(NCH, (GROUPS[g][-1] * P + P - 1) // CH + 1))
                            if g >= 2:
                                pe.wait_ge((t_dve, t_act)[g % 2], 1 + u * 2 + 1)
                            else:
                                pe.wait_ge((t_dve, t_act)[g % 2], 1 + u * 2)
                            for i, kt in enumerate(GROUPS[g]):
                                w = width(kt)
                                last = nc.tensor.transpose(tb[g % 2][0:w, i * P:(i + 1) * P],
                                                           prob[:, k % 2, kt * P:kt * P + w], identf[:])
                            last.then_inc(t_mm, 1)

                        if k == UNITS - 1 and more:
                            pe.wait_ge(q_lo, b * NP0 + p + 2)
                        next_scores(0)
                        next_scores(1)
                        turn(0)
                        if k == 0 and has_next:
                            make_q(b, p + 1, prev, b * NP0 + p - 1 if has_prev else b * NP0)
                        if k == 1:
                            make_v(b, p, 1, slot)
                        if k == 2:
                            make_v(b, p, 3, slot)
                        next_scores(2)
                        turn(1)
                        next_scores(3)
                        turn(2)
                        turn(3)
                        if has_prev and k < 3:
                            if k == 0:
                                pe.wait_ge(t_act, 1 + u * 2)
                                pe.wait_ge(t_dve, 1 + u * 2)
                                pe.wait_ge(v_act, (b * NP0 + p) * 2)
                                pe.wait_ge(v_dve, (b * NP0 + p) * 2)
                                pe.wait_ge(o_ev, 1 + 2 * (b * NP0 + p - 1))
                            values(prev, ([0, 1, 2, 3, 4], [5, 6, 7, 8], [9, 10, 11, 12])[k])
                        if k == 0:
                            make_v(b, p, 0, slot, has_next)
                        if k == 1:
                            make_v(b, p, 2, slot)
                        if k == 3 and has_prev:
                            pe.wait_ge(v_dve, (b * NP0 + p) * 2 + 2)
                            project(b, p - 1)

                walk(pe, pair)
                end = (b + 1) * NP0
                pe.wait_ge(t_act, 1 + end * UNITS * 2)
                pe.wait_ge(t_dve, 1 + end * UNITS * 2)
                pe.wait_ge(o_ev, 1 + 2 * (end - 1))
                values(1, list(range(KT)))
                pe.wait_ge(y_add, 1 + end - 1)
                project(b, NP0 - 1)

        @block.scalar
        def _(act):
            act.sem_inc(t_act, 1)
            act.sem_inc(o_ev, 1)
            act.preload_act_table(ACT.Exp)

            def q_high(n, slot):
                act.wait_ge(q_mm, 1 + n + 1)
                nc.scalar.copy(qh[:, slot, :, :], pX[:].rearrange("p (h q) -> p h q", h=2)).then_inc(q_hi, 1)

            def exps(u, k, slot, chunks):
                for c in chunks:
                    if c == 0:
                        act.wait_ge(mx, u + 1)
                    lo = CSKIP[c]
                    nc.scalar.activation(prob[:, k % 2, c * CH:c * CH + CH - lo], S[:, c, lo:CH], ACT.Exp,
                                         bias=negm[:, k % 2:k % 2 + 1],
                                         accum_out=dens[:, slot, k, c:c + 1]).then_inc(ex, 1)

            def t_copy(g, u, k, slot):
                act.wait_ge(t_mm, u * NG + g + 1)
                h, qt = k // QT, k % QT
                n, w = len(GROUPS[g]), width(GROUPS[g][-1])
                nc.scalar.copy(pT[slot][h][0:w, GROUPS[g][0]:GROUPS[g][-1] + 1, qt * P:(qt + 1) * P],
                               tb[g % 2][0:w, 0:n * P].rearrange("p (n q) -> p n q", n=n)).then_inc(t_act, 1)

            def v_copy(n, g, slot):
                act.wait_ge(v_mm, n * NG + g + 1)
                nc.scalar.copy(V[:, slot, GROUPS[g][0]:GROUPS[g][-1] + 1, :],
                               pX[:].rearrange("p (n e) -> p n e", n=TG)).then_inc(v_act, 1)

            def o_copy(n):
                act.wait_ge(o_mm, n + 1)
                act.wait_ge(y_mm, 1 + n)
                act.wait_ge(zeroed, 1)
                for h in range(2):
                    r = slice(h * HD0, (h + 1) * HD0)
                    nc.scalar.copy(OA[r, h, :], pO[r, 0:LQ]).then_inc(o_ev, 1)

            with act.Fori(0, B) as b:
                for g, kts in enumerate(GROUPS):
                    act.wait_ge(ct_mm, 1 + b * NG + g + 1)
                    n = (len(kts) - 1) * P + width(kts[-1])
                    nc.scalar.copy(cT[:, kts[0] * P:kts[0] * P + n], S[:, g, 0:n]).then_inc(ct_ev, 1)
                q_high(b * NP0, 0)
                act.wait_ge(padded, 1)
                act.wait_ge(kv_out, 1 + 16 * b)
                for i, kts in enumerate(KVG):
                    act.wait_ge(kv_mm, b * len(KVG) + i + 1)
                    w, n = width(kts[-1]), len(kts)
                    nc.scalar.copy(kv[0:w, kts[0]:kts[0] + n, :],
                                   kv_banks[i % 3][0:w, 0:n * 2 * D].rearrange("p (n d) -> p n d", n=n)).then_inc(kv_ev, 1)
                exps(b * NU, 0, 0, range(NCH))

                def pair(p, slot, has_prev, has_next):
                    prev = 1 - slot
                    n = b * NP0 + p
                    for k in range(UNITS):
                        u = n * UNITS + k
                        more = has_next or k < UNITS - 1
                        nk, nslot = (k + 1, slot) if k < UNITS - 1 else (0, prev)
                        if k == 0 and has_next:
                            q_high(n + 1, prev)
                        t_copy(1, u, k, slot)
                        if more:
                            exps(u + 1, nk, nslot, [0])
                        t_copy(3, u, k, slot)
                        if more:
                            exps(u + 1, nk, nslot, [1, 2])
                        if k == 0:
                            v_copy(n, 0, slot)
                        if k == 1:
                            v_copy(n, 2, slot)
                        if k == 2 and has_prev:
                            o_copy(n - 1)
                        if more:
                            exps(u + 1, nk, nslot, [3])

                walk(act, pair)
                o_copy((b + 1) * NP0 - 1)

        @block.vector
        def _(dve):
            dve.sem_inc(t_dve, 1)
            dve.sem_inc(y_add, 1)
            nc.vector.memset(OA[:], 0.0).then_inc(zeroed, 1)

            def q_low(n, slot):
                dve.wait_ge(q_hi, n + 1)
                nc.vector.tensor_tensor(ql[:, slot, :, :], pX[:].rearrange("p (h q) -> p h q", h=2),
                                        qh[:, slot, :, :].bitcast(F32), ALU.subtract).then_inc(q_lo, 1)

            def maxima(u, k, chunks):
                for c in chunks:
                    dve.wait_ge(s_mm, u * NCH + c + 1)
                    nc.vector.reduce_max(mx4[:, k % 2, c:c + 1], S[:, c, 0:CH], AX.X).then_inc(mx_c, 1)
                if chunks[-1] == NCH - 1:
                    dve.wait_ge(mx_c, (u + 1) * NCH)
                    nc.vector.tensor_reduce(negm[:, k % 2:k % 2 + 1], mx4[:, k % 2, :], AX.X, ALU.max,
                                            negate=True).then_inc(mx, 1)

            def t_copy(g, u, k, slot):
                dve.wait_ge(t_mm, u * NG + g + 1)
                h, qt = k // QT, k % QT
                nc.vector.tensor_copy(pT[slot][h][:, GROUPS[g][0]:GROUPS[g][-1] + 1, qt * P:(qt + 1) * P],
                                      tb[g % 2][:].rearrange("p (n q) -> p n q", n=TG)).then_inc(t_dve, 1)

            def v_copy(n, g, slot):
                dve.wait_ge(v_mm, n * NG + g + 1)
                w, m = width(GROUPS[g][-1]), len(GROUPS[g])
                nc.vector.tensor_copy(V[0:w, slot, GROUPS[g][0]:GROUPS[g][-1] + 1, :],
                                      pX[0:w, 0:m * P].rearrange("p (n e) -> p n e", n=m)).then_inc(v_dve, 1)

            def sums(n, slot):
                nc.vector.tensor_reduce(den[:, slot, :], dens[:, slot, :, :], AX.X, ALU.add).then_inc(den_s, 1)
                dve.wait_ge(den_s, n + 1)
                nc.vector.reciprocal(rden[:, slot, :], den[:, slot, :]).then_inc(den_r, 1)

            def add(b, n, slot):
                dve.wait_ge(y_mm, 1 + n + 1)
                dve.wait_ge(den_r, n + 1)
                for h in range(2):
                    if h:
                        dve.wait_ge(added, n + 1)
                    for qt in range(QT):
                        i = h * QT + qt
                        xt = xs[:, ds((b * QT + qt) * D, D)]
                        last = nc.vector.scalar_tensor_tensor(xt, pX[:, i * D:(i + 1) * D], rden[:, slot, i:i + 1], xt,
                                                              ALU.mult, ALU.add)
                    if h == 0:
                        last.then_inc(added, 1)
                last.then_inc(y_add, 1)

            with dve.Fori(0, B) as b:
                dve.wait_ge(ct_ev, (b + 1) * NG)
                nc.vector.tensor_copy(cTh[:, 0:LK], cT[:, 0:LK]).then_inc(ct_hi, 1)
                dve.wait_ge(ct_hi, b + 1)
                nc.vector.tensor_tensor(cTl[:, 0:LK], cT[:, 0:LK], cTh[:, 0:LK].bitcast(F32), ALU.subtract).then_inc(ct_lo, 1)
                q_low(b * NP0, 0)
                maxima(b * NU, 0, range(NCH))

                def pair(p, slot, has_prev, has_next):
                    prev = 1 - slot
                    n = b * NP0 + p
                    for k in range(UNITS):
                        u = n * UNITS + k
                        more = has_next or k < UNITS - 1
                        if more:
                            maxima(u + 1, k + 1, [0, 1])
                        t_copy(0, u, k, slot)
                        if k == 0 and has_next:
                            q_low(n + 1, prev)
                        if k == 1:
                            v_copy(n, 1, slot)
                        if k == 2:
                            v_copy(n, 3, slot)
                        if more:
                            maxima(u + 1, k + 1, [2, 3])
                        t_copy(2, u, k, slot)
                        if k == 0 and has_prev:
                            dve.wait_ge(ex, n * UNITS * NCH)
                            sums(n - 1, prev)
                        if k == 3 and has_prev:
                            add(b, n - 1, prev)

                walk(dve, pair)
                last = (b + 1) * NP0
                dve.wait_ge(ex, last * UNITS * NCH)
                sums(last - 1, 1)
                add(b, last - 1, 1)



def normed_projection(nc, name, xs, g, beta, w, b, rope, identf, q_hi, q_lo, kv_all, eps=1e-5):
    NT = B * QT
    n = len(w)
    with ExitStack() as ctx:
        def sb(nm, shape, dt=F32):
            return ctx.enter_context(nc.sbuf_tensor(f"{name}_{nm}", shape, dt))

        def sem(nm):
            return ctx.enter_context(nc.semaphore(f"{name}_{nm}"))

        wsb = sb("w", [P, n * D])
        bsb = sb("b", [P, n * D])
        gcol, bcol, eps_c = sb("g", [P, 1]), sb("beta", [P, 1]), sb("eps", [P, 1])
        tabs = sb("tabs", [P, 4, QT * D])
        stats, mv = sb("stats", [P, NT, 6]), sb("mv", [P, NT, 2])
        std, rstd = sb("std", [P, NT]), sb("rstd", [P, NT])
        xh = sb("xh", [P, NT * D])
        hT = sb("hT", [P, NT * D])
        qs = sb("qs", [P, NT * D])
        rot = sb("rot", [P, NT * D])
        rotk = sb("rotk", [P, NT * D])
        banks = [ctx.enter_context(nc.psum_tensor(f"{name}_bank{i}", [P, 512], F32)) for i in range(8)]
        c_in, st, ag, sd, rs, xn = sem("c_in"), sem("st"), sem("ag"), sem("sd"), sem("rs"), sem("xn")
        t_mm, t_ev, p_mm, p_ev = sem("t_mm"), sem("t_ev"), sem("p_mm"), sem("p_ev")
        r1, r2, r3, r4, k1, k2 = sem("r1"), sem("r2"), sem("r3"), sem("r4"), sem("k1"), sem("k2")
        block = ctx.enter_context(nc.Block())
        loads = 2 * n + 2 + 1

        @block.sync
        def _(sp):
            for i in range(n):
                sp.dma_start(wsb[:, i * D:(i + 1) * D], w[i]).then_inc(c_in, 16)
                sp.dma_start(bsb[:, i * D:(i + 1) * D], row_everywhere(b[i])).then_inc(c_in, 16)
            sp.dma_start(gcol[:], g.rearrange("(p o) -> p o", o=1)).then_inc(c_in, 16)
            sp.dma_start(bcol[:], beta.rearrange("(p o) -> p o", o=1)).then_inc(c_in, 16)
            sp.dma_start(tabs[:], rope).then_inc(c_in, 16)

        @block.vector
        def _(dve):
            nc.vector.memset(eps_c[:], eps)
            for t in range(NT):
                last = nc.vector.bn_stats(stats[:, t, :], xs[:, t * D:(t + 1) * D])
            last.then_inc(st, 1)
            dve.wait_ge(st, 1)
            for t in range(NT):
                last = nc.vector.bn_aggr(mv[:, t, :], stats[:, t, :])
            last.then_inc(ag, 1)
            dve.wait_ge(sd, 1)
            nc.vector.reciprocal(rstd[:], std[:]).then_inc(rs, 1)
            dve.wait_ge(rs, 1)
            for t in range(NT):
                nc.vector.tensor_scalar(xh[:, t * D:(t + 1) * D], xs[:, t * D:(t + 1) * D], mv[:, t, 0:1],
                                        rstd[:, t:t + 1], ALU.subtract, ALU.mult).then_inc(xn, 1)
            dve.wait_ge(c_in, 16 * loads)
            for t in range(NT):
                dve.wait_ge(p_mm, t + 1)
                bank = banks[4 + t % 4]
                last = nc.vector.tensor_tensor(qs[:, t * D:(t + 1) * D], bank[:, 0:D], bsb[:, 0:D], ALU.add)
                if n > 1:
                    last = nc.vector.tensor_tensor(kv_all[:, t, :], bank[:, D:3 * D], bsb[:, D:3 * D], ALU.add)
                last.then_inc(p_ev, 1)
            dve.wait_ge(p_ev, NT)
            half = HD1 // 2
            src = qs[:].rearrange("p (b m e) -> p b m e", b=B, e=HD1)
            dst = rot[:].rearrange("p (b m e) -> p b m e", b=B, e=HD1)
            tab = tabs[:, 1, :].rearrange("p (m e) -> p m e", e=HD1).unsqueeze(1).broadcast_to([P, B, QT * H1, HD1])
            for lo, hi in ((0, half), (half, 0)):
                last = nc.vector.tensor_tensor(dst[:, :, :, lo:lo + half], src[:, :, :, hi:hi + half],
                                               tab[:, :, :, lo:lo + half], ALU.mult)
            last.then_inc(r1, 1)
            dve.wait_ge(r1, 1)
            qb = qs[:].rearrange("p (b m) -> p b m", b=B)
            nc.vector.tensor_tensor(qb, qb, tabs[:, 0, :].unsqueeze(1).broadcast_to([P, B, QT * D]), ALU.mult).then_inc(r2, 1)
            dve.wait_ge(r2, 1)
            nc.vector.tensor_tensor(qs[:], qs[:], rot[:], ALU.add).then_inc(r3, 1)
            dve.wait_ge(r3, 1)
            nc.vector.tensor_copy(q_hi[:], qs[:]).then_inc(r4, 1)
            dve.wait_ge(r4, 1)
            nc.vector.tensor_tensor(q_lo[:], qs[:], q_hi[:].bitcast(F32), ALU.subtract)

        @block.gpsimd
        def _(pool):
            if n == 1:
                return
            pool.wait_ge(p_ev, NT)
            half = HD1 // 2
            keys = kv_all[:, :, 0:D].rearrange("p (b t) (h e) -> p b t h e", b=B, e=HD1)
            dst = rotk[:].rearrange("p (b t h e) -> p b t h e", b=B, t=QT, e=HD1)
            for t in range(QT):
                for lo, hi in ((0, half), (half, 0)):
                    tab = tabs[:, 3, t * D:(t + 1) * D].rearrange("p (h e) -> p h e", e=HD1)
                    last = nc.gpsimd.tensor_tensor(dst[:, :, t, :, lo:lo + half], keys[:, :, t, :, hi:hi + half],
                                                   tab[:, :, lo:lo + half].unsqueeze(1).broadcast_to([P, B, H1, half]), ALU.mult)
            last.then_inc(k1, 1)
            pool.wait_ge(k1, 1)
            for t in range(QT):
                kk = kv_all[:, :, 0:D].rearrange("p (b t) d -> p b t d", b=B)[:, :, t, :]
                last = nc.gpsimd.tensor_tensor(kk, kk, tabs[:, 2, t * D:(t + 1) * D].unsqueeze(1).broadcast_to([P, B, D]), ALU.mult)
            last.then_inc(k2, 1)
            pool.wait_ge(k2, 1)
            nc.gpsimd.tensor_tensor(kv_all[:, :, 0:D], kv_all[:, :, 0:D], rotk[:].rearrange("p (t d) -> p t d", d=D), ALU.add)

        @block.scalar
        def _(act):
            act.wait_ge(ag, 1)
            nc.scalar.activation(std[:], mv[:, :, 1], ACT.Sqrt, bias=eps_c[:]).then_inc(sd, 1)
            act.wait_ge(c_in, 16 * loads)
            for q in range(NT // 4):
                act.wait_ge(t_mm, q + 1)
                nc.scalar.activation(hT[:, q * 512:(q + 1) * 512], banks[q][:], ACT.Identity, bias=bcol[:],
                                     scale=gcol[:]).then_inc(t_ev, 1)

        @block.tensor
        def _(pe):
            pe.wait_ge(c_in, 16 * loads)
            for t in range(NT):
                pe.wait_ge(xn, t + 1)
                last = nc.tensor.transpose(banks[t // 4][:, (t % 4) * D:(t % 4 + 1) * D], xh[:, t * D:(t + 1) * D], identf[:])
                if t % 4 == 3:
                    last.then_inc(t_mm, 1)
            for t in range(NT):
                pe.wait_ge(t_ev, t // 4 + 1)
                if t >= 4:
                    pe.wait_ge(p_ev, t - 3)
                nc.tensor.matmul(banks[4 + t % 4][:, 0:n * D], hT[:, t * D:(t + 1) * D], wsb[:], start=True, stop=True).then_inc(p_mm, 1)


def layer1_attention(nc, name, xs, q_hi, q_lo, kv_all, kv_dram, wo, bo, nkt, last_w, causal, consts, identf, identb, maskq, maskk):
    NK = nkt
    LKC = (NK - 1) * P + last_w
    S1 = B * G1
    chunks = 1 if causal else NCH
    RING = 2

    def kw(kt):
        return last_w if kt == NK - 1 else P

    with ExitStack() as ctx:
        def sb(nm, shape, dt=F32):
            return ctx.enter_context(nc.sbuf_tensor(f"{name}_{nm}", shape, dt))

        def sem(nm):
            return ctx.enter_context(nc.semaphore(f"{name}_{nm}"))

        wo_sb, bo_sb = sb("wo", [P, D]), sb("bo", [P, D])
        hmask = sb("hmask", [P, HG])
        kvb = None if causal else sb("kvb", [P, NK, 2 * D])
        ksrc = sb("ksrc", [P, NK, 4, R])
        qsrc = sb("qsrc", [P, QT, 4, R])
        kraw = sb("kraw", [P, NK, R]) if causal else None
        KX = sb("KX", [P, G1, NK * P], F32R)
        QX = sb("QX", [P, H1, LQ], F32R)
        V = sb("V", [P, G1, NK, HG, 32])
        pT = sb("pT", [P, RING, HG * LQ])
        mxc = sb("mxc", [P, 2, QT, HG, NCH])
        negm = sb("negm", [P, 2, QT, HG])
        OT = sb("OT", [P, LQ])
        rden = sb("rden", [P, 2, QT, HG])
        A = sb("A", [P, QT, D])
        AT = sb("AT", [P, LQ])
        st = [ctx.enter_context(nc.psum_tensor(f"{name}_st{i}", [P, 1024], F32)) for i in range(2)]
        mb = [ctx.enter_context(nc.psum_tensor(f"{name}_mb{i}", [P, 512], F32)) for i in range(2)]
        pO = ctx.enter_context(nc.psum_tensor(f"{name}_pO", [P, 512], F32))
        pX = ctx.enter_context(nc.psum_tensor(f"{name}_pX", [P, 512], F32))
        pY = st[1][:, 512:1024] if causal else pX

        c_in, kv_in, fixed = sem("c_in"), sem("kv_in"), sem("fixed")
        khi_done, src_done, qsrc_done = sem("khi_done"), sem("src_done"), sem("qsrc_done")
        v_done = sem("v_done")
        x_mm, x_ev = sem("x_mm"), sem("x_ev")
        y_mm, y_ev = sem("y_mm"), sem("y_ev")
        c_mm, c_red = sem("c_mm"), sem("c_red")
        m_done = sem("m_done")
        s_mm, ex, pv = sem("s_mm"), sem("ex"), sem("pv")
        o_ev, rd, biased = sem("o_ev"), sem("rd"), sem("biased")
        block = ctx.enter_context(nc.Block())

        groups = [list(range(t, min(t + TG, NK))) for t in range(0, NK, TG)]
        NXG = len(groups)
        PREP = NXG + 1
        NC = HG * QT * chunks if not causal else HG

        def turned(t, what):
            i = NXG if what == "q" else what
            if isinstance(t, tuple):
                return t[0] * PREP + (t[1] * PREP + i + 1)
            return t * PREP + i + 1

        def output(b, g, i):
            return b * (G1 + 2) + (g + i + 1)

        def before_turned(t, what):
            i = NXG if what == "q" else what
            return t[0] * PREP + (t[1] * PREP + i) if isinstance(t, tuple) else t * PREP + i

        if causal:
            ktask, kcopy = {(0, 0): 0, (0, 1): "q"}, {0: [0], 1: ["q"]}
        else:
            ktask, kcopy = {(1, 2): 0, (3, 2): 1, (5, 2): 2, (7, 2): 3, (9, 2): "q"}, {2: [0], 4: [1], 6: [2], 8: [3], 10: ["q0"], 11: ["q1"]}

        TURN = 1 if causal else 2
        NI = NC + 1

        def item(t, m):
            if isinstance(t, tuple):
                return t[0] * NI + (t[1] * NI - 1 + m + 1)
            return t * NI + m + 1 - (1 if t else 0)

        def item_bank(g, m, first=False):
            return mb[(g * NI + m + (0 if first else 1)) % 2]

        places = [[[], [], []] for _ in range(NK)]
        if causal:
            places = [[[0, 1], [2], [3]], [[], [4], []]]
        else:
            full = sorted({kt for kt, _ in ktask} | {NK - 2, NK - 1})
            left = iter(range(NI))
            for kt in range(NK):
                for place in range(3 if kt in full else 2):
                    places[kt][place].append(next(left))
            assert next(left, None) is None
        def steps(eng, step):
            with eng.Fori(0, B - 1) as b:
                for g in range(G1):
                    step(b, g, True, "all", True)
            for g in range(G1):
                step(B - 1, g, g < G1 - 1, "all" if g < G1 - 2 else "turn" if g == G1 - 2 else "none", g < 1)

        def count(t, more=0):
            return t[0] + (t[1] + more) if isinstance(t, tuple) else t + more

        @block.sync
        def _(sp):
            sp.dma_start(wo_sb[:], wo).then_inc(c_in, 16)
            sp.dma_start(bo_sb[:], row_everywhere(bo)).then_inc(c_in, 16)
            sp.dma_start(hmask[:], consts["hmask"]).then_inc(c_in, 16)
            if not causal:
                with sp.Fori(0, B) as b:
                    sp.wait_ge(v_done, 1 + b * G1)
                    sp.wait_ge(src_done, 1 + b * G1)
                    sp.dma_start(kvb[:].rearrange("p t n -> p (t n)"),
                                 kv_dram[ds(b, 1)].rearrange("b p n -> p (b n)")).then_inc(kv_in, 16)

        @block.gpsimd
        def _(pool):
            pool.sem_inc(v_done, 1)
            pool.sem_inc(src_done, 1)
            for g in range(G1):
                nc.gpsimd.memset(V[:, g, :, :, HD1:32], 0.0)
            nc.gpsimd.memset(qsrc[:, :, 3, :], 0.0)
            nc.gpsimd.memset(ksrc[:, :, 3, :], 1.0).then_inc(fixed, 1)
            pool.wait_ge(fixed, 1)
            for g in range(G1):
                last = nc.gpsimd.memset(V[:, g, :, :, HD1:HD1 + 1], 1.0)
            last.then_inc(fixed, 1)

            def prepare(b, g):
                t = b * G1 + g
                cols = slice(g * R, (g + 1) * R)
                vcols = slice(D + g * R, D + (g + 1) * R)
                if causal:
                    k, v = kv_all[:, ds(b * QT, NK), cols], kv_all[:, ds(b * QT, NK), vcols]
                else:
                    pool.wait_ge(kv_in, 16 * (b + 1))
                    k, v = kvb[:, :, cols], kvb[:, :, vcols]
                pool.wait_ge(fixed, 2)
                if not (isinstance(t, int) and t == 0):
                    pool.wait_ge(x_mm, t * PREP)
                hi = ksrc[:].bitcast(F32R)

                def query(blk, part):
                    return nc.gpsimd.tensor_copy(qsrc[:, :, blk, :], part[:, ds(b * QT * D, QT * D)].bitcast(F32)
                                          .rearrange("p (t d) -> p t d", d=D)[:, :, cols])

                query(0, q_hi)
                if causal:
                    nc.gpsimd.tensor_copy(kraw[:], k)
                nc.gpsimd.tensor_copy(hi[:, :, 0:2, :], k.unsqueeze(2).broadcast_to([P, NK, 2, R])).then_inc(khi_done, 1)
                query(2, q_hi)
                pool.wait_ge(khi_done, t + 1)
                nc.gpsimd.tensor_tensor(ksrc[:, :, 2, :], kraw[:] if causal else k, ksrc[:, :, 0, :], ALU.subtract).then_inc(src_done, 1)
                if not (isinstance(t, int) and t < G1):
                    pool.wait_ge(pv, 1 + (t - G1 + 1) * NK)
                query(1, q_lo).then_inc(qsrc_done, 1)
                nc.gpsimd.tensor_copy(V[:, g, :, :, 0:HD1], v.rearrange("p t (j e) -> p t j e", e=HD1)).then_inc(v_done, 1)

            for g in range(3):
                prepare(0, g)

            def step(b, g, has_next, items, has_prep):
                if has_prep and g == 0:
                    prepare(b, G1 - 1)
                elif has_prep:
                    prepare(b + 1, g - 1)
            steps(pool, step)

        @block.tensor
        def _(pe):
            pe.sem_inc(pv, 1)
            pe.wait_ge(c_in, 48)

            def turn(t, what):
                if not (isinstance(t, int) and t == 0 and what == 0):
                    pe.wait_ge(x_ev, before_turned(t, what))
                if what == 0:
                    pe.wait_ge(src_done, 1 + count(t, 1))
                if what == "q":
                    pe.wait_ge(qsrc_done, count(t, 1))
                    for qt in range(QT):
                        last = nc.tensor.transpose(pX[:, qt * P:(qt + 1) * P], qsrc[:, qt, :, :].rearrange("p a r -> p (a r)"), identf[:])
                else:
                    for i, kt in enumerate(groups[what]):
                        w = kw(kt)
                        last = nc.tensor.transpose(pX[:, i * P:i * P + w], ksrc[0:w, kt, :, :].rearrange("p a r -> p (a r)"),
                                                   identf[0:w, 0:w])
                last.then_inc(x_mm, 1)

            def stream_item(t, g, m, first=False, only=False):
                bank = item_bank(g, m, first)
                if only or not first and m == TURN:
                    if causal:
                        pe.wait_ge(c_red, item(t, -1))
                    else:
                        pe.wait_ge(m_done, count(t))
                        pe.wait_ge(c_red, item(t, m - 2))
                    for qt in range(QT):
                        last = nc.tensor.transpose(bank[0:HG, qt * P:(qt + 1) * P], negm[:, (g + 1) % 2, qt, :], identf[:])
                    last.then_inc(c_mm, 1)
                    return
                if m >= 2 or not first:
                    pe.wait_ge(c_red, item(t, m - 2))
                n = m if first or m < TURN else m - 1
                if causal:
                    for qt in range(QT):
                        nc.tensor.matmul(bank[:, qt * LQ:(qt + 1) * LQ], QX[:, HG * g + n, qt * P:(qt + 1) * P], KX[:, g, 0:LQ],
                                         start=True, stop=False)
                        last = nc.tensor.matmul(bank[:, qt * LQ:(qt + 1) * LQ], identb[:], maskq[:, qt * LQ:(qt + 1) * LQ],
                                                start=False, stop=True)
                else:
                    j, qt, c = n // (QT * NCH), n // NCH % QT, n % NCH
                    last = nc.tensor.matmul(bank[:, 0:CH], QX[:, HG * g + j, qt * P:(qt + 1) * P],
                                            KX[:, g, CSTART[c]:CSTART[c] + CH], start=True, stop=True)
                last.then_inc(c_mm, 1)

            def key_scores(s, g, kt):
                i = g * NK + kt
                w = kw(kt)
                k = KX[:, g, kt * P:kt * P + w]
                out = st[i % 2]
                if causal and kt == 1:
                    nc.tensor.matmul(out[0:w, 0:HG * P].rearrange("p (j q) -> p j q", j=HG), k,
                                     QX[:, HG * g:HG * (g + 1), P:LQ], start=True, stop=False)
                    for j in range(HG):
                        last = nc.tensor.matmul(out[:, j * P:(j + 1) * P], identb[:], maskk[:], start=False, stop=j == HG - 1)
                else:
                    for h2 in range(2):
                        last = nc.tensor.matmul(out[0:w, h2 * 512:(h2 + 1) * 512], k,
                                                QX[:, HG * g + 2 * h2:HG * g + 2 * h2 + 2, :].rearrange("p h q -> p (h q)"),
                                                start=True, stop=not causal)
                        if causal:
                            for j in range(2):
                                at = h2 * 512 + j * LQ
                                last = nc.tensor.matmul(out[:, at:at + P], identb[:], maskk[:], start=False, stop=j == 1)
                last.then_inc(s_mm, 1)

            def values(s, g, kt):
                i = g * NK + kt
                w = kw(kt)
                lo, n = (P, P) if causal and kt == 1 else (0, LQ)
                for j in range(HG):
                    last = nc.tensor.matmul(pO[32 * j:32 * j + 32, lo:LQ], V[0:w, g, kt, j, :],
                                            pT[0:w, i % RING, j * n:(j + 1) * n], start=kt == 0, stop=kt == NK - 1)
                last.then_inc(pv, 1)

            pe.wait_ge(fixed, 2)
            for t in range(3):
                for i in range(NXG):
                    turn(t, i)
                turn(t, "q")
            pe.wait_ge(x_ev, 3 * PREP)
            for m in range(NC):
                stream_item(0, 0, m, True)
            for m in range(NI):
                stream_item(1, 1, m)
            pe.wait_ge(c_red, item(1, TURN))
            key_scores(0, 0, 0)
            key_scores(0, 0, 1)

            def step(b, g, has_next, items, has_prep):
                s = b * G1 + g
                ng = (g + 1) % G1

                def between(kt, place):
                    for m in places[kt][place]:
                        if items == "turn" and m == TURN:
                            stream_item((s, 2), (g + 2) % G1, 0, only=True)
                        elif items == "all":
                            stream_item((s, 2), (g + 2) % G1, m)
                    if has_prep and (kt, place) in ktask:
                        if not causal and ktask[kt, place] == 0:
                            pe.wait_ge(y_ev, output(b, g, 0))
                        turn((s, 3), ktask[kt, place])

                pe.wait_ge(v_done, 1 + s + 1)
                for kt in range(NK):
                    between(kt, 0)
                    pe.wait_ge(ex, s * NK + kt + 1)
                    if kt == 0:
                        pe.wait_ge(o_ev, 1 + s)
                    values(s, g, kt)
                    between(kt, 1)
                    if kt + 2 < NK:
                        key_scores(s, g, kt + 2)
                    elif has_next:
                        if kt + 2 == NK:
                            pe.wait_ge(c_red, item((s, 2), TURN if items == "all" else 0))
                        key_scores(s + 1, ng, kt + 2 - NK)
                    between(kt, 2)
                if not causal:
                    pe.wait_ge(x_ev, turned((s, 3), "q") if has_prep else S1 * PREP)
                pe.wait_ge(y_ev, output(b, g, 0))
                pe.wait_ge(o_ev, 1 + s + 1)
                for qt in range(QT):
                    last = nc.tensor.transpose(pY[:, qt * P:(qt + 1) * P], OT[:, qt * P:(qt + 1) * P], identf[:])
                last.then_inc(y_mm, 1)
                if g == G1 - 1:
                    pe.wait_ge(y_ev, output(b, g, 1))
                    for qt in range(QT):
                        last = nc.tensor.transpose(pY[:, qt * P:(qt + 1) * P], A[:, qt, :], identf[:])
                    last.then_inc(y_mm, 1)
                    pe.wait_ge(y_ev, output(b, g, 2))
                    for qt in range(QT):
                        last = nc.tensor.matmul(pY[:, qt * D:(qt + 1) * D], AT[:, qt * P:(qt + 1) * P], wo_sb[:], start=True, stop=True)
                    last.then_inc(y_mm, 1)

            steps(pe, step)

        @block.scalar
        def _(act):
            act.sem_inc(o_ev, 1)
            act.preload_act_table(ACT.Exp)

            def turned_copy(t, g, what):
                if isinstance(what, str):
                    act.wait_ge(x_mm, turned(t, "q"))
                    for j in {"q": range(HG), "q0": range(HG // 2), "q1": range(HG // 2, HG)}[what]:
                        last = nc.scalar.activation(QX[:, HG * g + j, :], pX[:, 0:LQ], ACT.Copy, scale=hmask[:, j:j + 1])
                    if what == "q0":
                        return
                else:
                    act.wait_ge(x_mm, turned(t, what))
                    kts = groups[what]
                    m = (len(kts) - 1) * P + kw(kts[-1])
                    last = nc.scalar.copy(KX[:, g, kts[0] * P:kts[0] * P + m], pX[:, 0:m])
                last.then_inc(x_ev, 1)

            act.wait_ge(c_in, 48)
            for t in range(3):
                for i in range(NXG):
                    turned_copy(t, t, i)
                turned_copy(t, t, "q")

            def step(b, g, has_next, items, has_prep):
                s = b * G1 + g
                for kt in range(NK):
                    i = g * NK + kt
                    w = kw(kt)
                    act.wait_ge(s_mm, s * NK + kt + 1)
                    n = HG * P if causal and kt == 1 else HG * LQ
                    nc.scalar.activation(pT[0:w, i % RING, 0:n], st[i % 2][0:w, 0:n], ACT.Exp).then_inc(ex, 1)
                    if has_prep:
                        for what in kcopy.get(kt, ()):
                            turned_copy((s, 3), (g + 3) % G1, what)
                act.wait_ge(pv, 1 + (s + 1) * NK)
                nc.scalar.copy(OT[:], pO[:, 0:LQ]).then_inc(o_ev, 1)
                if g == G1 - 1:
                    act.wait_ge(y_mm, output(b, g, 1))
                    nc.scalar.copy(AT[:], pY[:, 0:LQ]).then_inc(y_ev, 1)
            steps(act, step)

        @block.vector
        def _(dve):
            dve.sem_inc(y_ev, 1)
            dve.wait_ge(c_in, 48)
            xt = xs[:].rearrange("p (t d) -> p t d", d=D)
            nc.vector.tensor_tensor(xt, xt, bo_sb[:].unsqueeze(1).broadcast_to([P, B * QT, D]), ALU.add).then_inc(biased, 1)

            def stream_item(t, g, m, first=False, only=False):
                bank = item_bank(g, m, first)
                dve.wait_ge(c_mm, item(t, m))
                if only or not first and m == TURN:
                    rows, pg = slice(3 * R, 3 * R + HG), (g + G1 - 1) % G1
                    nc.vector.tensor_tensor(QX[rows, HG * pg:HG * (pg + 1), :],
                                            bank[0:HG, 0:LQ].unsqueeze(1).broadcast_to([HG, HG, LQ]),
                                            identf[0:HG, 0:HG].unsqueeze(2).broadcast_to([HG, HG, LQ]), ALU.mult).then_inc(c_red, 1)
                    return
                n = m if first or m < TURN else m - 1
                if causal:
                    nc.vector.tensor_reduce(negm[:, g % 2, :, n], bank[:].rearrange("p (a k) -> p a k", a=QT), AX.X, ALU.max,
                                            negate=True).then_inc(c_red, 1)
                else:
                    j, qt, c = n // (QT * NCH), n // NCH % QT, n % NCH
                    nc.vector.reduce_max(mxc[:, g % 2, qt, j, c:c + 1], bank[:, 0:CH], AX.X).then_inc(c_red, 1)
                    if n == NC - 1:
                        dve.wait_ge(c_red, item(t, m))
                        nc.vector.tensor_reduce(negm[:, g % 2], mxc[:, g % 2], AX.X, ALU.max, negate=True).then_inc(m_done, 1)

            for m in range(NC):
                stream_item(0, 0, m, True)
            for m in range(NI):
                stream_item(1, 1, m)

            def step(b, g, has_next, items, has_prep):
                s = b * G1 + g
                for kt in range(NK):
                    for place in places[kt]:
                        for m in place:
                            if items == "turn" and m == TURN:
                                stream_item((s, 2), (g + 2) % G1, 0, only=True)
                            elif items == "all":
                                stream_item((s, 2), (g + 2) % G1, m)
                dve.wait_ge(y_mm, output(b, g, 0))
                o = pY[:, 0:LQ].rearrange("p (t j e) -> p t j e", t=QT, e=32)
                nc.vector.reciprocal(rden[:, g % 2], o[:, :, :, HD1]).then_inc(rd, 1)
                dve.wait_ge(rd, s + 1)
                for qt in range(QT):
                    last = nc.vector.tensor_tensor(A[:, qt, g * R:(g + 1) * R].rearrange("p (j e) -> p j e", e=HD1),
                                                   o[:, qt, :, 0:HD1],
                                                   rden[:, g % 2, qt, :].unsqueeze(2).broadcast_to([P, HG, HD1]), ALU.mult)
                last.then_inc(y_ev, 1)
                if g == G1 - 1:
                    dve.wait_ge(y_mm, output(b, g, 2))
                    dve.wait_ge(biased, 1)
                    xb = xs[:, ds(b * QT * D, QT * D)]
                    nc.vector.tensor_tensor(xb, xb, pY[:, 0:QT * D], ALU.add).then_inc(y_ev, 1)
            steps(dve, step)


def mlp(nc, xs, g, beta, w1, b1, w2, b2, identf, out, eps=1e-5):
    NT = B * QT
    FF = w1.shape[1]
    NF = FF // P
    NB = NT // 4
    C0, C1 = 0.7978845608028654, 0.044715
    with ExitStack() as ctx:
        def sb(nm, shape, dt=F32):
            return ctx.enter_context(nc.sbuf_tensor(f"mlp_{nm}", shape, dt))

        def sem(nm):
            return ctx.enter_context(nc.semaphore(f"mlp_{nm}"))

        w1s, w2s = sb("w1", [P, FF]), sb("w2", [P, NF, D])
        b1c, b2s = sb("b1", [P, NF]), sb("b2", [P, D])
        gcol, bcol, eps_c = sb("g", [P, 1]), sb("beta", [P, 1]), sb("eps", [P, 1])
        stats, mv = sb("stats", [P, NT, 6]), sb("mv", [P, NT, 2])
        std, rstd = sb("std", [P, NT]), sb("rstd", [P, NT])
        xh, hT = sb("xh", [P, NT * D]), sb("hT", [P, NT * D])
        act_out = sb("gelu", [P, 2, NF, 512])
        banks = [ctx.enter_context(nc.psum_tensor(f"mlp_bank{i}", [P, 512], F32)) for i in range(8)]
        c_in, st, ag, sd, rs, xn = sem("c_in"), sem("st"), sem("ag"), sem("sd"), sem("rs"), sem("xn")
        t_mm, t_ev, f_mm, gl, y_mm, y_ev, stored = (sem("t_mm"), sem("t_ev"), sem("f_mm"), sem("gl"), sem("y_mm"),
                                                    sem("y_ev"), sem("stored"))
        biased = sem("biased")
        block = ctx.enter_context(nc.Block())

        @block.sync
        def _(sp):
            sp.dma_start(w1s[:], w1).then_inc(c_in, 16)
            sp.dma_start(w2s[:], w2.rearrange("(n p) d -> p n d", p=P)).then_inc(c_in, 16)
            for f in range(NF):
                sp.dma_start(b1c[:, f:f + 1], b1[f * P:(f + 1) * P].rearrange("(p o) -> p o", o=1)).then_inc(c_in, 16)
            sp.dma_start(b2s[:], row_everywhere(b2)).then_inc(c_in, 16)
            sp.dma_start(gcol[:], g.rearrange("(p o) -> p o", o=1)).then_inc(c_in, 16)
            sp.dma_start(bcol[:], beta.rearrange("(p o) -> p o", o=1)).then_inc(c_in, 16)
            o = out.rearrange("b (t p) d -> p (b t) d", p=P)
            for k in range(NB):
                sp.wait_ge(y_ev, k + 1)
                sp.dma_start(o[:, 4 * k:4 * k + 4, :], xs[:, k * 512:(k + 1) * 512].rearrange("p (t d) -> p t d", d=D)).then_inc(stored, 16)
            sp.wait_ge(stored, 16 * NB)

        @block.vector
        def _(dve):
            nc.vector.memset(eps_c[:], eps)
            for t in range(NT):
                last = nc.vector.bn_stats(stats[:, t, :], xs[:, t * D:(t + 1) * D])
            last.then_inc(st, 1)
            dve.wait_ge(st, 1)
            for t in range(NT):
                last = nc.vector.bn_aggr(mv[:, t, :], stats[:, t, :])
            last.then_inc(ag, 1)
            dve.wait_ge(sd, 1)
            nc.vector.reciprocal(rstd[:], std[:]).then_inc(rs, 1)
            dve.wait_ge(rs, 1)
            for t in range(NT):
                nc.vector.tensor_scalar(xh[:, t * D:(t + 1) * D], xs[:, t * D:(t + 1) * D], mv[:, t, 0:1],
                                        rstd[:, t:t + 1], ALU.subtract, ALU.mult).then_inc(xn, 1)
            dve.wait_ge(c_in, 16 * (5 + NF))
            xt = xs[:].rearrange("p (t d) -> p t d", d=D)
            dve.wait_ge(xn, NT)
            nc.vector.tensor_tensor(xt, xt, b2s[:].unsqueeze(1).broadcast_to([P, NT, D]), ALU.add).then_inc(biased, 1)
            dve.wait_ge(biased, 1)
            for k in range(NB):
                dve.wait_ge(y_mm, k + 1)
                xb = xs[:, k * 512:(k + 1) * 512]
                nc.vector.tensor_tensor(xb, xb, banks[6 + k % 2][:], ALU.add).then_inc(y_ev, 1)

        @block.scalar
        def _(act):
            act.wait_ge(ag, 1)
            nc.scalar.activation(std[:], mv[:, :, 1], ACT.Sqrt, bias=eps_c[:]).then_inc(sd, 1)
            act.wait_ge(c_in, 16 * (5 + NF))
            for q in range(NB):
                act.wait_ge(t_mm, q + 1)
                nc.scalar.activation(hT[:, q * 512:(q + 1) * 512], banks[q][:], ACT.Identity, bias=bcol[:], scale=gcol[:]).then_inc(t_ev, 1)
            for k in range(NB):
                for f in range(NF):
                    act.wait_ge(f_mm, k * NF + f + 1)
                    if k >= 2:
                        act.wait_ge(y_mm, k - 1)
                    nc.scalar.activation(act_out[:, k % 2, f, :], banks[(k * NF + f) % 4][:], ACT.Gelu_apprx_tanh,
                                         bias=b1c[:, f:f + 1]).then_inc(gl, 1)

        @block.tensor
        def _(pe):
            pe.wait_ge(c_in, 16 * (5 + NF))
            for t in range(NT):
                pe.wait_ge(xn, t + 1)
                last = nc.tensor.transpose(banks[t // 4][:, (t % 4) * D:(t % 4 + 1) * D], xh[:, t * D:(t + 1) * D], identf[:])
                if t % 4 == 3:
                    last.then_inc(t_mm, 1)
            pe.wait_ge(t_ev, NB)

            def up(k):
                for f in range(NF):
                    if k:
                        pe.wait_ge(gl, (k - 1) * NF + f + 1)
                    nc.tensor.matmul(banks[f][:], w1s[:, f * P:(f + 1) * P], hT[:, k * 512:(k + 1) * 512], start=True, stop=True).then_inc(f_mm, 1)

            up(0)
            for k in range(NB):
                if k + 1 < NB:
                    up(k + 1)
                pe.wait_ge(gl, (k + 1) * NF)
                if k >= 2:
                    pe.wait_ge(y_ev, k - 1)
                for i in range(4):
                    for f in range(NF):
                        last = nc.tensor.matmul(banks[6 + k % 2][:, i * D:(i + 1) * D], act_out[:, k % 2, f, i * P:(i + 1) * P],
                                                w2s[:, f, :], start=f == 0, stop=f == NF - 1)
                last.then_inc(y_mm, 1)


def build(nc, x, ctx_in, w, consts, out):
    kv_dram = nc.dram_tensor("kv_scratch", (B, P, KT * 2 * D), F32).ap()

    def w1(name):
        return w["L1_xattn_" + name]

    with ExitStack() as ctx:
        def sb(name, shape, dt=F32):
            return ctx.enter_context(nc.sbuf_tensor(name, shape, dt))

        xs = sb("xs", [P, B * QT * D])
        identf = sb("identf", [P, P])
        with ExitStack() as layer0:
            xnT = layer0.enter_context(nc.sbuf_tensor("xnT", [P, B * LQ], F32))
            M = layer0.enter_context(nc.sbuf_tensor("M", [P, H0 * D], F32))
            epsc = layer0.enter_context(nc.sbuf_tensor("epsc", [P, 1], F32))
            layer0_setup(nc, x, w["L0_xattn_norm_w"], w["L0_xattn_wq"], w["L0_xattn_wk"], consts["ident"], xs, xnT, M,
                         identf, epsc)
            layer0_attention(nc, ctx_in, w["L0_xattn_wv"], w["L0_xattn_wo"], w1("ca_wk"), w1("ca_wv"), w1("ca_bk"),
                             w1("ca_bv"), consts["cos_k"], consts["sin_k"], kv_dram, xs, xnT, M, identf)
        identb, maskq, maskk = sb("identb", [P, P], BF16), sb("maskq", [P, QT * LQ], BF16), sb("maskk", [P, P], BF16)
        q_hi, q_lo = sb("q_hi", [P, B * QT * D], F32R), sb("q_lo", [P, B * QT * D], F32R)
        with ExitStack() as self_attention:
            kv_all = self_attention.enter_context(nc.sbuf_tensor("kv_all", [P, B * QT, 2 * D], F32))
            load_masks(nc, consts, identf, identb, maskq, maskk)
            normed_projection(nc, "self", xs, w1("ln1_g"), w1("ln1_b"), [w1("sa_wq"), w1("sa_wk"), w1("sa_wv")],
                              [w1("sa_bq"), w1("sa_bk"), w1("sa_bv")], consts["rope"], identf, q_hi, q_lo, kv_all)
            layer1_attention(nc, "sa", xs, q_hi, q_lo, kv_all, None, w1("sa_wo"), w1("sa_bo"), QT, P, True, consts,
                             identf, identb, maskq, maskk)
        normed_projection(nc, "cross", xs, w1("ln2_g"), w1("ln2_b"), [w1("ca_wq")], [w1("ca_bq")], consts["rope"], identf,
                          q_hi, q_lo, None)
        layer1_attention(nc, "ca", xs, q_hi, q_lo, None, kv_dram, w1("ca_wo"), w1("ca_bo"), KT, LAST, False, consts,
                         identf, identb, maskq, maskk)
        mlp(nc, xs, w1("ln3_g"), w1("ln3_b"), w1("fc1_w"), w1("fc1_b"), w1("fc2_w"), w1("fc2_b"), identf, out)


def load_masks(nc, consts, identf, identb, maskq, maskk):
    with ExitStack() as ctx:
        mq = ctx.enter_context(nc.sbuf_tensor("mq32", [P, QT * LQ], F32))
        mk = ctx.enter_context(nc.sbuf_tensor("mk32", [P, P], F32))
        m_in = ctx.enter_context(nc.semaphore("masks_in"))
        block = ctx.enter_context(nc.Block())

        @block.sync
        def _(sp):
            sp.dma_start(mq[:], consts["mask_q"]).then_inc(m_in, 16)
            sp.dma_start(mk[:], consts["mask_k"]).then_inc(m_in, 16)

        @block.vector
        def _(dve):
            nc.vector.tensor_copy(identb[:], identf[:])
            dve.wait_ge(m_in, 32)
            nc.vector.tensor_copy(maskq[:], mq[:])
            nc.vector.tensor_copy(maskk[:], mk[:])


def constants():
    f = np.float32
    inv = (f(1.0) / np.power(f(10000.0), np.arange(0, HD1, 2, dtype=f) / f(HD1))).astype(f)
    pos = np.arange(KT * P, dtype=f)
    ang = np.outer(pos, inv).astype(f)
    cos, sin = np.cos(ang).astype(f), np.sin(ang).astype(f)
    live = (pos < LK)[:, None]
    cos8 = np.where(live, np.concatenate([cos, cos], 1), f(0))
    sin8 = np.where(live, np.concatenate([-sin, sin], 1), f(0))
    tiles = lambda a: np.ascontiguousarray(a.reshape(-1, P, HD1).transpose(1, 0, 2)).astype(f)
    heads = lambda a: np.repeat(tiles(a[:LQ])[:, :, None, :], H1, 2).reshape(P, QT * D)
    scale = f(HD1 ** -0.5)
    rope = np.stack([heads(cos8) * scale, heads(sin8) * scale, heads(cos8), heads(sin8)], 1).astype(f)
    r = np.arange(P)[:, None]
    j = np.arange(HG)[None, :]
    hmask = np.where(r < 3 * R, (r % R) // HD1 == j, r - 3 * R == j).astype(f)
    q, k = np.arange(LQ)[:, None], np.arange(LQ)[None, :]
    mask = np.where(k <= q, f(0), f(NEG)).astype(f)
    return {"ident": np.eye(P, dtype=f), "cos_k": tiles(cos8), "sin_k": tiles(sin8), "rope": rope, "hmask": hmask,
            "mask_q": np.ascontiguousarray(mask.reshape(QT, P, LQ).transpose(1, 0, 2).reshape(P, QT * LQ)),
            "mask_k": np.ascontiguousarray(mask[:P, :P].T)}


def kernel(**inputs):
    import concourse.bacc as bacc
    from concourse.bass_utils import run_bass_kernel_spmd

    nc = bacc.Bacc("TRN2", target_bir_lowering=False, num_devices=1)
    arrays, aps = {}, {}
    for name, a in [*inputs.items(), *constants().items()]:
        a = np.ascontiguousarray(a)
        arrays[f"in_{name}"] = a
        aps[name] = nc.dram_tensor(f"in_{name}", a.shape, mybir.dt.from_np(a.dtype), kind="ExternalInput").ap()
    out = nc.dram_tensor("out", (B, LQ, D), F32, kind="ExternalOutput").ap()
    build(nc, aps["x"], aps["ctx_1024"], aps, aps, out)
    return run_bass_kernel_spmd(nc, [arrays], core_ids=[0]).results[0]["out"]
```

```python
from contextlib import ExitStack

import numpy as np

import concourse.bass as bass
from concourse import mybir

F32 = mybir.dt.float32
F32R = mybir.dt.float32r
BF16 = mybir.dt.bfloat16
ALU = mybir.AluOpType
ACT = mybir.ActivationFunctionType
AX = mybir.AxisListType
ds = bass.ds

P = 128
B, LQ, D = 8, 256, 128
LK = 1601
QT = LQ // P
KT = (LK + P - 1) // P
LAST = LK - (KT - 1) * P
NCH = 4
CH = (LK + NCH - 1) // NCH
CH += CH % 2
CSTART = [min(c * CH, LK - CH) for c in range(NCH)]
CSKIP = [c * CH - CSTART[c] for c in range(NCH)]
H0, HD0 = 16, 64
NP0 = H0 // 2
TG = 4
GROUPS = [list(range(g, min(g + TG, KT))) for g in range(0, KT, TG)]
NG = len(GROUPS)
UNITS = 2 * QT
H1, HD1 = 16, 8
KVG = [list(range(t, min(t + 2, KT))) for t in range(0, KT, 2)]
HG = 4
G1 = H1 // HG
R = HG * HD1
NEG = -1e30


def width(kt):
    return LAST if kt == KT - 1 else P


def row_everywhere(row):
    return row.rearrange("(o n) -> o n", o=1).broadcast_to([P, row.shape[0]])


def layer0_setup(nc, ctx, x, norm_w, wq, wk, ident, mask_q, mask_k, xs, xnT, M, identf, identb, maskq, maskk, banks):
    NT = B * QT

    def sb(name, shape, dt=F32):
        return ctx.enter_context(nc.sbuf_tensor(name, shape, dt))

    def sem(name):
        return ctx.enter_context(nc.semaphore(name))

    wq_sb = sb("wq_sb", [P, H0 * HD0])
    wk_sb = sb("wk_sb", [P, H0 * HD0])
    wqT = sb("wqT", [P, NP0, D])
    wkT = sb("wkT", [P, NP0, D])
    sq = sb("sq", [P, NT * D])
    ms = sb("ms", [P, 4, NT])
    nw = sb("nw", [P, 1])
    epsc = sb("epsc", [P, 1])
    mq, mk = sb("mq32", [P, QT * LQ]), sb("mk32", [P, P])

    x_in, w_in, c_in, masks_in = sem("x_in"), sem("w_in"), sem("c_in"), sem("masks_in")
    squared, meansq, rms, inv, normed = sem("squared"), sem("meansq"), sem("rms"), sem("inv"), sem("normed")
    wT_mm, wT_act, wT_dve = sem("wT_mm"), sem("wT_act"), sem("wT_dve")
    m_mm, m_ev = sem("m_mm"), sem("m_ev")
    xt_mm, xt_ev = sem("xt_mm"), sem("xt_ev")

    def sync(sp):
        sp.dma_start(identf[:], ident).then_inc(c_in, 16)
        sp.dma_start(wq_sb[:], wq).then_inc(w_in, 16)
        sp.dma_start(wk_sb[:], wk).then_inc(w_in, 16)
        sp.dma_start(xs[:].rearrange("p (t d) -> p t d", d=D),
                     x.rearrange("b (t p) d -> p (b t) d", p=P)).then_inc(x_in, 16)
        sp.dma_start(nw[:], norm_w.rearrange("(p o) -> p o", o=1)).then_inc(c_in, 16)

    def sync_masks(sp):
        sp.dma_start(mq[:], mask_q).then_inc(masks_in, 16)
        sp.dma_start(mk[:], mask_k).then_inc(masks_in, 16)

    def vector(dve):
        dve.wait_ge(wT_mm, 2)
        nc.vector.tensor_copy(wqT[:, 4:8, :], banks[1][:].rearrange("p (n d) -> p n d", d=D)).then_inc(wT_dve, 1)
        dve.wait_ge(wT_mm, 4)
        nc.vector.tensor_copy(wkT[:, 4:8, :], banks[3][:].rearrange("p (n d) -> p n d", d=D)).then_inc(wT_dve, 1)
        dve.wait_ge(x_in, 16)
        nc.vector.memset(epsc[:], 1e-6)
        nc.vector.tensor_tensor(sq[:], xs[:], xs[:], ALU.mult).then_inc(squared, 1)
        dve.wait_ge(squared, 1)
        nc.vector.tensor_reduce(ms[:, 0, :], sq[:].rearrange("p (t d) -> p t d", d=D), AX.X, ALU.add).then_inc(meansq, 1)
        dve.wait_ge(rms, 1)
        nc.vector.reciprocal(ms[:, 2, :], ms[:, 1, :]).then_inc(inv, 1)
        dve.wait_ge(inv, 1)
        nc.vector.tensor_tensor(sq[:].rearrange("p (t d) -> p t d", d=D), xs[:].rearrange("p (t d) -> p t d", d=D),
                                ms[:, 2, :].unsqueeze(2).broadcast_to([P, NT, D]), ALU.mult).then_inc(normed, 1)
        for g in range(4):
            dve.wait_ge(m_mm, g + 1)
            nc.vector.tensor_copy(M[:].rearrange("p (n r d) -> p n r d", r=2, d=D)[:, 4 * (g // 2):4 * (g // 2) + 4, g % 2, :],
                                  banks[4 + g % 2][:].rearrange("p (n d) -> p n d", d=D)).then_inc(m_ev, 1)

    def scalar(act):
        act.wait_ge(wT_mm, 1)
        nc.scalar.copy(wqT[:, 0:4, :], banks[0][:].rearrange("p (n d) -> p n d", d=D)).then_inc(wT_act, 1)
        act.wait_ge(wT_mm, 3)
        nc.scalar.copy(wkT[:, 0:4, :], banks[2][:].rearrange("p (n d) -> p n d", d=D)).then_inc(wT_act, 1)
        act.wait_ge(meansq, 1)
        nc.scalar.activation(ms[:, 1, :], ms[:, 0, :], ACT.Sqrt, bias=epsc[:], scale=1.0 / D).then_inc(rms, 1)
        act.wait_ge(c_in, 32)
        for g in range(4):
            act.wait_ge(xt_mm, g + 1)
            nc.scalar.activation(xnT[:, g * 512:(g + 1) * 512], banks[6 + g % 2][:], ACT.Copy,
                                 scale=nw[:]).then_inc(xt_ev, 1)

    def tensor(pe):
        pe.wait_ge(c_in, 32)
        pe.wait_ge(w_in, 32)
        for w, src in enumerate((wq_sb, wk_sb)):
            for n in range(NP0):
                last = nc.tensor.transpose(banks[2 * w + n // 4][:, (n % 4) * D:(n % 4 + 1) * D],
                                           src[:, n * P:(n + 1) * P], identf[:])
                if n % 4 == 3:
                    last.then_inc(wT_mm, 1)
        pe.wait_ge(wT_act, 2)
        pe.wait_ge(wT_dve, 2)
        for g in range(4):
            if g >= 2:
                pe.wait_ge(m_ev, g - 1)
            rows = slice((g % 2) * HD0, (g % 2 + 1) * HD0)
            for i in range(4):
                n = 4 * (g // 2) + i
                last = nc.tensor.matmul(banks[4 + g % 2][:, i * D:(i + 1) * D], wqT[rows, n, :],
                                        wkT[rows, n, :], start=True, stop=True)
            last.then_inc(m_mm, 1)
        pe.wait_ge(normed, 1)
        for g in range(4):
            if g >= 2:
                pe.wait_ge(xt_ev, g - 1)
            for i in range(4):
                t = 4 * g + i
                last = nc.tensor.transpose(banks[6 + g % 2][:, i * D:(i + 1) * D], sq[:, t * D:(t + 1) * D], identf[:])
            last.then_inc(xt_mm, 1)
        pe.wait_ge(m_ev, 4)
        pe.wait_ge(xt_ev, 4)

    def vector_masks(dve):
        dve.wait_ge(masks_in, 32)
        nc.vector.tensor_copy(identb[:], identf[:])
        nc.vector.tensor_copy(maskq[:], mq[:])
        nc.vector.tensor_copy(maskk[:], mk[:])

    return (sync, sync_masks, vector, vector_masks, scalar, tensor), m_ev


def layer0_attention(nc, setup_in, ctx_in, wv, wo, cross_wk, cross_wv, cross_bk, cross_bv, cos_k, sin_k, kv_dram, xs, xnT, M, identf):
    with ExitStack() as ctx:
        def sb(name, shape, dt=F32):
            return ctx.enter_context(nc.sbuf_tensor(name, shape, dt))

        def sem(name):
            return ctx.enter_context(nc.semaphore(name))

        tok = sb("ctx_tok", [P, KT, D])
        cT = sb("cT", [P, LK + 1])
        cTh = sb("cTh", [P, LK + 1], F32R)
        cTl = sb("cTl", [P, LK + 1], F32R)
        wv_sb = sb("wv_sb", [P, H0 * HD0])
        wo_sb = sb("wo_sb", [P, NP0, D])
        Mr = sb("Mr", [P, 2, 2 * D])
        qh = sb("qh", [P, 2, 2, LQ], F32R)
        ql = sb("ql", [P, 2, 2, LQ], F32R)
        prob = sb("prob", [P, 2, KT * P])
        pT = [[sb(f"pT{s}{h}", [P, KT, LQ]) for h in range(2)] for s in range(2)]
        V = sb("V0", [P, 2, KT, P])
        OA = sb("OA", [P, 2, LQ])
        wkv = sb("wkv", [P, 2 * D])
        bkv = sb("bkv", [P, 2 * D])
        cosk = sb("cosk", [P, KT, HD1])
        sink = sb("sink", [P, KT, HD1])
        kv = sb("kv", [P, KT, 2 * D])
        rot = sb("rot", [P, KT, D])
        mx4 = sb("mx4", [P, 2, NCH])
        negm = sb("negm", [P, 2])
        dens = sb("dens", [P, 2, UNITS, NCH])
        den = sb("den", [P, 2, UNITS])
        rden = sb("rden", [P, 2, UNITS])
        S = ctx.enter_context(nc.psum_tensor("S0", [P, NCH, 512], F32))
        tb = [ctx.enter_context(nc.psum_tensor(f"tb{i}", [P, 512], F32)) for i in range(2)]
        pO = ctx.enter_context(nc.psum_tensor("pO", [P, 512], F32))
        pX = ctx.enter_context(nc.psum_tensor("pX", [P, 512], F32))

        (setup_sync, setup_sync_masks, setup_vector, setup_vector_masks, setup_scalar, setup_tensor), m_ev = layer0_setup(
            nc, ctx, *setup_in, [S[:, c, :] for c in range(NCH)] + [tb[0], tb[1], pO, pX])
        w_in, tok_in = sem("w_in0"), sem("tok_in")
        m_in = [sem(f"m_in{i}") for i in range(2)]
        zeroed = sem("zeroed")
        ct_mm, ct_ev, ct_hi, ct_lo = sem("ct_mm"), sem("ct_ev"), sem("ct_hi"), sem("ct_lo")
        q_mm, q_hi, q_lo = sem("q_mm"), sem("q_hi"), sem("q_lo")
        s_mm = sem("s_mm")
        mx_c, mx = sem("mx_c"), sem("mx")
        ex = sem("ex")
        t_mm = sem("t_mm")
        t_act, t_dve = sem("t_act"), sem("t_dve")
        v_mm, v_act, v_dve = sem("v_mm"), sem("v_act"), sem("v_dve")
        o_mm, o_ev = sem("o_mm"), sem("o_ev")
        y_mm, y_add = sem("y_mm"), sem("y_add")
        kv_mm, kv_ev, kv_bias, kv_rot, kv_cos, kv_done, kv_out = (
            sem("kv_mm"), sem("kv_ev"), sem("kv_bias"), sem("kv_rot"), sem("kv_cos"), sem("kv_done"), sem("kv_out"))
        padded = sem("padded")
        den_s, den_r, added = sem("den_s"), sem("den_r"), sem("added")
        kv_banks = [tb[0], tb[1], tb[0]] + [pO] * (len(KVG) - 3)
        KV_BESIDE = [[3], [4], [5], list(range(6, len(KVG)))]
        block = ctx.enter_context(nc.Block())

        NU = NP0 * UNITS

        VALUES_AT = {0: 0, 1: 1, 2: 2}
        VALUES_TILES = ([0, 1, 2, 3], [4, 5, 6, 7], [8, 9, 10, 11, 12])

        def walk(eng, pair):
            pair(0, 0, False, True)
            with eng.Fori(0, (NP0 - 2) // 2) as j:
                pair(2 * j + 1, 1, True, True)
                pair(2 * j + 2, 0, True, True)
            pair(NP0 - 1, 1, True, False)

        @block.sync
        def _(sp):
            sp.sem_inc(kv_out, 1)
            setup_sync(sp)
            sp.dma_start(wv_sb[:], wv).then_inc(w_in, 16)
            sp.dma_start(wo_sb[:], wo.rearrange("(n p) d -> p n d", p=P)).then_inc(w_in, 16)
            for i, (w, bias) in enumerate(((cross_wk, cross_bk), (cross_wv, cross_bv))):
                sp.dma_start(wkv[:, i * D:(i + 1) * D], w).then_inc(w_in, 16)
                sp.dma_start(bkv[:, i * D:(i + 1) * D], row_everywhere(bias)).then_inc(w_in, 16)
            sp.dma_start(cosk[:], cos_k).then_inc(w_in, 16)
            sp.dma_start(sink[:], sin_k).then_inc(w_in, 16)
            setup_sync_masks(sp)
            with sp.Fori(0, B) as b:
                sp.wait_ge(ct_mm, 1 + b * NG)
                sp.dma_start(tok[:, 0:KT - 1, :],
                             ctx_in[ds(b, 1), 0:(KT - 1) * P, :].rearrange("b (t p) d -> p (b t) d", p=P)).then_inc(tok_in, 16)
                sp.dma_start(tok[0:LAST, KT - 1, :],
                             ctx_in[ds(b, 1), (KT - 1) * P:LK, :].rearrange("b p d -> p (b d)")).then_inc(tok_in, 16)
                sp.wait_ge(m_ev, 4)
                for p in range(2):
                    sp.wait_ge(q_mm, 1 + b * NP0)
                    sp.dma_start(Mr[:, p, :], M[:, p * 2 * D:(p + 1) * 2 * D]).then_inc(m_in[p], 16)

                def refill(p, slot, has_prev, has_next):
                    sp.wait_ge(q_mm, 1 + b * NP0 + p + 1)
                    sp.dma_start(Mr[:, slot, :], M[:, ds((p + 2) * 2 * D, 2 * D)]).then_inc(m_in[slot], 16)
                with sp.Fori(0, (NP0 - 2) // 2) as j:
                    refill(2 * j, 0, True, True)
                    refill(2 * j + 1, 1, True, True)
                sp.wait_ge(kv_done, b + 1)
                sp.dma_start(kv_dram[ds(b, 1)].rearrange("b p n -> p (b n)"),
                             kv[:].rearrange("p t n -> p (t n)")).then_inc(kv_out, 16)
            sp.wait_ge(kv_out, 1 + 16 * B)

        @block.gpsimd
        def _(pool):
            nc.gpsimd.memset(kv[LAST // 32 * 32:, KT - 1, :], 0.0).then_inc(padded, 1)
            pool.wait_ge(w_in, 8 * 16)
            heads = kv[:, :, 0:D].rearrange("p t (h e) -> p t h e", e=HD1)
            rheads = rot[:].rearrange("p t (h e) -> p t h e", e=HD1)
            half = HD1 // 2
            with pool.Fori(0, B) as b:
                pool.wait_ge(kv_ev, (b + 1) * len(KVG))
                nc.gpsimd.tensor_tensor(kv[:], kv[:], bkv[:].unsqueeze(1).broadcast_to([P, KT, 2 * D]),
                                        ALU.add).then_inc(kv_bias, 1)
                pool.wait_ge(kv_bias, b + 1)
                for lo, hi in ((0, half), (half, 0)):
                    last = nc.gpsimd.tensor_tensor(rheads[:, :, :, lo:lo + half], heads[:, :, :, hi:hi + half],
                                                   sink[:, :, lo:lo + half].unsqueeze(2).broadcast_to([P, KT, H1, half]), ALU.mult)
                last.then_inc(kv_rot, 1)
                pool.wait_ge(kv_rot, b + 1)
                nc.gpsimd.tensor_tensor(heads, heads, cosk[:].unsqueeze(2).broadcast_to([P, KT, H1, HD1]), ALU.mult).then_inc(kv_cos, 1)
                pool.wait_ge(kv_cos, b + 1)
                nc.gpsimd.tensor_tensor(kv[:, :, 0:D], kv[:, :, 0:D], rot[:], ALU.add).then_inc(kv_done, 1)

        @block.tensor
        def _(pe):
            pe.sem_inc(ct_mm, 1)
            pe.sem_inc(q_mm, 1)
            pe.sem_inc(y_mm, 1)
            setup_tensor(pe)
            pe.wait_ge(w_in, 8 * 16)

            def make_q(b, p, slot, nbefore):
                pe.wait_ge(m_in[slot], 8 * (b * NP0 + p - slot) + 16)
                pe.wait_ge(y_add, 1 + nbefore)
                for h in range(2):
                    last = nc.tensor.matmul(pX[:, h * LQ:(h + 1) * LQ], Mr[:, slot, h * D:(h + 1) * D],
                                            xnT[:, ds(b * LQ, LQ)], start=True, stop=True)
                last.then_inc(q_mm, 1)

            def scores(c, slot, u):
                h, qt = u // QT, u % QT
                k = slice(CSTART[c], CSTART[c] + CH)
                q = slice(qt * P, (qt + 1) * P)
                nc.tensor.matmul(S[:, c, 0:CH], qh[:, slot, h, q], cTh[:, k], start=True, stop=False)
                nc.tensor.matmul(S[:, c, 0:CH], ql[:, slot, h, q], cTh[:, k], start=False, stop=False)
                nc.tensor.matmul(S[:, c, 0:CH], qh[:, slot, h, q], cTl[:, k], start=False, stop=True).then_inc(s_mm, 1)

            def make_v(b, p, g, slot, has_next=True):
                if g == 0 and has_next:
                    pe.wait_ge(q_lo, b * NP0 + p + 2)
                elif g == 0:
                    pe.wait_ge(y_add, 1 + b * NP0 + p - 1)
                elif g % 2:
                    pe.wait_ge(v_act, (b * NP0 + p) * 2 + g // 2 + 1)
                else:
                    pe.wait_ge(v_dve, (b * NP0 + p) * 2 + g // 2)
                for i, kt in enumerate(GROUPS[g]):
                    w = width(kt)
                    last = nc.tensor.matmul(pX[0:w, i * P:(i + 1) * P], cT[:, kt * P:kt * P + w],
                                            wv_sb[:, ds(p * P, P)], start=True, stop=True)
                last.then_inc(v_mm, 1)

            def values(prev, kts):
                for kt in kts:
                    w = width(kt)
                    for h in range(2):
                        last = nc.tensor.matmul(pO[h * HD0:(h + 1) * HD0, 0:LQ], V[0:w, prev, kt, h * HD0:(h + 1) * HD0],
                                                pT[prev][h][0:w, kt, :], start=kt == 0, stop=kt == KT - 1)
                if kts[-1] == KT - 1:
                    last.then_inc(o_mm, 1)

            def project(b, pp):
                pe.wait_ge(o_ev, 1 + 2 * (b * NP0 + pp + 1))
                for h in range(2):
                    for qt in range(QT):
                        i = h * QT + qt
                        last = nc.tensor.matmul(pX[:, i * D:(i + 1) * D], OA[:, h, qt * P:(qt + 1) * P],
                                                wo_sb[:, ds(pp, 1), :].rearrange("p a d -> p (a d)"), start=True, stop=True)
                last.then_inc(y_mm, 1)

            def context_turn(b):
                pe.wait_ge(tok_in, 32 * (b + 1))
                for g, kts in enumerate(GROUPS):
                    for i, kt in enumerate(kts):
                        w = width(kt)
                        last = nc.tensor.transpose(S[:, g, i * P:i * P + w], tok[0:w, kt, :], identf[0:w, 0:w])
                    last.then_inc(ct_mm, 1)

            def layer1_kv(b, i):
                if i == 2 or i > 3:
                    pe.wait_ge(kv_ev, b * len(KVG) + (i if i > 3 else 1))
                for n, kt in enumerate(KVG[i]):
                    w = width(kt)
                    last = nc.tensor.matmul(kv_banks[i][0:w, n * 2 * D:(n + 1) * 2 * D], cT[:, kt * P:kt * P + w],
                                            wkv[:], start=True, stop=True)
                last.then_inc(kv_mm, 1)

            def first_scores(b):
                pe.wait_ge(ct_lo, b + 1)
                pe.wait_ge(q_lo, b * NP0 + 1)
                for c in range(NCH):
                    scores(c, 0, 0)

            EARLY = KT // 2 + 2

            def batch(b, last_batch):
                def pair(p, slot, has_prev, has_next):
                    prev = 1 - slot
                    for k in range(UNITS):
                        u = (b * NP0 + p) * UNITS + k
                        more = has_next or k < UNITS - 1
                        nslot, nu = (slot, k + 1) if k < UNITS - 1 else (prev, 0)

                        def next_scores(c):
                            if more:
                                pe.wait_ge(ex, u * NCH + c + 1)
                                scores(c, nslot, nu)

                        def turn(g):
                            pe.wait_ge(ex, u * NCH + min(NCH, (GROUPS[g][-1] * P + P - 1) // CH + 1))
                            if not has_prev and k == 0 and g < 2:
                                pe.wait_ge(kv_ev, b * len(KVG) + (3, 2)[g])
                            if g >= 2:
                                pe.wait_ge((t_dve, t_act)[g % 2], 1 + u * 2 + 1)
                            else:
                                pe.wait_ge((t_dve, t_act)[g % 2], 1 + u * 2)
                            for i, kt in enumerate(GROUPS[g]):
                                w = width(kt)
                                last = nc.tensor.transpose(tb[g % 2][0:w, i * P:(i + 1) * P],
                                                           prob[:, k % 2, kt * P:kt * P + w], identf[:])
                            last.then_inc(t_mm, 1)

                        if k == UNITS - 1 and more:
                            pe.wait_ge(q_lo, b * NP0 + p + 2)
                        next_scores(0)
                        next_scores(1)
                        turn(0)
                        if k == 0 and has_next:
                            make_q(b, p + 1, prev, b * NP0 + p - 1 if has_prev else b * NP0)
                        if k == 1:
                            make_v(b, p, 1, slot)
                        if k == 2:
                            make_v(b, p, 3, slot)
                        next_scores(2)
                        turn(1)
                        next_scores(3)
                        for where in range(3):
                            if has_prev and VALUES_AT.get(k) == where:
                                if k == 0:
                                    pe.wait_ge(t_act, 1 + u * 2)
                                    pe.wait_ge(t_dve, 1 + u * 2)
                                    pe.wait_ge(v_act, (b * NP0 + p) * 2)
                                    pe.wait_ge(v_dve, (b * NP0 + p) * 2)
                                    pe.wait_ge(o_ev, 1 + 2 * (b * NP0 + p - 1))
                                    pe.wait_ge(kv_ev, (b + 1) * len(KVG))
                                values(prev, VALUES_TILES[k])
                            if not has_prev and where == 2:
                                for i in KV_BESIDE[k]:
                                    layer1_kv(b, i)
                            if k == 0 and where == 2:
                                make_v(b, p, 0, slot, has_next)
                            if k == 1 and where == 2:
                                make_v(b, p, 2, slot)
                            if k == 3 and has_prev and where == 2:
                                pe.wait_ge(v_dve, (b * NP0 + p) * 2 + 2)
                                project(b, p - 1)
                            if where < 2:
                                turn(2 + where)

                walk(pe, pair)
                end = (b + 1) * NP0
                pe.wait_ge(t_act, 1 + end * UNITS * 2)
                pe.wait_ge(t_dve, 1 + end * UNITS * 2)
                pe.wait_ge(o_ev, 1 + 2 * (end - 1))
                if not last_batch:
                    pe.wait_ge(ex, end * UNITS * NCH)
                    context_turn(b + 1)
                    make_q(b + 1, 0, 0, end - 1)
                values(1, list(range(EARLY)))
                if not last_batch:
                    first_scores(b + 1)
                values(1, list(range(EARLY, KT)))
                if not last_batch:
                    layer1_kv(b + 1, 0)
                    layer1_kv(b + 1, 1)
                else:
                    pe.wait_ge(y_add, 1 + end - 1)
                project(b, NP0 - 1)
                if not last_batch:
                    layer1_kv(b + 1, 2)

            context_turn(0)
            make_q(0, 0, 0, 0)
            pe.wait_ge(ct_ev, NG)
            layer1_kv(0, 0)
            layer1_kv(0, 1)
            layer1_kv(0, 2)
            first_scores(0)
            with pe.Fori(0, B - 1) as b:
                batch(b, False)
            batch(B - 1, True)

        @block.scalar
        def _(act):
            act.sem_inc(t_act, 1)
            act.sem_inc(o_ev, 1)
            setup_scalar(act)
            act.preload_act_table(ACT.Exp)

            def q_high(n, slot):
                act.wait_ge(q_mm, 1 + n + 1)
                nc.scalar.copy(qh[:, slot, :, :], pX[:].rearrange("p (h q) -> p h q", h=2)).then_inc(q_hi, 1)

            def exps(u, k, slot, chunks):
                for c in chunks:
                    if c == 0:
                        act.wait_ge(mx, u + 1)
                    lo = CSKIP[c]
                    nc.scalar.activation(prob[:, k % 2, c * CH:c * CH + CH - lo], S[:, c, lo:CH], ACT.Exp,
                                         bias=negm[:, k % 2:k % 2 + 1],
                                         accum_out=dens[:, slot, k, c:c + 1]).then_inc(ex, 1)

            def t_copy(g, u, k, slot):
                act.wait_ge(t_mm, u * NG + g + 1)
                h, qt = k // QT, k % QT
                n, w = len(GROUPS[g]), width(GROUPS[g][-1])
                nc.scalar.copy(pT[slot][h][0:w, GROUPS[g][0]:GROUPS[g][-1] + 1, qt * P:(qt + 1) * P],
                               tb[g % 2][0:w, 0:n * P].rearrange("p (n q) -> p n q", n=n)).then_inc(t_act, 1)

            def v_copy(n, g, slot):
                act.wait_ge(v_mm, n * NG + g + 1)
                nc.scalar.copy(V[:, slot, GROUPS[g][0]:GROUPS[g][-1] + 1, :],
                               pX[:].rearrange("p (n e) -> p n e", n=TG)).then_inc(v_act, 1)

            def o_copy(n):
                act.wait_ge(o_mm, n + 1)
                act.wait_ge(y_mm, 1 + n)
                act.wait_ge(zeroed, 1)
                for h in range(2):
                    r = slice(h * HD0, (h + 1) * HD0)
                    nc.scalar.copy(OA[r, h, :], pO[r, 0:LQ]).then_inc(o_ev, 1)

            def context_copy(b):
                for g, kts in enumerate(GROUPS):
                    act.wait_ge(ct_mm, 1 + b * NG + g + 1)
                    n = (len(kts) - 1) * P + width(kts[-1])
                    nc.scalar.copy(cT[:, kts[0] * P:kts[0] * P + n], S[:, g, 0:n]).then_inc(ct_ev, 1)

            def kv_copy(b, i):
                if i == 0:
                    act.wait_ge(kv_out, 1 + 16 * b)
                kts = KVG[i]
                act.wait_ge(kv_mm, b * len(KVG) + i + 1)
                w, n = width(kts[-1]), len(kts)
                nc.scalar.copy(kv[0:w, kts[0]:kts[0] + n, :],
                               kv_banks[i][0:w, 0:n * 2 * D].rearrange("p (n d) -> p n d", n=n)).then_inc(kv_ev, 1)

            def batch(b, last_batch):
                def pair(p, slot, has_prev, has_next):
                    prev = 1 - slot
                    n = b * NP0 + p
                    for k in range(UNITS):
                        u = n * UNITS + k
                        more = has_next or k < UNITS - 1
                        nk, nslot = (k + 1, slot) if k < UNITS - 1 else (0, prev)
                        if k == 0 and has_next:
                            q_high(n + 1, prev)
                        t_copy(1, u, k, slot)
                        if more:
                            exps(u + 1, nk, nslot, [0, 1])
                        t_copy(3, u, k, slot)
                        if more:
                            exps(u + 1, nk, nslot, [2])
                        if k == 0:
                            v_copy(n, 0, slot)
                        if k == 1:
                            v_copy(n, 2, slot)
                        if not has_prev:
                            for i in KV_BESIDE[k]:
                                kv_copy(b, i)
                        if k == 2 and has_prev:
                            o_copy(n - 1)
                        if more:
                            exps(u + 1, nk, nslot, [3])
                walk(act, pair)
                if not last_batch:
                    context_copy(b + 1)
                    q_high((b + 1) * NP0, 0)
                    exps((b + 1) * NU, 0, 0, range(NCH))
                    kv_copy(b + 1, 0)
                o_copy((b + 1) * NP0 - 1)
                if not last_batch:
                    kv_copy(b + 1, 1)
                    kv_copy(b + 1, 2)

            act.wait_ge(padded, 1)
            context_copy(0)
            q_high(0, 0)
            kv_copy(0, 0)
            kv_copy(0, 1)
            kv_copy(0, 2)
            exps(0, 0, 0, range(NCH))
            with act.Fori(0, B - 1) as b:
                batch(b, False)
            batch(B - 1, True)

        @block.vector
        def _(dve):
            dve.sem_inc(t_dve, 1)
            dve.sem_inc(y_add, 1)
            setup_vector(dve)
            nc.vector.memset(OA[:], 0.0).then_inc(zeroed, 1)

            def q_low(n, slot):
                dve.wait_ge(q_hi, n + 1)
                nc.vector.tensor_tensor(ql[:, slot, :, :], pX[:].rearrange("p (h q) -> p h q", h=2),
                                        qh[:, slot, :, :].bitcast(F32), ALU.subtract).then_inc(q_lo, 1)

            def maxima(u, k, chunks):
                for c in chunks:
                    dve.wait_ge(s_mm, u * NCH + c + 1)
                    nc.vector.reduce_max(mx4[:, k % 2, c:c + 1], S[:, c, 0:CH], AX.X).then_inc(mx_c, 1)
                if chunks[-1] == NCH - 1:
                    dve.wait_ge(mx_c, (u + 1) * NCH)
                    nc.vector.tensor_reduce(negm[:, k % 2:k % 2 + 1], mx4[:, k % 2, :], AX.X, ALU.max,
                                            negate=True).then_inc(mx, 1)

            def t_copy(g, u, k, slot):
                dve.wait_ge(t_mm, u * NG + g + 1)
                h, qt = k // QT, k % QT
                nc.vector.tensor_copy(pT[slot][h][:, GROUPS[g][0]:GROUPS[g][-1] + 1, qt * P:(qt + 1) * P],
                                      tb[g % 2][:].rearrange("p (n q) -> p n q", n=TG)).then_inc(t_dve, 1)

            def v_copy(n, g, slot):
                dve.wait_ge(v_mm, n * NG + g + 1)
                w, m = width(GROUPS[g][-1]), len(GROUPS[g])
                nc.vector.tensor_copy(V[0:w, slot, GROUPS[g][0]:GROUPS[g][-1] + 1, :],
                                      pX[0:w, 0:m * P].rearrange("p (n e) -> p n e", n=m)).then_inc(v_dve, 1)

            def sums(n, slot):
                nc.vector.tensor_reduce(den[:, slot, :], dens[:, slot, :, :], AX.X, ALU.add).then_inc(den_s, 1)
                dve.wait_ge(den_s, n + 1)
                nc.vector.reciprocal(rden[:, slot, :], den[:, slot, :]).then_inc(den_r, 1)

            def add(b, n, slot):
                dve.wait_ge(y_mm, 1 + n + 1)
                dve.wait_ge(den_r, n + 1)
                for h in range(2):
                    if h:
                        dve.wait_ge(added, n + 1)
                    for qt in range(QT):
                        i = h * QT + qt
                        xt = xs[:, ds((b * QT + qt) * D, D)]
                        last = nc.vector.scalar_tensor_tensor(xt, pX[:, i * D:(i + 1) * D], rden[:, slot, i:i + 1], xt,
                                                              ALU.mult, ALU.add)
                    if h == 0:
                        last.then_inc(added, 1)
                last.then_inc(y_add, 1)

            def open_batch(b):
                dve.wait_ge(ct_ev, (b + 1) * NG)
                nc.vector.tensor_copy(cTh[:, 0:LK], cT[:, 0:LK]).then_inc(ct_hi, 1)
                dve.wait_ge(ct_hi, b + 1)
                nc.vector.tensor_tensor(cTl[:, 0:LK], cT[:, 0:LK], cTh[:, 0:LK].bitcast(F32), ALU.subtract).then_inc(ct_lo, 1)
                q_low(b * NP0, 0)
                maxima(b * NU, 0, range(NCH))

            def batch(b, last_batch):
                def pair(p, slot, has_prev, has_next):
                    prev = 1 - slot
                    n = b * NP0 + p
                    for k in range(UNITS):
                        u = n * UNITS + k
                        more = has_next or k < UNITS - 1
                        if more:
                            maxima(u + 1, k + 1, [0, 1])
                        t_copy(0, u, k, slot)
                        if k == 0 and has_next:
                            q_low(n + 1, prev)
                        if k == 1:
                            v_copy(n, 1, slot)
                        if k == 2:
                            v_copy(n, 3, slot)
                        if more:
                            maxima(u + 1, k + 1, [2, 3])
                        t_copy(2, u, k, slot)
                        if k == 0 and has_prev:
                            dve.wait_ge(ex, n * UNITS * NCH)
                            sums(n - 1, prev)
                        if k == 3 and has_prev:
                            add(b, n - 1, prev)

                walk(dve, pair)
                last = (b + 1) * NP0
                if not last_batch:
                    open_batch(b + 1)
                dve.wait_ge(ex, last * UNITS * NCH)
                sums(last - 1, 1)
                add(b, last - 1, 1)

            open_batch(0)
            setup_vector_masks(dve)
            with dve.Fori(0, B - 1) as b:
                batch(b, False)
            batch(B - 1, True)



def normed_projection(nc, ctx, name, xs, g, beta, w, b, rope, identf, q_hi, q_lo, kv_all, turn_banks, out_banks, eps=1e-5):
    NT = B * QT
    n = len(w)

    def sb(nm, shape, dt=F32):
        return ctx.enter_context(nc.sbuf_tensor(f"{name}_{nm}", shape, dt))

    def sem(nm):
        return ctx.enter_context(nc.semaphore(f"{name}_{nm}"))

    wsb = sb("w", [P, n * D])
    bsb = sb("b", [P, n * D])
    gcol, bcol, eps_c = sb("g", [P, 1]), sb("beta", [P, 1]), sb("eps", [P, 1])
    tabs = sb("tabs", [P, 4, QT * D])
    stats, mv = sb("stats", [P, NT, 6]), sb("mv", [P, NT, 2])
    std, rstd = sb("std", [P, NT]), sb("rstd", [P, NT])
    xh = sb("xh", [P, NT * D])
    hT = sb("hT", [P, NT * D])
    qs = sb("qs", [P, NT * D])
    rot = sb("rot", [P, NT * D])
    rotk = sb("rotk", [P, NT * D]) if n > 1 else None
    w_in, st, ag, sd, rs, xn = sem("w_in"), sem("st"), sem("ag"), sem("sd"), sem("rs"), sem("xn")
    t_mm, t_ev, p_mm, p_ev = sem("t_mm"), sem("t_ev"), sem("p_mm"), sem("p_ev")
    r1, r2, r3, q_ready, k1, k2, k_ready = sem("r1"), sem("r2"), sem("r3"), sem("q_ready"), sem("k1"), sem("k2"), sem("k_ready")
    loads = 16 * (2 * n + 2 + 1)
    NOUT = len(out_banks)

    def load(sp):
        for i in range(n):
            sp.dma_start(wsb[:, i * D:(i + 1) * D], w[i]).then_inc(w_in, 16)
            sp.dma_start(bsb[:, i * D:(i + 1) * D], row_everywhere(b[i])).then_inc(w_in, 16)
        sp.dma_start(gcol[:], g.rearrange("(p o) -> p o", o=1)).then_inc(w_in, 16)
        sp.dma_start(bcol[:], beta.rearrange("(p o) -> p o", o=1)).then_inc(w_in, 16)
        sp.dma_start(tabs[:], rope).then_inc(w_in, 16)

    def vector(dve):
        nc.vector.memset(eps_c[:], eps)
        for t in range(NT):
            last = nc.vector.bn_stats(stats[:, t, :], xs[:, t * D:(t + 1) * D])
        last.then_inc(st, 1)
        dve.wait_ge(st, 1)
        for t in range(NT):
            last = nc.vector.bn_aggr(mv[:, t, :], stats[:, t, :])
        last.then_inc(ag, 1)
        dve.wait_ge(sd, 1)
        nc.vector.reciprocal(rstd[:], std[:]).then_inc(rs, 1)
        dve.wait_ge(rs, 1)
        for t in range(NT):
            nc.vector.tensor_scalar(xh[:, t * D:(t + 1) * D], xs[:, t * D:(t + 1) * D], mv[:, t, 0:1],
                                    rstd[:, t:t + 1], ALU.subtract, ALU.mult).then_inc(xn, 1)
        dve.wait_ge(w_in, loads)
        for t in range(NT):
            dve.wait_ge(p_mm, t + 1)
            bank = out_banks[t % NOUT]
            last = nc.vector.tensor_tensor(qs[:, t * D:(t + 1) * D], bank[:, 0:D], bsb[:, 0:D], ALU.add)
            if n > 1:
                last = nc.vector.tensor_tensor(kv_all[:, t, :], bank[:, D:3 * D], bsb[:, D:3 * D], ALU.add)
            last.then_inc(p_ev, 1)
        dve.wait_ge(p_ev, NT)
        half = HD1 // 2
        for part, (b0, b1) in enumerate(((0, 1), (1, B))):
            n_b = b1 - b0
            cols = slice(b0 * QT * D, b1 * QT * D)
            src = qs[:, cols].rearrange("p (b m e) -> p b m e", b=n_b, e=HD1)
            dst = rot[:, cols].rearrange("p (b m e) -> p b m e", b=n_b, e=HD1)
            tab = tabs[:, 1, :].rearrange("p (m e) -> p m e", e=HD1).unsqueeze(1).broadcast_to([P, n_b, QT * H1, HD1])
            for lo, hi in ((0, half), (half, 0)):
                last = nc.vector.tensor_tensor(dst[:, :, :, lo:lo + half], src[:, :, :, hi:hi + half],
                                               tab[:, :, :, lo:lo + half], ALU.mult)
            last.then_inc(r1, 1)
            dve.wait_ge(r1, part + 1)
            qb = qs[:, cols].rearrange("p (b m) -> p b m", b=n_b)
            nc.vector.tensor_tensor(qb, qb, tabs[:, 0, :].unsqueeze(1).broadcast_to([P, n_b, QT * D]), ALU.mult).then_inc(r2, 1)
            dve.wait_ge(r2, part + 1)
            nc.vector.tensor_tensor(qs[:, cols], qs[:, cols], rot[:, cols], ALU.add).then_inc(r3, 1)
            dve.wait_ge(r3, part + 1)
            nc.vector.tensor_copy(q_hi[:, cols], qs[:, cols]).then_inc(q_ready, 1)
            dve.wait_ge(q_ready, 2 * part + 1)
            nc.vector.tensor_tensor(q_lo[:, cols], qs[:, cols], q_hi[:, cols].bitcast(F32), ALU.subtract).then_inc(q_ready, 1)

    def gpsimd(pool):
        pool.wait_ge(p_ev, NT)
        half = HD1 // 2
        keys = kv_all[:, :, 0:D].rearrange("p (b t) (h e) -> p b t h e", b=B, e=HD1)
        dst = rotk[:].rearrange("p (b t h e) -> p b t h e", b=B, t=QT, e=HD1)
        for t in range(QT):
            for lo, hi in ((0, half), (half, 0)):
                tab = tabs[:, 3, t * D:(t + 1) * D].rearrange("p (h e) -> p h e", e=HD1)
                last = nc.gpsimd.tensor_tensor(dst[:, :, t, :, lo:lo + half], keys[:, :, t, :, hi:hi + half],
                                               tab[:, :, lo:lo + half].unsqueeze(1).broadcast_to([P, B, H1, half]), ALU.mult)
        last.then_inc(k1, 1)
        pool.wait_ge(k1, 1)
        for t in range(QT):
            kk = kv_all[:, :, 0:D].rearrange("p (b t) d -> p b t d", b=B)[:, :, t, :]
            last = nc.gpsimd.tensor_tensor(kk, kk, tabs[:, 2, t * D:(t + 1) * D].unsqueeze(1).broadcast_to([P, B, D]), ALU.mult)
        last.then_inc(k2, 1)
        pool.wait_ge(k2, 1)
        nc.gpsimd.tensor_tensor(kv_all[:, :, 0:D], kv_all[:, :, 0:D], rotk[:].rearrange("p (t d) -> p t d", d=D), ALU.add).then_inc(k_ready, 1)

    def scalar(act):
        act.wait_ge(ag, 1)
        nc.scalar.activation(std[:], mv[:, :, 1], ACT.Sqrt, bias=eps_c[:]).then_inc(sd, 1)
        act.wait_ge(w_in, loads)
        for q in range(NT // 4):
            act.wait_ge(t_mm, q + 1)
            nc.scalar.activation(hT[:, q * 512:(q + 1) * 512], turn_banks[q], ACT.Identity, bias=bcol[:],
                                 scale=gcol[:]).then_inc(t_ev, 1)

    def tensor_turns(pe):
        for t in range(NT):
            pe.wait_ge(xn, t + 1)
            last = nc.tensor.transpose(turn_banks[t // 4][:, (t % 4) * D:(t % 4 + 1) * D], xh[:, t * D:(t + 1) * D], identf[:])
            if t % 4 == 3:
                last.then_inc(t_mm, 1)

    def tensor_products(pe):
        pe.wait_ge(w_in, loads)
        for t in range(NT):
            pe.wait_ge(t_ev, t // 4 + 1)
            if t >= NOUT:
                pe.wait_ge(p_ev, t - NOUT + 1)
            nc.tensor.matmul(out_banks[t % NOUT][:, 0:n * D], hT[:, t * D:(t + 1) * D], wsb[:], start=True, stop=True).then_inc(p_mm, 1)

    return (load, vector, gpsimd, scalar, tensor_turns, tensor_products), (q_ready, k_ready, p_ev)


def layer1_attention(nc, name, xs, norm, w, b, q_hi, q_lo, kv_all, kv_dram, wo, bo, nkt, last_w, causal, consts, identf, identb, maskq, maskk):
    NK = nkt
    LKC = (NK - 1) * P + last_w
    S1 = B * G1
    chunks = 1 if causal else NCH
    RING = 4

    def kw(kt):
        return last_w if kt == NK - 1 else P

    with ExitStack() as ctx:
        def sb(nm, shape, dt=F32):
            return ctx.enter_context(nc.sbuf_tensor(f"{name}_{nm}", shape, dt))

        def sem(nm):
            return ctx.enter_context(nc.semaphore(f"{name}_{nm}"))

        wo_sb, bo_sb = sb("wo", [P, D]), sb("bo", [P, D])
        hmask = sb("hmask", [P, HG])
        kvb = None if causal else sb("kvb", [P, NK, 2 * D])
        ksrc = sb("ksrc", [P, NK, 4, R])
        qsrc = sb("qsrc", [P, QT, 4, R])
        kraw = sb("kraw", [P, NK, R]) if causal else None
        KX = sb("KX", [P, G1, NK * P], F32R)
        QX = sb("QX", [P, H1, LQ], F32R)
        V = sb("V", [P, G1, NK, HG, 32])
        pT = sb("pT", [P, RING, HG * LQ])
        mxc = sb("mxc", [P, 2, QT, HG, NCH])
        negm = sb("negm", [P, 2, QT, HG])
        OT = sb("OT", [P, LQ])
        rden = sb("rden", [P, 2, QT, HG])
        A = sb("A", [P, QT, D])
        AT = sb("AT", [P, LQ])
        st = [ctx.enter_context(nc.psum_tensor(f"{name}_st{i}", [P, 1024], F32)) for i in range(2)]
        mb = [ctx.enter_context(nc.psum_tensor(f"{name}_mb{i}", [P, 512], F32)) for i in range(2)]
        pO = ctx.enter_context(nc.psum_tensor(f"{name}_pO", [P, 512], F32))
        pX = ctx.enter_context(nc.psum_tensor(f"{name}_pX", [P, 512], F32))
        pY = st[1][:, 512:1024] if causal else pX

        (project_load, project_vector, project_gpsimd, project_scalar, project_turns, project_products), (
            q_ready, k_ready, projected) = normed_projection(
                nc, ctx, name, xs, *norm, w, b, consts["rope"], identf, q_hi, q_lo, kv_all,
                [st[0][:, 0:512], st[0][:, 512:1024], st[1][:, 0:512], st[1][:, 512:1024]], [mb[0], mb[1], pO])
        c_in, kv_in, fixed = sem("c_in"), sem("kv_in"), sem("fixed")
        khi_done, src_done, qsrc_done = sem("khi_done"), sem("src_done"), sem("qsrc_done")
        v_done = sem("v_done")
        x_mm, x_ev = sem("x_mm"), sem("x_ev")
        y_mm, y_ev = sem("y_mm"), sem("y_ev")
        c_mm, c_red = sem("c_mm"), sem("c_red")
        m_done = sem("m_done")
        qx_dve = sem("qx_dve")
        s_mm, ex, pv = sem("s_mm"), sem("ex"), sem("pv")
        o_ev, rd, biased = sem("o_ev"), sem("rd"), sem("biased")
        block = ctx.enter_context(nc.Block())

        groups = [list(range(t, min(t + TG, NK))) for t in range(0, NK, TG)]
        NXG = len(groups)
        PREP = NXG + 1
        NC = HG * QT * chunks if not causal else HG

        def turned(t, what):
            i = NXG if what == "q" else what
            if isinstance(t, tuple):
                return t[0] * PREP + (t[1] * PREP + i + 1)
            return t * PREP + i + 1

        def output(b, g, i):
            return b * (G1 + 2) + (g + i + 1)

        def before_turned(t, what):
            i = NXG if what == "q" else what
            return t[0] * PREP + (t[1] * PREP + i) if isinstance(t, tuple) else t * PREP + i

        QUERY_KT = 9
        ACT_HEADS = HG if causal else HG // 2
        if causal:
            ktask, kcopy = {(0, 0): 0, (0, 1): "q"}, {0: [(0, "all")], 1: [("q", range(HG))]}
        else:
            ktask, kcopy = {(1, 2): 0, (3, 2): 1, (5, 2): 2, (7, 2): 3, (QUERY_KT, 2): "q"}, {NK - 1: [("q", [0, 1])]}
            for i in range(NXG):
                kcopy[2 * i + 2], kcopy[2 * i + 3] = [(i, "first")], [(i, "last")]

        TURN = 1 if causal else 2
        NI = NC + 1

        def item(t, m):
            if isinstance(t, tuple):
                return t[0] * NI + (t[1] * NI - 1 + m + 1)
            return t * NI + m + 1 - (1 if t else 0)

        def item_bank(t, g, m):
            if isinstance(t, int):
                return st[m // 2 % 2][:, m % 2 * 512:(m % 2 + 1) * 512]
            return mb[(g * NI + m + 1) % 2]

        def item_before(t, m):
            return item(t, m - (4 if isinstance(t, int) else 2))

        places = [[[], [], []] for _ in range(NK)]
        if causal:
            places = [[[0, 1], [2], [3]], [[], [4], []]]
        else:
            full = (2, 3, 5, 7, 9, 11, 12)
            left = iter(range(NI))
            for kt in range(NK):
                for place in range(3 if kt in full else 2):
                    places[kt][place].append(next(left))
            assert next(left, None) is None
        def steps(eng, step):
            step(0, 0, True, "all", True, False)
            with eng.Fori(0, B - 1) as b:
                for g in range(1, G1):
                    step(b, g, True, "all", True, False)
                step(b + 1, 0, True, "all", True, True)
            for g in range(1, G1):
                step(B - 1, g, g < G1 - 1, "all" if g < G1 - 2 else "turn" if g == G1 - 2 else "none", False, False)

        def count(t, more=0):
            return t[0] + (t[1] + more) if isinstance(t, tuple) else t + more

        @block.sync
        def _(sp):
            project_load(sp)
            sp.dma_start(wo_sb[:], wo).then_inc(c_in, 16)
            sp.dma_start(bo_sb[:], row_everywhere(bo)).then_inc(c_in, 16)
            sp.dma_start(hmask[:], consts["hmask"]).then_inc(c_in, 16)
            if not causal:
                with sp.Fori(0, B) as b:
                    sp.wait_ge(v_done, 1 + b * G1)
                    sp.wait_ge(src_done, 1 + b * G1)
                    sp.dma_start(kvb[:].rearrange("p t n -> p (t n)"),
                                 kv_dram[ds(b, 1)].rearrange("b p n -> p (b n)")).then_inc(kv_in, 16)

        @block.gpsimd
        def _(pool):
            pool.sem_inc(v_done, 1)
            pool.sem_inc(src_done, 1)
            nc.gpsimd.memset(qsrc[:, :, 3, :], 0.0)
            nc.gpsimd.memset(ksrc[:, :, 3, :], 1.0).then_inc(fixed, 1)
            hi = ksrc[:].bitcast(F32R)

            def beside_values():
                for g in range(G1):
                    last = nc.gpsimd.memset(V[:, g, :, :, HD1:32], 0.0)
                last.then_inc(fixed, 1)
                pool.wait_ge(fixed, 2)
                for g in range(G1):
                    last = nc.gpsimd.memset(V[:, g, :, :, HD1:HD1 + 1], 1.0)
                last.then_inc(fixed, 1)

            if causal:
                beside_values()
                project_gpsimd(pool)
                pool.wait_ge(k_ready, 1)

            def query(b, g, blk, part):
                return nc.gpsimd.tensor_copy(qsrc[:, :, blk, :], part[:, ds(b * QT * D, QT * D)].bitcast(F32)
                                             .rearrange("p (t d) -> p t d", d=D)[:, :, g * R:(g + 1) * R])

            def key_value(b, g):
                k, v = slice(g * R, (g + 1) * R), slice(D + g * R, D + (g + 1) * R)
                if causal:
                    return kv_all[:, ds(b * QT, NK), k], kv_all[:, ds(b * QT, NK), v]
                return kvb[:, :, k], kvb[:, :, v]

            def key_high(k):
                if causal:
                    nc.gpsimd.tensor_copy(kraw[:], k)
                nc.gpsimd.tensor_copy(hi[:, :, 0:2, :], k.unsqueeze(2).broadcast_to([P, NK, 2, R])).then_inc(khi_done, 1)

            def key_low(k, t):
                pool.wait_ge(khi_done, t + 1)
                nc.gpsimd.tensor_tensor(ksrc[:, :, 2, :], kraw[:] if causal else k, ksrc[:, :, 0, :], ALU.subtract).then_inc(src_done, 1)

            def value_copy(g, v):
                nc.gpsimd.tensor_copy(V[:, g, :, :, 0:HD1], v.rearrange("p t (j e) -> p t j e", e=HD1)).then_inc(v_done, 1)

            def prepare(b, g):
                t = b * G1 + g
                k, v = key_value(b, g)
                if not causal:
                    pool.wait_ge(kv_in, 16 * (b + 1))
                pool.wait_ge(x_mm, t * PREP)
                query(b, g, 0, q_hi)
                key_high(k)
                query(b, g, 2, q_hi)
                key_low(k, t)
                if not (isinstance(t, int) and t < G1):
                    pool.wait_ge(pv, 1 + (t - G1 + 1) * NK)
                query(b, g, 1, q_lo).then_inc(qsrc_done, 1)
                value_copy(g, v)

            if not causal:
                pool.wait_ge(kv_in, 16)
            for t in range(3):
                if t:
                    pool.wait_ge(x_mm, turned(t - 1, NXG - 1))
                k, _ = key_value(0, t)
                key_high(k)
                key_low(k, t)
                pool.wait_ge(q_ready, 2)
                if t:
                    pool.wait_ge(x_mm, turned(t - 1, "q"))
                query(0, t, 0, q_hi)
                query(0, t, 2, q_hi)
                query(0, t, 1, q_lo).then_inc(qsrc_done, 1)
            for g in range(3):
                value_copy(g, key_value(0, g)[1])
            if not causal:
                beside_values()
            pool.wait_ge(q_ready, 4)

            def step(b, g, has_next, items, has_prep, has_output):
                if has_prep and g == 0:
                    prepare(b, G1 - 1)
                elif has_prep:
                    prepare(b + 1, g - 1)
            steps(pool, step)

        @block.tensor
        def _(pe):
            pe.sem_inc(pv, 1)
            pe.wait_ge(c_in, 48)

            def turn(t, what):
                if not (isinstance(t, int) and t == 0 and what == 0):
                    pe.wait_ge(x_ev, before_turned(t, what))
                if what == 0:
                    pe.wait_ge(src_done, 1 + count(t, 1))
                if what == "q":
                    pe.wait_ge(qsrc_done, count(t, 1))
                    for qt in range(QT):
                        last = nc.tensor.transpose(pX[:, qt * P:(qt + 1) * P], qsrc[:, qt, :, :].rearrange("p a r -> p (a r)"), identf[:])
                else:
                    for i, kt in enumerate(groups[what]):
                        w = kw(kt)
                        last = nc.tensor.transpose(pX[:, i * P:i * P + w], ksrc[0:w, kt, :, :].rearrange("p a r -> p (a r)"),
                                                   identf[0:w, 0:w])
                last.then_inc(x_mm, 1)

            def stream_item(t, g, m, first=False, only=False):
                bank = item_bank(t, g, m)
                if only or not first and m == TURN:
                    if causal:
                        pe.wait_ge(c_red, item(t, -1))
                    else:
                        pe.wait_ge(m_done, count(t))
                        pe.wait_ge(c_red, item_before(t, m))
                    for qt in range(QT):
                        last = nc.tensor.transpose(bank[0:HG, qt * P:(qt + 1) * P], negm[:, (g + 1) % 2, qt, :], identf[:])
                    last.then_inc(c_mm, 1)
                    return
                if m >= 4 or not first:
                    pe.wait_ge(c_red, item_before(t, m))
                n = m if first or m < TURN else m - 1
                if causal:
                    for qt in range(QT):
                        nc.tensor.matmul(bank[:, qt * LQ:(qt + 1) * LQ], QX[:, HG * g + n, qt * P:(qt + 1) * P], KX[:, g, 0:LQ],
                                         start=True, stop=False)
                        last = nc.tensor.matmul(bank[:, qt * LQ:(qt + 1) * LQ], identb[:], maskq[:, qt * LQ:(qt + 1) * LQ],
                                                start=False, stop=True)
                else:
                    j, qt, c = n // (QT * NCH), n // NCH % QT, n % NCH
                    last = nc.tensor.matmul(bank[:, 0:CH], QX[:, HG * g + j, qt * P:(qt + 1) * P],
                                            KX[:, g, CSTART[c]:CSTART[c] + CH], start=True, stop=True)
                last.then_inc(c_mm, 1)

            def key_scores(s, g, kt):
                i = g * NK + kt
                w = kw(kt)
                k = KX[:, g, kt * P:kt * P + w]
                out = st[i % 2]
                if causal and kt == 1:
                    nc.tensor.matmul(out[0:w, 0:HG * P].rearrange("p (j q) -> p j q", j=HG), k,
                                     QX[:, HG * g:HG * (g + 1), P:LQ], start=True, stop=False)
                    for j in range(HG):
                        last = nc.tensor.matmul(out[:, j * P:(j + 1) * P], identb[:], maskk[:], start=False, stop=j == HG - 1)
                else:
                    for h2 in range(2):
                        last = nc.tensor.matmul(out[0:w, h2 * 512:(h2 + 1) * 512], k,
                                                QX[:, HG * g + 2 * h2:HG * g + 2 * h2 + 2, :].rearrange("p h q -> p (h q)"),
                                                start=True, stop=not causal)
                        if causal:
                            for j in range(2):
                                at = h2 * 512 + j * LQ
                                last = nc.tensor.matmul(out[:, at:at + P], identb[:], maskk[:], start=False, stop=j == 1)
                last.then_inc(s_mm, 1)

            def values(s, g, kt):
                i = g * NK + kt
                w = kw(kt)
                lo, n = (P, P) if causal and kt == 1 else (0, LQ)
                for j in range(HG):
                    last = nc.tensor.matmul(pO[32 * j:32 * j + 32, lo:LQ], V[0:w, g, kt, j, :],
                                            pT[0:w, i % RING, j * n:(j + 1) * n], start=kt == 0, stop=kt == NK - 1)
                last.then_inc(pv, 1)

            beside = {NC * (i + 1) // (NXG + 2): i for i in range(NXG)} | {NC * (NXG + 1) // (NXG + 2): "q"}

            project_turns(pe)
            pe.wait_ge(fixed, 1)
            project_products(pe)
            for what in [*range(NXG), "q"]:
                turn(0, what)
            for t in range(2):
                pe.wait_ge(x_ev, (t + 1) * PREP)
                for m in range(NC if t == 0 else NI):
                    stream_item(t, t, m, t == 0)
                    if m in beside:
                        turn(t + 1, beside[m])
            pe.wait_ge(x_ev, 3 * PREP)
            pe.wait_ge(projected, B * QT)
            pe.wait_ge(fixed, 3)
            pe.wait_ge(c_red, item(1, NI - 1))
            key_scores(0, 0, 0)
            key_scores(0, 0, 1)

            def turn_output(before):
                pe.wait_ge(y_ev, before)
                for qt in range(QT):
                    last = nc.tensor.transpose(pY[:, qt * P:(qt + 1) * P], A[:, qt, :], identf[:])
                last.then_inc(y_mm, 1)

            def project_output(before):
                pe.wait_ge(y_ev, before)
                for qt in range(QT):
                    last = nc.tensor.matmul(pY[:, qt * D:(qt + 1) * D], AT[:, qt * P:(qt + 1) * P], wo_sb[:], start=True, stop=True)
                last.then_inc(y_mm, 1)

            def step(b, g, has_next, items, has_prep, has_output):
                s = b * G1 + g
                ng = (g + 1) % G1

                def between(kt, place):
                    for m in places[kt][place]:
                        if items == "turn" and m == TURN:
                            stream_item((s, 2), (g + 2) % G1, 0, only=True)
                        elif items == "all":
                            stream_item((s, 2), (g + 2) % G1, m)
                    if has_prep and (kt, place) in ktask:
                        if not causal and ktask[kt, place] == 0:
                            pe.wait_ge(y_ev, output(b, g, 0))
                        turn((s, 3), ktask[kt, place])

                pe.wait_ge(v_done, 1 + s + 1)
                def next_key_scores(kt):
                    if kt + 2 < NK:
                        key_scores(s, g, kt + 2)
                    elif has_next:
                        if kt + 2 == NK:
                            pe.wait_ge(c_red, item((s, 2), TURN if items == "all" else 0))
                        key_scores(s + 1, ng, kt + 2 - NK)

                for kt in range(NK):
                    scores_first = not causal and kt < NK - 1
                    between(kt, 0)
                    if has_output and kt == 0:
                        turn_output(output(b, 0, -2))
                    if has_output and kt == 1:
                        project_output(output(b, 0, -1))
                    pe.wait_ge(ex, s * NK + kt + 1)
                    if scores_first:
                        next_key_scores(kt)
                        between(kt, 1)
                    if kt == 0:
                        pe.wait_ge(o_ev, 1 + s)
                    values(s, g, kt)
                    if not scores_first:
                        between(kt, 1)
                        next_key_scores(kt)
                    between(kt, 2)
                if not causal:
                    pe.wait_ge(x_ev, turned((s, 3), "q") if has_prep else S1 * PREP)
                    if has_prep:
                        pe.wait_ge(qx_dve, s + 1)
                pe.wait_ge(y_ev, output(b, g, 0))
                pe.wait_ge(o_ev, 1 + s + 1)
                for qt in range(QT):
                    last = nc.tensor.transpose(pY[:, qt * P:(qt + 1) * P], OT[:, qt * P:(qt + 1) * P], identf[:])
                last.then_inc(y_mm, 1)
                if g == G1 - 1 and not has_next:
                    turn_output(output(b, g, 1))
                    project_output(output(b, g, 2))

            steps(pe, step)

        @block.scalar
        def _(act):
            act.sem_inc(o_ev, 1)

            def turned_copy(t, g, what, part):
                act.wait_ge(x_mm, turned(t, what))
                if what == "q":
                    for j in part:
                        last = nc.scalar.activation(QX[:, HG * g + j, :], pX[:, 0:LQ], ACT.Copy, scale=hmask[:, j:j + 1])
                    done = part[-1] == (ACT_HEADS if isinstance(t, tuple) else HG) - 1
                else:
                    kts = groups[what]
                    whole = (len(kts) - 1) * P + kw(kts[-1])
                    half = min(whole, TG * P // 2)
                    lo, hi = {"all": (0, whole), "first": (0, half), "last": (half, whole)}[part]
                    done = part != "first"
                    if hi > lo:
                        last = nc.scalar.copy(KX[:, g, kts[0] * P + lo:kts[0] * P + hi], pX[:, lo:hi])
                    elif done:
                        act.sem_inc(x_ev, 1)
                        return
                if done:
                    last.then_inc(x_ev, 1)

            project_scalar(act)
            act.preload_act_table(ACT.Exp)
            act.wait_ge(c_in, 48)
            for t in range(3):
                for i in range(NXG):
                    turned_copy(t, t, i, "all")
                turned_copy(t, t, "q", range(HG))

            def output_copy(n):
                act.wait_ge(y_mm, n)
                nc.scalar.copy(AT[:], pY[:, 0:LQ]).then_inc(y_ev, 1)

            def step(b, g, has_next, items, has_prep, has_output):
                s = b * G1 + g
                for kt in range(NK):
                    i = g * NK + kt
                    w = kw(kt)
                    act.wait_ge(s_mm, s * NK + kt + 1)
                    n = HG * P if causal and kt == 1 else HG * LQ
                    nc.scalar.activation(pT[0:w, i % RING, 0:n], st[i % 2][0:w, 0:n], ACT.Exp).then_inc(ex, 1)
                    if has_output and kt == 0:
                        output_copy(output(b, 0, -2))
                    if has_prep:
                        for what, part in kcopy.get(kt, ()):
                            if what == "q" and not causal:
                                act.wait_ge(qx_dve, s + 1)
                            turned_copy((s, 3), (g + 3) % G1, what, part)
                act.wait_ge(pv, 1 + (s + 1) * NK)
                nc.scalar.copy(OT[:], pO[:, 0:LQ]).then_inc(o_ev, 1)
                if g == G1 - 1 and not has_next:
                    output_copy(output(b, g, 1))
            steps(act, step)

        @block.vector
        def _(dve):
            dve.sem_inc(y_ev, 1)
            project_vector(dve)
            dve.wait_ge(c_in, 48)
            xt = xs[:].rearrange("p (t d) -> p t d", d=D)
            nc.vector.tensor_tensor(xt, xt, bo_sb[:].unsqueeze(1).broadcast_to([P, B * QT, D]), ALU.add).then_inc(biased, 1)

            def stream_item(t, g, m, first=False, only=False):
                bank = item_bank(t, g, m)
                dve.wait_ge(c_mm, item(t, m))
                if only or not first and m == TURN:
                    rows, pg = slice(3 * R, 3 * R + HG), (g + G1 - 1) % G1
                    nc.vector.tensor_tensor(QX[rows, HG * pg:HG * (pg + 1), :],
                                            bank[0:HG, 0:LQ].unsqueeze(1).broadcast_to([HG, HG, LQ]),
                                            identf[0:HG, 0:HG].unsqueeze(2).broadcast_to([HG, HG, LQ]), ALU.mult).then_inc(c_red, 1)
                    return
                n = m if first or m < TURN else m - 1
                if causal:
                    nc.vector.tensor_reduce(negm[:, g % 2, :, n], bank[:].rearrange("p (a k) -> p a k", a=QT), AX.X, ALU.max,
                                            negate=True).then_inc(c_red, 1)
                else:
                    j, qt, c = n // (QT * NCH), n // NCH % QT, n % NCH
                    nc.vector.reduce_max(mxc[:, g % 2, qt, j, c:c + 1], bank[:, 0:CH], AX.X).then_inc(c_red, 1)
                    if n == NC - 1:
                        dve.wait_ge(c_red, item(t, m))
                        nc.vector.tensor_reduce(negm[:, g % 2], mxc[:, g % 2], AX.X, ALU.max, negate=True).then_inc(m_done, 1)

            for m in range(NC):
                stream_item(0, 0, m, True)
            for m in range(NI):
                stream_item(1, 1, m)

            def add_output(b, n):
                dve.wait_ge(y_mm, n)
                dve.wait_ge(biased, 1)
                xb = xs[:, ds(b * QT * D, QT * D)]
                nc.vector.tensor_tensor(xb, xb, pY[:, 0:QT * D], ALU.add).then_inc(y_ev, 1)

            def step(b, g, has_next, items, has_prep, has_output):
                s = b * G1 + g
                for kt in range(NK):
                    for at, place in enumerate(places[kt]):
                        if has_output and kt == 1 and at == 1:
                            add_output(b - 1, output(b, 0, -1))
                        for m in place:
                            if items == "turn" and m == TURN:
                                stream_item((s, 2), (g + 2) % G1, 0, only=True)
                            elif items == "all":
                                stream_item((s, 2), (g + 2) % G1, m)
                    if has_prep and not causal and kt == QUERY_KT:
                        dve.wait_ge(x_mm, turned((s, 3), "q"))
                        heads = slice(HG * ((g + 3) % G1) + ACT_HEADS, HG * ((g + 3) % G1 + 1))
                        nc.vector.tensor_tensor(QX[:, heads, :], pX[:, 0:LQ].unsqueeze(1).broadcast_to([P, HG - ACT_HEADS, LQ]),
                                                hmask[:, ACT_HEADS:HG].unsqueeze(2).broadcast_to([P, HG - ACT_HEADS, LQ]),
                                                ALU.mult).then_inc(qx_dve, 1)
                dve.wait_ge(y_mm, output(b, g, 0))
                o = pY[:, 0:LQ].rearrange("p (t j e) -> p t j e", t=QT, e=32)
                nc.vector.reciprocal(rden[:, g % 2], o[:, :, :, HD1]).then_inc(rd, 1)
                dve.wait_ge(rd, s + 1)
                for qt in range(QT):
                    last = nc.vector.tensor_tensor(A[:, qt, g * R:(g + 1) * R].rearrange("p (j e) -> p j e", e=HD1),
                                                   o[:, qt, :, 0:HD1],
                                                   rden[:, g % 2, qt, :].unsqueeze(2).broadcast_to([P, HG, HD1]), ALU.mult)
                last.then_inc(y_ev, 1)
                if g == G1 - 1 and not has_next:
                    add_output(b, output(b, g, 2))
            steps(dve, step)


def mlp(nc, xs, g, beta, w1, b1, w2, b2, identf, out, eps=1e-5):
    NT = B * QT
    FF = w1.shape[1]
    NF = FF // P
    NB = NT // 4
    C0, C1 = 0.7978845608028654, 0.044715
    with ExitStack() as ctx:
        def sb(nm, shape, dt=F32):
            return ctx.enter_context(nc.sbuf_tensor(f"mlp_{nm}", shape, dt))

        def sem(nm):
            return ctx.enter_context(nc.semaphore(f"mlp_{nm}"))

        w1s, w2s = sb("w1", [P, FF]), sb("w2", [P, NF, D])
        b1c, b2s = sb("b1", [P, NF]), sb("b2", [P, D])
        gcol, bcol, eps_c = sb("g", [P, 1]), sb("beta", [P, 1]), sb("eps", [P, 1])
        stats, mv = sb("stats", [P, NT, 6]), sb("mv", [P, NT, 2])
        std, rstd = sb("std", [P, NT]), sb("rstd", [P, NT])
        xh, hT = sb("xh", [P, NT * D]), sb("hT", [P, NT * D])
        act_out = sb("gelu", [P, 2, NF, 512])
        banks = [ctx.enter_context(nc.psum_tensor(f"mlp_bank{i}", [P, 512], F32)) for i in range(8)]
        c_in, st, ag, sd, rs, xn = sem("c_in"), sem("st"), sem("ag"), sem("sd"), sem("rs"), sem("xn")
        t_mm, t_ev, f_mm, gl, y_mm, y_ev, stored = (sem("t_mm"), sem("t_ev"), sem("f_mm"), sem("gl"), sem("y_mm"),
                                                    sem("y_ev"), sem("stored"))
        biased = sem("biased")
        block = ctx.enter_context(nc.Block())

        @block.sync
        def _(sp):
            sp.dma_start(w1s[:], w1).then_inc(c_in, 16)
            sp.dma_start(w2s[:], w2.rearrange("(n p) d -> p n d", p=P)).then_inc(c_in, 16)
            for f in range(NF):
                sp.dma_start(b1c[:, f:f + 1], b1[f * P:(f + 1) * P].rearrange("(p o) -> p o", o=1)).then_inc(c_in, 16)
            sp.dma_start(b2s[:], row_everywhere(b2)).then_inc(c_in, 16)
            sp.dma_start(gcol[:], g.rearrange("(p o) -> p o", o=1)).then_inc(c_in, 16)
            sp.dma_start(bcol[:], beta.rearrange("(p o) -> p o", o=1)).then_inc(c_in, 16)
            o = out.rearrange("b (t p) d -> p (b t) d", p=P)
            for k in range(NB):
                sp.wait_ge(y_ev, k + 1)
                sp.dma_start(o[:, 4 * k:4 * k + 4, :], xs[:, k * 512:(k + 1) * 512].rearrange("p (t d) -> p t d", d=D)).then_inc(stored, 16)
            sp.wait_ge(stored, 16 * NB)

        @block.vector
        def _(dve):
            nc.vector.memset(eps_c[:], eps)
            for t in range(NT):
                last = nc.vector.bn_stats(stats[:, t, :], xs[:, t * D:(t + 1) * D])
            last.then_inc(st, 1)
            dve.wait_ge(st, 1)
            for t in range(NT):
                last = nc.vector.bn_aggr(mv[:, t, :], stats[:, t, :])
            last.then_inc(ag, 1)
            dve.wait_ge(sd, 1)
            nc.vector.reciprocal(rstd[:], std[:]).then_inc(rs, 1)
            dve.wait_ge(rs, 1)
            for t in range(NT):
                nc.vector.tensor_scalar(xh[:, t * D:(t + 1) * D], xs[:, t * D:(t + 1) * D], mv[:, t, 0:1],
                                        rstd[:, t:t + 1], ALU.subtract, ALU.mult).then_inc(xn, 1)
            dve.wait_ge(c_in, 16 * (5 + NF))
            xt = xs[:].rearrange("p (t d) -> p t d", d=D)
            dve.wait_ge(xn, NT)
            nc.vector.tensor_tensor(xt, xt, b2s[:].unsqueeze(1).broadcast_to([P, NT, D]), ALU.add).then_inc(biased, 1)
            dve.wait_ge(biased, 1)
            for k in range(NB):
                dve.wait_ge(y_mm, k + 1)
                xb = xs[:, k * 512:(k + 1) * 512]
                nc.vector.tensor_tensor(xb, xb, banks[6 + k % 2][:], ALU.add).then_inc(y_ev, 1)

        @block.scalar
        def _(act):
            act.wait_ge(ag, 1)
            nc.scalar.activation(std[:], mv[:, :, 1], ACT.Sqrt, bias=eps_c[:]).then_inc(sd, 1)
            act.wait_ge(c_in, 16 * (5 + NF))
            for q in range(NB):
                act.wait_ge(t_mm, q + 1)
                nc.scalar.activation(hT[:, q * 512:(q + 1) * 512], banks[q][:], ACT.Identity, bias=bcol[:], scale=gcol[:]).then_inc(t_ev, 1)
            for k in range(NB):
                for f in range(NF):
                    act.wait_ge(f_mm, k * NF + f + 1)
                    if k >= 2:
                        act.wait_ge(y_mm, k - 1)
                    nc.scalar.activation(act_out[:, k % 2, f, :], banks[(k * NF + f) % 4][:], ACT.Gelu_apprx_tanh,
                                         bias=b1c[:, f:f + 1]).then_inc(gl, 1)

        @block.tensor
        def _(pe):
            pe.wait_ge(c_in, 16 * (5 + NF))
            for t in range(NT):
                pe.wait_ge(xn, t + 1)
                last = nc.tensor.transpose(banks[t // 4][:, (t % 4) * D:(t % 4 + 1) * D], xh[:, t * D:(t + 1) * D], identf[:])
                if t % 4 == 3:
                    last.then_inc(t_mm, 1)
            pe.wait_ge(t_ev, NB)

            def up(k):
                for f in range(NF):
                    if k:
                        pe.wait_ge(gl, (k - 1) * NF + f + 1)
                    nc.tensor.matmul(banks[f][:], w1s[:, f * P:(f + 1) * P], hT[:, k * 512:(k + 1) * 512], start=True, stop=True).then_inc(f_mm, 1)

            up(0)
            for k in range(NB):
                if k + 1 < NB:
                    up(k + 1)
                pe.wait_ge(gl, (k + 1) * NF)
                if k >= 2:
                    pe.wait_ge(y_ev, k - 1)
                for i in range(4):
                    for f in range(NF):
                        last = nc.tensor.matmul(banks[6 + k % 2][:, i * D:(i + 1) * D], act_out[:, k % 2, f, i * P:(i + 1) * P],
                                                w2s[:, f, :], start=f == 0, stop=f == NF - 1)
                last.then_inc(y_mm, 1)


def build(nc, x, ctx_in, w, consts, out):
    kv_dram = nc.dram_tensor("kv_scratch", (B, P, KT * 2 * D), F32).ap()

    def w1(name):
        return w["L1_xattn_" + name]

    with ExitStack() as ctx:
        def sb(name, shape, dt=F32):
            return ctx.enter_context(nc.sbuf_tensor(name, shape, dt))

        xs = sb("xs", [P, B * QT * D])
        identf = sb("identf", [P, P])
        identb, maskq, maskk = sb("identb", [P, P], BF16), sb("maskq", [P, QT * LQ], BF16), sb("maskk", [P, P], BF16)
        with ExitStack() as layer0:
            xnT = layer0.enter_context(nc.sbuf_tensor("xnT", [P, B * LQ], F32))
            M = layer0.enter_context(nc.sbuf_tensor("M", [P, H0 * D], F32))
            layer0_attention(nc, (x, w["L0_xattn_norm_w"], w["L0_xattn_wq"], w["L0_xattn_wk"], consts["ident"],
                                  consts["mask_q"], consts["mask_k"], xs, xnT, M, identf, identb, maskq, maskk),
                             ctx_in, w["L0_xattn_wv"], w["L0_xattn_wo"], w1("ca_wk"), w1("ca_wv"), w1("ca_bk"),
                             w1("ca_bv"), consts["cos_k"], consts["sin_k"], kv_dram, xs, xnT, M, identf)
        q_hi, q_lo = sb("q_hi", [P, B * QT * D], F32R), sb("q_lo", [P, B * QT * D], F32R)
        with ExitStack() as self_attention:
            kv_all = self_attention.enter_context(nc.sbuf_tensor("kv_all", [P, B * QT, 2 * D], F32))
            layer1_attention(nc, "sa", xs, (w1("ln1_g"), w1("ln1_b")), [w1("sa_wq"), w1("sa_wk"), w1("sa_wv")],
                             [w1("sa_bq"), w1("sa_bk"), w1("sa_bv")], q_hi, q_lo, kv_all, None, w1("sa_wo"), w1("sa_bo"),
                             QT, P, True, consts, identf, identb, maskq, maskk)
        layer1_attention(nc, "ca", xs, (w1("ln2_g"), w1("ln2_b")), [w1("ca_wq")], [w1("ca_bq")], q_hi, q_lo, None, kv_dram,
                         w1("ca_wo"), w1("ca_bo"), KT, LAST, False, consts, identf, identb, maskq, maskk)
        mlp(nc, xs, w1("ln3_g"), w1("ln3_b"), w1("fc1_w"), w1("fc1_b"), w1("fc2_w"), w1("fc2_b"), identf, out)


def constants():
    f = np.float32
    inv = (f(1.0) / np.power(f(10000.0), np.arange(0, HD1, 2, dtype=f) / f(HD1))).astype(f)
    pos = np.arange(KT * P, dtype=f)
    ang = np.outer(pos, inv).astype(f)
    cos, sin = np.cos(ang).astype(f), np.sin(ang).astype(f)
    live = (pos < LK)[:, None]
    cos8 = np.where(live, np.concatenate([cos, cos], 1), f(0))
    sin8 = np.where(live, np.concatenate([-sin, sin], 1), f(0))
    tiles = lambda a: np.ascontiguousarray(a.reshape(-1, P, HD1).transpose(1, 0, 2)).astype(f)
    heads = lambda a: np.repeat(tiles(a[:LQ])[:, :, None, :], H1, 2).reshape(P, QT * D)
    scale = f(HD1 ** -0.5)
    rope = np.stack([heads(cos8) * scale, heads(sin8) * scale, heads(cos8), heads(sin8)], 1).astype(f)
    r = np.arange(P)[:, None]
    j = np.arange(HG)[None, :]
    hmask = np.where(r < 3 * R, (r % R) // HD1 == j, r - 3 * R == j).astype(f)
    q, k = np.arange(LQ)[:, None], np.arange(LQ)[None, :]
    mask = np.where(k <= q, f(0), f(NEG)).astype(f)
    return {"ident": np.eye(P, dtype=f), "cos_k": tiles(cos8), "sin_k": tiles(sin8), "rope": rope, "hmask": hmask,
            "mask_q": np.ascontiguousarray(mask.reshape(QT, P, LQ).transpose(1, 0, 2).reshape(P, QT * LQ)),
            "mask_k": np.ascontiguousarray(mask[:P, :P].T)}


def kernel(**inputs):
    import concourse.bacc as bacc
    from concourse.bass_utils import run_bass_kernel_spmd

    nc = bacc.Bacc("TRN2", target_bir_lowering=False, num_devices=1)
    arrays, aps = {}, {}
    for name, a in [*inputs.items(), *constants().items()]:
        a = np.ascontiguousarray(a)
        arrays[f"in_{name}"] = a
        aps[name] = nc.dram_tensor(f"in_{name}", a.shape, mybir.dt.from_np(a.dtype), kind="ExternalInput").ap()
    out = nc.dram_tensor("out", (B, LQ, D), F32, kind="ExternalOutput").ap()
    build(nc, aps["x"], aps["ctx_1024"], aps, aps, out)
    return run_bass_kernel_spmd(nc, [arrays], core_ids=[0]).results[0]["out"]
```
